# Optimizing a Trainium2 kernel written in Bass

```python
import numpy as np
import jax
import jax.numpy as jnp

def _softmax(x, axis=-1):
    return jax.nn.softmax(x, axis=axis)

def _gelu(x):
    return jax.nn.gelu(x, approximate=True)

def _silu(x):
    return jax.nn.silu(x)

def _sigmoid(x):
    return jax.nn.sigmoid(x)

def _layernorm(x, axis=-1, eps=1e-05):
    m = jnp.mean(x, axis=axis, keepdims=True)
    v = jnp.var(x, axis=axis, keepdims=True)
    return (x - m) / jnp.sqrt(v + eps)

def _scatter_add(tgt, idx, src, axis=0):
    return tgt.at[idx].add(src)

def _segment_sum(src, seg, n):
    return jax.ops.segment_sum(src, seg, n)
kernel_name = 'mk_perceiver_d2_seqx_r4_be4b20'

def setup_inputs(seed: int=0):
    np.random.seed(seed)
    _w = jnp.asarray

    def _rec_inputs():
        import jax
        import jax.numpy as jnp
        _rk = jax.random.key(seed)
        x = 7.22e-05 + 1 * jax.random.normal(jax.random.fold_in(_rk, 1), (1, 256, 512), jnp.float32)
        _lenS = 256 - jax.random.randint(jax.random.fold_in(_rk, 7), (1,), 0, max(1, 256 // 4) + 1, jnp.int32)
        _lenS2 = 4096 - jax.random.randint(jax.random.fold_in(_rk, 8), (1,), 0, max(1, 4096 // 4) + 1, jnp.int32)
        _ctx_512P = jax.random.normal(jax.random.fold_in(_rk, 11), (1, 16, 128), jnp.float32)
        _ctx_512c = jax.random.dirichlet(jax.random.fold_in(_rk, 511), 0.3 * jnp.ones((16,), jnp.float32), (1, 4096))
        _ctx_512t = jnp.einsum('bsk,bkd->bsd', _ctx_512c, _ctx_512P)
        _ctx_512t = _ctx_512t * jax.lax.rsqrt(jnp.mean(jnp.square(_ctx_512t)) + 1e-12) * 0.953939
        ctx_512 = -0.000514642 + 1.00011 * (_ctx_512t + 0.3 * jax.random.normal(jax.random.fold_in(_rk, 611), (1, 4096, 128), jnp.float32))
        return (x, ctx_512)
    x, ctx_512 = _rec_inputs()

    def _L0_xattn_setup():
        import jax, jax.numpy as jnp
        import numpy as np
        B, S, H, NH, L = (2, 512, 512, 16, 128)
        HD = H // NH
        key = jax.random.key(seed)
        k1, k2, k3, k4, k5 = jax.random.split(key, 5)
        scale = 0.02
        return {'q': jax.random.normal(k1, (B, S, H), dtype=jnp.float32), 'latent_kv': jax.random.normal(k2, (B, S, L), dtype=jnp.float32), 'Wq': jax.random.normal(k3, (H, H), dtype=jnp.float32) * scale, 'Wkv_expand': jax.random.normal(k4, (2 * H, L), dtype=jnp.float32) * scale, 'Wout': jax.random.normal(k5, (H, H), dtype=jnp.float32) * scale}
    _L0_xattn_all = _L0_xattn_setup()
    _L0_xattn_in = {k: v for k, v in _L0_xattn_all.items() if k in ('Wq', 'Wkv_expand', 'Wout')}
    del _L0_xattn_all

    def _L0_attn_setup():
        import jax, jax.numpy as jnp
        import numpy as np
        D_MODEL = 512
        N_HEADS = 16
        N_KV_HEADS = 4
        D_K = D_MODEL // N_HEADS
        N_REP = N_HEADS // N_KV_HEADS
        WINDOW = 128
        RMS_EPS = 1e-08
        ROPE_BASE = 10000.0
        MASK_FILL = -10000.0

        def _rmsnorm(x, w):
            rms = jnp.sqrt(jnp.mean(x * x, axis=-1, keepdims=True) + RMS_EPS)
            return x / rms * w

        def _rope(x, cos, sin):
            B, S, H, dk = x.shape
            xr = x.reshape(B, S, H, dk // 2, 2)
            x1, x2 = (xr[..., 0], xr[..., 1])
            c = cos[None, :, None, :]
            s = sin[None, :, None, :]
            o1 = x1 * c - x2 * s
            o2 = x1 * s + x2 * c
            return jnp.stack([o1, o2], axis=-1).reshape(B, S, H, dk)
        key = jax.random.key(seed)
        ks = jax.random.split(key, 10)
        B, S = (2, 512)
        std = 1.0 / np.sqrt(D_MODEL)
        inp = {'x': jax.random.normal(ks[0], (B, S, D_MODEL), dtype=jnp.float32), 'Wq': jax.random.normal(ks[1], (D_MODEL, D_MODEL), dtype=jnp.float32) * std, 'bq': jnp.zeros((D_MODEL,), dtype=jnp.float32), 'Wk': jax.random.normal(ks[2], (N_KV_HEADS * D_K, D_MODEL), dtype=jnp.float32) * std, 'bk': jnp.zeros((N_KV_HEADS * D_K,), dtype=jnp.float32), 'Wv': jax.random.normal(ks[3], (N_KV_HEADS * D_K, D_MODEL), dtype=jnp.float32) * std, 'bv': jnp.zeros((N_KV_HEADS * D_K,), dtype=jnp.float32), 'Wo': jax.random.normal(ks[4], (D_MODEL, D_MODEL), dtype=jnp.float32) * std, 'bo': jnp.zeros((D_MODEL,), dtype=jnp.float32), 'qn_w': jnp.ones((D_K,), dtype=jnp.float32), 'kn_w': jnp.ones((D_K,), dtype=jnp.float32), 'scale': jnp.asarray(1.0 / np.sqrt(D_K), dtype=jnp.float32)}
        return inp
    _L0_attn_all = _L0_attn_setup()
    _L0_attn_in = {k: v for k, v in _L0_attn_all.items() if k in ('Wq', 'bq', 'Wk', 'bk', 'Wv', 'bv', 'Wo', 'bo', 'qn_w', 'kn_w', 'scale')}
    del _L0_attn_all

    def _L0_ffn_setup():
        import jax, jax.numpy as jnp
        import numpy as np
        B, S, H, E, K, I = (2, 256, 512, 32, 8, 192)
        key = jax.random.key(seed)
        ks = jax.random.split(key, 5)
        scaled = lambda k, shp, fan: jax.random.normal(k, shp, jnp.float32) * fan ** (-0.5)
        return {'hidden_states': jax.random.normal(ks[0], (B, S, H), jnp.float32), 'router_w': scaled(ks[1], (E, H), H), 'w_gate': scaled(ks[2], (E, H, I), H), 'w_up': scaled(ks[3], (E, H, I), H), 'w_down': scaled(ks[4], (E, I, H), I)}
    _L0_ffn_all = _L0_ffn_setup()
    _L0_ffn_in = {k: v for k, v in _L0_ffn_all.items() if k in ('router_w', 'w_gate', 'w_up', 'w_down')}
    del _L0_ffn_all

    def _L1_xattn_setup():
        import jax, jax.numpy as jnp
        import numpy as np
        B, S, L = (2, 256, 256)
        DIM_Q, H, K, D_C, D_CQ, R = (512, 16, 128, 128, 384, 64)

        def _rope_tables(length, dim):
            inv = 1.0 / 10000.0 ** (jnp.arange(0, dim, 2, dtype=jnp.float32) / dim)
            f = jnp.arange(length, dtype=jnp.float32)[:, None] * inv[None, :]
            sin = jnp.repeat(jnp.sin(f), 2, axis=-1)
            cos = jnp.repeat(jnp.cos(f), 2, axis=-1)
            return (sin, cos)

        def _rotate_half(x):
            half = x.shape[-1] // 2
            return jnp.concatenate([-x[..., half:], x[..., :half]], axis=-1)

        def _apply_rope(x, sin, cos):
            return x * cos + _rotate_half(x) * sin
        key = jax.random.key(seed)
        ks = jax.random.split(key, 8)
        return {'hidden_q': jax.random.normal(ks[0], (B, S, DIM_Q), jnp.float32), 'kv_c': jax.random.normal(ks[1], (B, L, D_C), jnp.float32), 'Wq': jax.random.normal(ks[2], (H * K, DIM_Q), jnp.float32) / np.sqrt(DIM_Q).astype(np.float32), 'w_kc_q': jax.random.normal(ks[3], (H, K, D_CQ), jnp.float32) / np.sqrt(K).astype(np.float32), 'w_kc_kv': jax.random.normal(ks[4], (H, K, D_C), jnp.float32) / np.sqrt(K).astype(np.float32), 'W_qr': jax.random.normal(ks[5], (H, D_CQ, R), jnp.float32) / np.float32(np.sqrt(D_CQ) * np.sqrt(R)), 'W_kr': jax.random.normal(ks[6], (H, D_C, R), jnp.float32) / np.sqrt(D_C).astype(np.float32), 'Wo': jax.random.normal(ks[7], (DIM_Q, H * K), jnp.float32) / np.sqrt(H * K).astype(np.float32)}
    _L1_xattn_all = _L1_xattn_setup()
    _L1_xattn_in = {k: v for k, v in _L1_xattn_all.items() if k in ('Wq', 'w_kc_q', 'w_kc_kv', 'W_qr', 'W_kr', 'Wo')}
    del _L1_xattn_all

    def _L1_attn_setup():
        import jax, jax.numpy as jnp
        import numpy as np
        D_MODEL = 512
        EXPAND = 2
        D_INNER = EXPAND * D_MODEL
        D_SSM = D_INNER
        D_STATE = 128
        NGROUPS = 1
        HEADDIM = 64
        NHEADS = D_SSM // HEADDIM
        D_CONV = 4
        CHUNK = 64
        CONV_DIM = D_SSM + 2 * NGROUPS * D_STATE
        D_IN_PROJ = 2 * D_INNER + 2 * NGROUPS * D_STATE + NHEADS
        EPS = 1e-05

        def silu(x):
            return x * jax.nn.sigmoid(x)

        def softplus(x):
            return jnp.log1p(jnp.exp(-jnp.abs(x))) + jnp.maximum(x, 0)

        def segsum(x):
            T = x.shape[-1]
            xe = jnp.broadcast_to(x[..., :, None], x.shape + (T,))
            mask_lo = jnp.tril(jnp.ones((T, T), dtype=bool), k=-1)
            xe = jnp.where(mask_lo, xe, 0.0)
            s = jnp.cumsum(xe, axis=-2)
            mask = jnp.tril(jnp.ones((T, T), dtype=bool), k=0)
            return jnp.where(mask, s, -jnp.inf)

        def ssd(x, A, B, C, chunk_size):
            b, s, h, p = x.shape
            c = s // chunk_size
            resh = lambda m: m.reshape((b, c, chunk_size) + m.shape[2:])
            x, A, B, C = (resh(x), resh(A), resh(B), resh(C))
            A = jnp.transpose(A, (0, 3, 1, 2))
            A_cumsum = jnp.cumsum(A, axis=-1)
            L = jnp.exp(segsum(A))
            Y_diag = jnp.einsum('bclhn,bcshn,bhcls,bcshp->bclhp', C, B, L, x)
            decay_states = jnp.exp(A_cumsum[..., -1:] - A_cumsum)
            states = jnp.einsum('bclhn,bhcl,bclhp->bchpn', B, decay_states, x)
            init = jnp.zeros_like(states[:, :1])
            states = jnp.concatenate([init, states], axis=1)
            A_last = jnp.pad(A_cumsum[:, :, :, -1], ((0, 0), (0, 0), (1, 0)))
            decay_chunk = jnp.exp(segsum(A_last))
            new_states = jnp.einsum('bhzc,bchpn->bzhpn', decay_chunk, states)
            states, final_state = (new_states[:, :-1], new_states[:, -1])
            state_decay_out = jnp.exp(A_cumsum)
            Y_off = jnp.einsum('bclhn,bchpn,bhcl->bclhp', C, states, state_decay_out)
            Y = (Y_diag + Y_off).reshape(b, s, h, p)
            return (Y, final_state)
        key = jax.random.key(seed)
        ks = jax.random.split(key, 8)
        u = jax.random.normal(ks[0], (2, 1024, D_MODEL), dtype=jnp.float32)
        W_in = jax.random.normal(ks[1], (D_MODEL, D_IN_PROJ), dtype=jnp.float32) * D_MODEL ** (-0.5)
        conv_w = jax.random.uniform(ks[2], (D_CONV, CONV_DIM), dtype=jnp.float32, minval=-0.1, maxval=0.1)
        conv_b = jnp.zeros((CONV_DIM,), dtype=jnp.float32)
        dt = jnp.exp(jax.random.uniform(ks[3], (NHEADS,)) * (np.log(0.1) - np.log(0.001)) + np.log(0.001))
        dt = jnp.clip(dt, 0.0001)
        dt_bias = dt + jnp.log(jnp.expm1(dt))
        A_log = jnp.log(jax.random.uniform(ks[4], (NHEADS,), minval=1.0, maxval=16.0))
        D = jnp.ones((NHEADS,), dtype=jnp.float32)
        norm_scale = jnp.ones((D_SSM,), dtype=jnp.float32)
        W_out = jax.random.normal(ks[5], (D_INNER, D_MODEL), dtype=jnp.float32) * D_INNER ** (-0.5)
        return {'u': u, 'W_in': W_in, 'conv_w': conv_w, 'conv_b': conv_b, 'dt_bias': dt_bias, 'A_log': A_log, 'D': D, 'norm_scale': norm_scale, 'W_out': W_out}
    _L1_attn_all = _L1_attn_setup()
    _L1_attn_in = {k: v for k, v in _L1_attn_all.items() if k in ('W_in', 'conv_w', 'conv_b', 'dt_bias', 'A_log', 'D', 'norm_scale', 'W_out')}
    del _L1_attn_all

    def _L1_ffn_setup():
        import jax, jax.numpy as jnp
        import numpy as np
        QMAX = 127.0
        EPS = 1e-08

        def _quant_dequant(v, axis):
            scale = jnp.max(jnp.abs(v), axis=axis, keepdims=True) / QMAX
            scale = jnp.maximum(scale, EPS)
            q = jnp.clip(jnp.round(v / scale), -QMAX, QMAX)
            return q * scale

        def _ste(v, axis):
            return v + jax.lax.stop_gradient(_quant_dequant(v, axis) - v)
        key = jax.random.key(seed)
        k1, k2, k3 = jax.random.split(key, 3)
        H, I = (512, 1408)
        x = jax.random.normal(k1, (4, 512, H), dtype=jnp.float32)
        w_gate_up = jax.random.normal(k2, (2 * I, H), dtype=jnp.float32) * H ** (-0.5)
        w_down = jax.random.normal(k3, (H, I), dtype=jnp.float32) * I ** (-0.5)
        return {'x': x, 'w_gate_up': w_gate_up, 'w_down': w_down}
    _L1_ffn_all = _L1_ffn_setup()
    _L1_ffn_in = {k: v for k, v in _L1_ffn_all.items() if k in ('w_gate_up', 'w_down')}
    del _L1_ffn_all
    return {'x': x, 'ctx_512': ctx_512, 'L0_xattn_Wq': _L0_xattn_in['Wq'], 'L0_xattn_Wkv_expand': _L0_xattn_in['Wkv_expand'], 'L0_xattn_Wout': _L0_xattn_in['Wout'], 'L0_attn_Wq': _L0_attn_in['Wq'], 'L0_attn_bq': _L0_attn_in['bq'], 'L0_attn_Wk': _L0_attn_in['Wk'], 'L0_attn_bk': _L0_attn_in['bk'], 'L0_attn_Wv': _L0_attn_in['Wv'], 'L0_attn_bv': _L0_attn_in['bv'], 'L0_attn_Wo': _L0_attn_in['Wo'], 'L0_attn_bo': _L0_attn_in['bo'], 'L0_attn_qn_w': _L0_attn_in['qn_w'], 'L0_attn_kn_w': _L0_attn_in['kn_w'], 'L0_attn_scale': _L0_attn_in['scale'], 'L0_ffn_router_w': _L0_ffn_in['router_w'], 'L0_ffn_w_gate': _L0_ffn_in['w_gate'], 'L0_ffn_w_up': _L0_ffn_in['w_up'], 'L0_ffn_w_down': _L0_ffn_in['w_down'], 'L1_xattn_Wq': _L1_xattn_in['Wq'], 'L1_xattn_w_kc_q': _L1_xattn_in['w_kc_q'], 'L1_xattn_w_kc_kv': _L1_xattn_in['w_kc_kv'], 'L1_xattn_W_qr': _L1_xattn_in['W_qr'], 'L1_xattn_W_kr': _L1_xattn_in['W_kr'], 'L1_xattn_Wo': _L1_xattn_in['Wo'], 'L1_attn_W_in': _L1_attn_in['W_in'], 'L1_attn_conv_w': _L1_attn_in['conv_w'], 'L1_attn_conv_b': _L1_attn_in['conv_b'], 'L1_attn_dt_bias': _L1_attn_in['dt_bias'], 'L1_attn_A_log': _L1_attn_in['A_log'], 'L1_attn_D': _L1_attn_in['D'], 'L1_attn_norm_scale': _L1_attn_in['norm_scale'], 'L1_attn_W_out': _L1_attn_in['W_out'], 'L1_ffn_w_gate_up': _L1_ffn_in['w_gate_up'], 'L1_ffn_w_down': _L1_ffn_in['w_down']}

def reference(x, ctx_512, L0_xattn_Wq, L0_xattn_Wkv_expand, L0_xattn_Wout, L0_attn_Wq, L0_attn_bq, L0_attn_Wk, L0_attn_bk, L0_attn_Wv, L0_attn_bv, L0_attn_Wo, L0_attn_bo, L0_attn_qn_w, L0_attn_kn_w, L0_attn_scale, L0_ffn_router_w, L0_ffn_w_gate, L0_ffn_w_up, L0_ffn_w_down, L1_xattn_Wq, L1_xattn_w_kc_q, L1_xattn_w_kc_kv, L1_xattn_W_qr, L1_xattn_W_kr, L1_xattn_Wo, L1_attn_W_in, L1_attn_conv_w, L1_attn_conv_b, L1_attn_dt_bias, L1_attn_A_log, L1_attn_D, L1_attn_norm_scale, L1_attn_W_out, L1_ffn_w_gate_up, L1_ffn_w_down):
    import jax
    import jax.numpy as jnp

    def _L0_xattn_ref(q, latent_kv, Wq, Wkv_expand, Wout):
        import jax, jax.numpy as jnp
        import numpy as np
        B, S, H, NH, L = (2, 512, 512, 16, 128)
        HD = H // NH
        b, sq, _ = q.shape
        sk = latent_kv.shape[1]
        qp = q @ Wq.T
        kv = latent_kv @ Wkv_expand.T
        k, v = jnp.split(kv, 2, axis=-1)
        qh = qp.reshape(b, sq, NH, HD).transpose(0, 2, 1, 3)
        kh = k.reshape(b, sk, NH, HD).transpose(0, 2, 1, 3)
        vh = v.reshape(b, sk, NH, HD).transpose(0, 2, 1, 3)
        inv_sqrt_d = 1.0 / jnp.sqrt(jnp.float32(HD))
        scores = jnp.einsum('bhqd,bhkd->bhqk', qh, kh) * inv_sqrt_d
        causal = jnp.tril(jnp.ones((sq, sk), dtype=bool))
        scores = jnp.where(causal, scores, jnp.finfo(scores.dtype).min)
        attn = jax.nn.softmax(scores, axis=-1)
        out = jnp.einsum('bhqk,bhkd->bhqd', attn, vh)
        out = out.transpose(0, 2, 1, 3).reshape(b, sq, H)
        return out @ Wout.T

    def _L0_attn_ref(x, Wq, bq, Wk, bk, Wv, bv, Wo, bo, qn_w, kn_w, scale):
        import jax, jax.numpy as jnp
        import numpy as np
        D_MODEL = 512
        N_HEADS = 16
        N_KV_HEADS = 4
        D_K = D_MODEL // N_HEADS
        N_REP = N_HEADS // N_KV_HEADS
        WINDOW = 128
        RMS_EPS = 1e-08
        ROPE_BASE = 10000.0
        MASK_FILL = -10000.0

        def _rmsnorm(x, w):
            rms = jnp.sqrt(jnp.mean(x * x, axis=-1, keepdims=True) + RMS_EPS)
            return x / rms * w

        def _rope(x, cos, sin):
            B, S, H, dk = x.shape
            xr = x.reshape(B, S, H, dk // 2, 2)
            x1, x2 = (xr[..., 0], xr[..., 1])
            c = cos[None, :, None, :]
            s = sin[None, :, None, :]
            o1 = x1 * c - x2 * s
            o2 = x1 * s + x2 * c
            return jnp.stack([o1, o2], axis=-1).reshape(B, S, H, dk)
        B, S, D = x.shape
        q = (x @ Wq.T + bq).reshape(B, S, N_HEADS, D_K)
        k = (x @ Wk.T + bk).reshape(B, S, N_KV_HEADS, D_K)
        v = (x @ Wv.T + bv).reshape(B, S, N_KV_HEADS, D_K)
        q = _rmsnorm(q, qn_w)
        k = _rmsnorm(k, kn_w)
        inv_freq = 1.0 / ROPE_BASE ** (jnp.arange(0, D_K, 2, dtype=jnp.float32) / D_K)
        t = jnp.arange(S, dtype=jnp.float32)
        freqs = t[:, None] * inv_freq[None, :]
        cos, sin = (jnp.cos(freqs), jnp.sin(freqs))
        q = _rope(q, cos, sin)
        k = _rope(k, cos, sin)
        q = q.transpose(0, 2, 1, 3)
        k = k.transpose(0, 2, 1, 3)
        v = v.transpose(0, 2, 1, 3)
        k = jnp.repeat(k, N_REP, axis=1)
        v = jnp.repeat(v, N_REP, axis=1)
        scores = jnp.einsum('bhqd,bhkd->bhqk', q, k) * scale
        idx = jnp.arange(S)
        causal = idx[:, None] < idx[None, :]
        local = jnp.abs(idx[:, None] - idx[None, :]) > WINDOW // 2
        mask = causal | local
        scores = jnp.where(mask[None, None, :, :], MASK_FILL, scores)
        attn = jax.nn.softmax(scores, axis=-1)
        out = jnp.einsum('bhqk,bhkd->bhqd', attn, v)
        out = out.transpose(0, 2, 1, 3).reshape(B, S, D)
        return out @ Wo.T + bo

    def _L0_ffn_ref(hidden_states, router_w, w_gate, w_up, w_down):
        import jax, jax.numpy as jnp
        import numpy as np
        B, S, H, E, K, I = (2, 256, 512, 32, 8, 192)
        Bq, Sq, Hd = hidden_states.shape
        x = hidden_states.reshape(-1, Hd)
        logits = x @ router_w.T
        probs = jax.nn.softmax(logits.astype(jnp.float32), axis=-1)
        rw, sel = jax.lax.top_k(probs, K)
        rw = rw / jnp.sum(rw, axis=-1, keepdims=True)
        rw = rw.astype(x.dtype)

        def body(acc, operand):
            e, wg, wu, wd = operand
            w_e = jnp.sum(jnp.where(sel == e, rw, jnp.zeros_like(rw)), axis=-1)
            h = jax.nn.silu(x @ wg) * (x @ wu)
            return (acc + h @ wd * w_e[:, None], None)
        acc0 = jnp.zeros_like(x)
        acc, _ = jax.lax.scan(body, acc0, (jnp.arange(E), w_gate, w_up, w_down))
        return acc.reshape(Bq, Sq, Hd)

    def _L1_xattn_ref(hidden_q, kv_c, Wq, w_kc_q, w_kc_kv, W_qr, W_kr, Wo):
        import jax, jax.numpy as jnp
        import numpy as np
        B, S, L = (2, 256, 256)
        DIM_Q, H, K, D_C, D_CQ, R = (512, 16, 128, 128, 384, 64)

        def _rope_tables(length, dim):
            inv = 1.0 / 10000.0 ** (jnp.arange(0, dim, 2, dtype=jnp.float32) / dim)
            f = jnp.arange(length, dtype=jnp.float32)[:, None] * inv[None, :]
            sin = jnp.repeat(jnp.sin(f), 2, axis=-1)
            cos = jnp.repeat(jnp.cos(f), 2, axis=-1)
            return (sin, cos)

        def _rotate_half(x):
            half = x.shape[-1] // 2
            return jnp.concatenate([-x[..., half:], x[..., :half]], axis=-1)

        def _apply_rope(x, sin, cos):
            return x * cos + _rotate_half(x) * sin
        Bv, Sv, _ = hidden_q.shape
        _, Lv, _ = kv_c.shape
        q_hk = (hidden_q @ Wq.T).reshape(Bv, Sv, H, K)
        q_big = jnp.einsum('bshk,hkq->bshq', q_hk, w_kc_q)
        sin_q, cos_q = _rope_tables(Sv, D_CQ)
        q_big = _apply_rope(q_big, sin_q[None, :, None, :], cos_q[None, :, None, :])
        sin_k, cos_k = _rope_tables(Lv, D_C)
        kv_r = _apply_rope(kv_c, sin_k[None], cos_k[None])
        q_r = jnp.einsum('bshq,hqr->bhsr', q_big, W_qr)
        k_r = jnp.einsum('bld,hdr->bhlr', kv_r, W_kr)
        scores = jnp.einsum('bhsr,bhlr->bhsl', q_r, k_r)
        attn = jax.nn.softmax(scores, axis=-1)
        ctx_c = jnp.einsum('bhsl,bld->bhsd', attn, kv_r)
        ctx_lat = jnp.einsum('bhsd,hkd->bhsk', ctx_c, w_kc_kv)
        ctx = ctx_lat.transpose(0, 2, 1, 3).reshape(Bv, Sv, H * K)
        return ctx @ Wo.T

    def _L1_attn_ref(u, W_in, conv_w, conv_b, dt_bias, A_log, D, norm_scale, W_out):
        import jax, jax.numpy as jnp
        import numpy as np
        D_MODEL = 512
        EXPAND = 2
        D_INNER = EXPAND * D_MODEL
        D_SSM = D_INNER
        D_STATE = 128
        NGROUPS = 1
        HEADDIM = 64
        NHEADS = D_SSM // HEADDIM
        D_CONV = 4
        CHUNK = 64
        CONV_DIM = D_SSM + 2 * NGROUPS * D_STATE
        D_IN_PROJ = 2 * D_INNER + 2 * NGROUPS * D_STATE + NHEADS
        EPS = 1e-05

        def silu(x):
            return x * jax.nn.sigmoid(x)

        def softplus(x):
            return jnp.log1p(jnp.exp(-jnp.abs(x))) + jnp.maximum(x, 0)

        def segsum(x):
            T = x.shape[-1]
            xe = jnp.broadcast_to(x[..., :, None], x.shape + (T,))
            mask_lo = jnp.tril(jnp.ones((T, T), dtype=bool), k=-1)
            xe = jnp.where(mask_lo, xe, 0.0)
            s = jnp.cumsum(xe, axis=-2)
            mask = jnp.tril(jnp.ones((T, T), dtype=bool), k=0)
            return jnp.where(mask, s, -jnp.inf)

        def ssd(x, A, B, C, chunk_size):
            b, s, h, p = x.shape
            c = s // chunk_size
            resh = lambda m: m.reshape((b, c, chunk_size) + m.shape[2:])
            x, A, B, C = (resh(x), resh(A), resh(B), resh(C))
            A = jnp.transpose(A, (0, 3, 1, 2))
            A_cumsum = jnp.cumsum(A, axis=-1)
            L = jnp.exp(segsum(A))
            Y_diag = jnp.einsum('bclhn,bcshn,bhcls,bcshp->bclhp', C, B, L, x)
            decay_states = jnp.exp(A_cumsum[..., -1:] - A_cumsum)
            states = jnp.einsum('bclhn,bhcl,bclhp->bchpn', B, decay_states, x)
            init = jnp.zeros_like(states[:, :1])
            states = jnp.concatenate([init, states], axis=1)
            A_last = jnp.pad(A_cumsum[:, :, :, -1], ((0, 0), (0, 0), (1, 0)))
            decay_chunk = jnp.exp(segsum(A_last))
            new_states = jnp.einsum('bhzc,bchpn->bzhpn', decay_chunk, states)
            states, final_state = (new_states[:, :-1], new_states[:, -1])
            state_decay_out = jnp.exp(A_cumsum)
            Y_off = jnp.einsum('bclhn,bchpn,bhcl->bclhp', C, states, state_decay_out)
            Y = (Y_diag + Y_off).reshape(b, s, h, p)
            return (Y, final_state)
        b, s, _ = u.shape
        zxbcdt = u @ W_in
        z, xBC, dt = jnp.split(zxbcdt, [D_INNER, D_INNER + D_SSM + 2 * NGROUPS * D_STATE], axis=-1)
        xp = jnp.pad(xBC, ((0, 0), (D_CONV - 1, 0), (0, 0)))
        conv = conv_b
        for i in range(D_CONV):
            conv = conv + xp[:, i:i + s, :] * conv_w[i]
        xBC = silu(conv)
        x, B, C = jnp.split(xBC, [D_SSM, D_SSM + NGROUPS * D_STATE], axis=-1)
        x = x.reshape(b, s, NHEADS, HEADDIM)
        dt = softplus(dt + dt_bias)
        A = -jnp.exp(A_log)
        Bh = jnp.broadcast_to(B[:, :, None, :], (b, s, NHEADS, D_STATE))
        Ch = jnp.broadcast_to(C[:, :, None, :], (b, s, NHEADS, D_STATE))
        y, _final = ssd(x * dt[..., None], A * dt, Bh, Ch, CHUNK)
        y = y + x * D[None, None, :, None]
        y = y.reshape(b, s, D_SSM)
        y = y * silu(z)
        var = jnp.mean(jnp.square(y), axis=-1, keepdims=True)
        y = y * jax.lax.rsqrt(var + EPS) * norm_scale
        return y @ W_out

    def _L1_ffn_ref(x, w_gate_up, w_down):
        import jax, jax.numpy as jnp
        import numpy as np
        QMAX = 127.0
        EPS = 1e-08

        def _quant_dequant(v, axis):
            scale = jnp.max(jnp.abs(v), axis=axis, keepdims=True) / QMAX
            scale = jnp.maximum(scale, EPS)
            q = jnp.clip(jnp.round(v / scale), -QMAX, QMAX)
            return q * scale

        def _ste(v, axis):
            return v + jax.lax.stop_gradient(_quant_dequant(v, axis) - v)
        I = w_down.shape[1]
        xq = _ste(x, axis=-1)
        w1q = _ste(w_gate_up, axis=-1)
        gate_up = jnp.einsum('bsh,oh->bso', xq, w1q)
        gate, up = (gate_up[..., :I], gate_up[..., I:])
        h = jax.nn.silu(gate) * up
        hq = _ste(h, axis=-1)
        w2q = _ste(w_down, axis=-1)
        return jnp.einsum('bsi,oi->bso', hq, w2q)
    x = x + _L0_xattn_ref(_layernorm(x, axis=-1), ctx_512, L0_xattn_Wq, L0_xattn_Wkv_expand, L0_xattn_Wout)
    x = x + _L0_attn_ref(_layernorm(x, axis=-1), L0_attn_Wq, L0_attn_bq, L0_attn_Wk, L0_attn_bk, L0_attn_Wv, L0_attn_bv, L0_attn_Wo, L0_attn_bo, L0_attn_qn_w, L0_attn_kn_w, L0_attn_scale)
    x = x + _L0_ffn_ref(_layernorm(x, axis=-1), L0_ffn_router_w, L0_ffn_w_gate, L0_ffn_w_up, L0_ffn_w_down)
    x = x + _L1_xattn_ref(_layernorm(x, axis=-1), ctx_512, L1_xattn_Wq, L1_xattn_w_kc_q, L1_xattn_w_kc_kv, L1_xattn_W_qr, L1_xattn_W_kr, L1_xattn_Wo)
    x = x + _L1_attn_ref(_layernorm(x, axis=-1), L1_attn_W_in, L1_attn_conv_w, L1_attn_conv_b, L1_attn_dt_bias, L1_attn_A_log, L1_attn_D, L1_attn_norm_scale, L1_attn_W_out)
    x = x + _L1_ffn_ref(_layernorm(x, axis=-1), L1_ffn_w_gate_up, L1_ffn_w_down)
    return x

_drawn_inputs = setup_inputs


def setup_inputs(seed=0):
    import zlib

    import numpy as np

    out = dict(_drawn_inputs(seed))
    spreads = {'L0_attn_bq': (0.0, 0.1),
     'L0_attn_bk': (0.0, 0.302),
     'L0_attn_bv': (0.0, 0.1),
     'L0_attn_bo': (0.0, 0.1),
     'L0_attn_qn_w': (1.0, 0.2),
     'L0_attn_kn_w': (1.0, 0.2),
     'L1_attn_conv_b': (0.0, 0.1),
     'L1_attn_D': (1.0, 0.2),
     'L1_attn_norm_scale': (1.0, 0.2)}
    factors = {'L0_xattn_Wq': 4.82, 'L1_attn_dt_bias': 4.703, 'L1_attn_A_log': 5.357}
    for name, (base, spread) in spreads.items():
        noise = np.random.default_rng([zlib.crc32(name.encode()), seed]).standard_normal(out[name].shape)
        drawn = base * np.exp(spread * noise) if base else spread * noise
        out[name] = jnp.asarray(drawn.astype(out[name].dtype))
    for name, factor in factors.items():
        out[name] = (out[name] * factor).astype(out[name].dtype)
    return out
```

```python
from contextlib import ExitStack

import concourse.bass as bass
from concourse import mybir

P = 128
D = 512
KT = D // P
T = 256
NT = T // P
CD = 128
L = 4096
NH, HD = 16, 32
KVH = 4
HALF = HD // 2
WINDOW = 64
QKV = (NH + 2 * KVH) * HD
LN_EPS, RMS_EPS = 1e-5, 1e-8
NEG = -1e30
NE, TOPK, FI = 32, 8, 192
XH, XK, XQ, XR = 16, 128, 384, 64
QP = XQ // 4
CH = 512
NCH = L // CH
DI, DS, SH, HP, CONV = 1024, 128, 16, 64, 4
XBC = DI + 2 * DS
CT = XBC // P
IT = DI // P
DIN = DI + XBC + SH
FF = 1408
GT, DT, FT = 2 * FF // P, D // P, FF // P
FC = FF // 4
FR = FC // (2 * FF // P)
QMAX, QEPS = 127.0, 1e-8
ROUND = 1.5 * 2 ** 23
RB1, RB2 = 2 * FF // XH, D // XH
BLOCKS = KT * GT + FT * DT
BG = 8
STORES = 16 * (KT + DT + 2)
PAIRS = NE // 2

F32 = mybir.dt.float32
F32R = mybir.dt.float32r
BF16 = mybir.dt.bfloat16
ALU = mybir.AluOpType
ACT = mybir.ActivationFunctionType
AX = mybir.AxisListType


class Chain:

    def __init__(self, engine, sem):
        self.engine, self.sem, self.n, self.base = engine, sem, 0, 0

    def __call__(self, instruction):
        instruction.then_inc(self.sem, 1)
        self.n += 1
        self.engine.wait_ge(self.sem, self.base + self.n)


class Marks:

    def __init__(self, sem, **counts):
        self.sem, self.before, n = sem, {}, 0
        for name, count in counts.items():
            self.before[name] = n
            n += count

    def at(self, name, k):
        return self.before[name] + k


def perceiver(nc, a, out):
    ctx = ExitStack()
    with ctx:
        def sb(name, shape, dt=F32, at=ctx):
            return at.enter_context(nc.sbuf_tensor(name, shape, dt))

        def sem(name):
            return ctx.enter_context(nc.semaphore(name))

        PS = ctx.enter_context(nc.psum_tensor("PS", [P, 8, 512], F32))

        PSb = PS[:].rearrange("p b n -> p (b n)").bitcast(BF16).rearrange("p (b n) -> p b n", b=8)

        x = sb("x", [P, NT, D])
        xn = sb("xn", [P, NT, D])
        xnT = sb("xnT", [P, KT, T])
        ident = sb("ident", [P, P])
        ln_st = sb("ln_st", [P, NT, 6])
        ln_mv = sb("ln_mv", [P, NT, 2])
        ln_ve = sb("ln_ve", [P, NT])
        ln_rs = sb("ln_rs", [P, NT])
        mhalf = sb("mhalf", [P, NT])
        early = ExitStack()
        kvr = sb("kvr", [P, L // P, CD], F32, early)
        xH = sb("xH", [P, KT, T], F32R, early)
        xL = sb("xL", [P, KT, T], F32R, early)
        early.close()
        early = ExitStack()
        wblk = sb("wblk", [P, BLOCKS, P], BF16, early)
        early.close()
        win = sb("win", [P, KT, DIN])

        arena = ExitStack()
        A = lambda n, s, d=F32: sb(n, s, d, arena)
        wqA = A("wqA", [P, KT, D]); wkvA = A("wkvA", [P, 2 * D]); woA = A("woA", [P, KT, D])
        ctxT = A("ctxT", [P, T])
        kTA = A("kTA", [P, KT, T]); vA = A("vA", [P, NT, D]); qTA = A("qTA", [P, KT, T])
        maskA = A("maskA", [P, NT, T]); maskB = A("maskB", [P, NT, T])
        sm = A("sm", [P, 2, 4, 512]); pr = A("pr", [P, 2, 4, 512])
        mx = A("mx", [P, 8]); nmx = A("nmx", [P, 2, 8]); sums = A("sums", [P, NT, NH]); rec = A("rec", [P, NT, NH])
        PT = A("PT", [P, 4, 3, P])
        on = A("on", [P, NT, D]); oT = A("oT", [P, KT, T])
        wqkvB = A("wqkvB", [P, KT, QKV]); woB = A("woB", [P, KT, D])
        bqkv = A("bqkv", [P, QKV]); boB = A("boB", [P, D]); nw = A("nw", [P, NH + KVH, HD])
        scB = A("scB", [P, 1])
        qkv = A("qkv", [P, NT, QKV]); ms = A("ms", [P, NT, NH + KVH])
        rt = A("rt", [P, 4, (NH + KVH) * HALF]); qk = A("qk", [P, NT, NH + KVH, HD])
        cosB = A("cosB", [P, NT, HALF]); sinB = A("sinB", [P, NT, HALF])
        qkT = A("qkT", [P, 5, T])
        CC = 8
        craw = A("craw", [P, 2, CC, CD]); ccos = A("ccos", [P, 2, CC, CD // 2]); csin = A("csin", [P, 2, CC, CD // 2])
        crot = A("crot", [P, CC, CD])
        arena.close()

        arena = ExitStack()
        rawG, rawU, rawD = (A(n, [P, 2, 1536]) for n in ("rawG", "rawU", "rawD"))
        gH, gL, uH, uL = (A(n, [P, 2, KT, 3, P], F32R) for n in ("gH", "gL", "uH", "uL"))
        dH, dL = (A(n, [P, 2, 3, D], F32R) for n in ("dH", "dL"))
        wb = A("wb", [P, 2, 3, T])
        sg, hu, hw = (A(n, [P, 3, T]) for n in ("sg", "hu", "hw"))
        hH, hL = (A(n, [P, 2, 3, T], F32R) for n in ("hH", "hL"))
        wr = A("wr", [P, KT, NE])
        lmx = A("lmx", [P, NT]); ex = A("ex", [P, NT, NE]); top = A("top", [P, NT, TOPK]); rest = A("rest", [P, NT, NE])
        wsum = A("wsum", [P, NT]); wt = A("wt", [P, NT, NE]); wT = A("wT", [NE, T])
        w_rows = nc.dram_tensor("w_rows", [NE, T], F32)
        arena.close()

        arena = ExitStack()
        kvH, kvL = (A(n, [P, L // P, CD], F32R) for n in ("kvH", "kvL"))
        kvTH, kvTL = (A(n, [P, L], F32R) for n in ("kvTH", "kvTL"))
        qp = A("qp", [P, XH, T])
        both = arena
        arena = ExitStack()
        wqX = A("wqX", [P, 2, KT, XK]); kcq = A("kcq", [P, 2, XQ]); wqr = A("wqr", [QP, 2, 4, XR]); wkr = A("wkr", [XR, 2, CD])
        cosQ = A("cosQ", [QP, 4, T]); sinQ = A("sinQ", [QP, 4, T])
        qh = A("qh", [P, 2, T]); qm1 = A("qm1", [QP, 4, T]); qm2 = A("qm2", [QP, 4, T]); qb = A("qb", [QP, 2, 4, T]); qr = A("qr", [XR, T])
        arena.close()
        arena = ExitStack()
        sp_ = A("scores", [P, NT, L])
        pH, pL = (A(n, [P, 2, 4, T], F32R) for n in ("pH", "pL"))
        qsH, qsL = (A(n, [P, 2, T], F32R) for n in ("qsH", "qsL"))
        kcv = A("kcv", [P, 2, CD]); woX = A("woX", [P, 2, D]); w3 = A("w3", [P, 2, D]); cT = A("cT", [P, 2, T])
        cmax = A("cmax", [P, NT, NCH]); nmX = A("nmX", [P, 2, NT]); csum = A("csum", [P, 2, NT, NCH]); recX = A("recX", [P, 2, NT])
        wrow1 = A("wrow1", [RB1 // 2, 2, D])
        wrow2 = A("wrow2", [RB2, FF])
        wint1 = A("wint1", [RB1 // 2, 2, D], BF16); wint2 = A("wint2", [RB2, FF], BF16)
        rounding = A("rounding", [P, 2]); wmax = A("wmax", [RB1 // 2, 4]); wscale, winv = (A(n, [RB1 // 2, 3]) for n in ("wscale", "winv"))
        blocks = nc.dram_tensor("blocks", [P, BLOCKS, P], BF16)
        s_rows = nc.dram_tensor("s_rows", [2 * FF + D], F32)
        arena.close()
        both.close()

        arena = ExitStack()
        wturned = A("wturned", [P, BLOCKS * P], BF16)
        w1T = wturned[:, 0:KT * GT * P].rearrange("p (k t r) -> p k t r", k=KT, r=P); w2T = wturned[:, KT * GT * P:].rearrange("p (k n) -> p k n", k=FT)
        identb = A("identb", [P, P], BF16)
        quant = arena
        arena = ExitStack()
        wout = A("wout", [P, IT, D])
        cw = A("cw", [P, CT, CONV]); cb = A("cb", [P, CT]); dtb = A("dtb", [P, SH]); alog = A("alog", [P, SH]); dskip = A("dskip", [P, SH])
        ns = A("ns", [P, IT])
        xp = A("xp", [P, CT, CONV - 1 + T]); cv = A("cv", [P, CT, T]); act_ = A("act_", [P, CT, T])
        zs = A("zs", [P, NT, DI]); xs = A("xs", [P, NT, DI]); xdt = A("xdt", [P, NT, DI]); y = A("y", [P, NT, DI])
        dtv = A("dtv", [P, NT, SH]); dta = A("dta", [P, NT, SH]); dte = A("dte", [P, NT, SH]); dts = A("dts", [P, NT, SH])
        dtq = A("dtq", [P, NT, SH]); dtp = A("dtp", [P, NT, SH]); av = A("av", [P, NT, SH])
        after = A("after", [P, P]); upto = A("upto", [P, T]); gm = A("gm", [P, 3 * P])
        ua = A("ua", [P, 2, 3, P]); ones = A("ones", [P, P]); decay = A("decay", [P, 2, 3 * P]); mh = A("mh", [P, 2, 3 * P])
        ss = A("ss", [P, NT]); yrs = A("yrs", [P, NT])
        yT = cv
        arena.close()
        arena = ExitStack()
        swb = A("swb", [P, (GT + DT) * P])
        sx = A("sx", [P, NT]); sxi = A("sxi", [P, NT]); xr = A("xr", [P, NT, D]); xq = A("xq", [P, NT, D], BF16); xqT = A("xqT", [P, KT, T], BF16)
        gs = A("gs", [P, 2, FC]); sgF = A("sgF", [P, 2, FC]); us = A("us", [P, 2, FC]); hF = A("hF", [P, NT, FF])
        hr = A("hr", [P, NT, FF]); hq = A("hq", [P, NT, FF], BF16); hqT = A("hqT", [P, FT, T], BF16)
        hs = A("hs", [P, NT]); hsi = A("hsi", [P, NT]); of = A("of", [P, NT, DT, P])
        arena.close()
        quant.close()

        x_in = sem("x_in"); ctxT_in = sem("ctxT_in"); wkvA_in = sem("wkvA_in"); wqA_in = sem("wqA_in")
        woA_in = sem("woA_in"); wqkvB_in = sem("wqkvB_in"); woB_in = sem("woB_in"); smallB_in = sem("smallB_in")
        ctx_in = [sem("ctx_in0"), sem("ctx_in1")]; ctx_used = sem("ctx_used")
        consts_ready = sem("consts_ready")
        ln_var = sem("ln_var"); ln_rstd = sem("ln_rstd"); xn_ready = sem("xn_ready")
        xnT_ps = sem("xnT_ps"); xnT_ready = sem("xnT_ready")
        kvA_ps = sem("kvA_ps"); kvA_ready = sem("kvA_ready")
        q_ps = sem("q_ps"); q_ready = sem("q_ready")
        s_ps = sem("s_ps"); s_masked = sem("s_masked"); max_ready = sem("max_ready"); p_ready = sem("p_ready")
        pT_ps = sem("pT_ps"); pT_even = sem("pT_even"); pT_odd = sem("pT_odd"); o_ps = sem("o_ps")
        on_ready = sem("on_ready"); oT_ps = sem("oT_ps"); oT_ready = sem("oT_ready"); proj_ps = sem("proj_ps")
        qkv_ps = sem("qkv_ps"); qk_ready = sem("qk_ready"); qkT_ps = sem("qkT_ps"); qkT_ready = sem("qkT_ready")
        msq = sem("msq"); rms_ready = sem("rms_ready")
        wr_in = sem("wr_in"); raw_in = [sem("raw_in0"), sem("raw_in1")]; wb_in = [sem("wb_in0"), sem("wb_in1")]
        wH_ready = sem("wH_ready"); wL_ready = sem("wL_ready"); d_ready = sem("d_ready"); dH_ready = sem("dH_ready")
        gu_done = sem("gu_done"); sg_ready = sem("sg_ready"); hu_ready = sem("hu_ready"); hw_ready = sem("hw_ready")
        hH_ready = sem("hH_ready"); hL_ready = sem("hL_ready"); down_done = sem("down_done")
        xH_ready = sem("xH_ready"); xL_ready = sem("xL_ready")
        logit_ps = sem("logit_ps"); lmax_ready = sem("lmax_ready"); ex_ready = sem("ex_ready"); wt_ready = sem("wt_ready")
        wT_ps = sem("wT_ps"); wT_ready = sem("wT_ready"); w_stored = sem("w_stored")
        kvT_ps = sem("kvT_ps"); kvTH_ready = sem("kvTH_ready"); kvTL_ready = sem("kvTL_ready"); kvH_ready = sem("kvH_ready"); kvL_ready = sem("kvL_ready")
        qtab_in = sem("qtab_in")
        wqX_in, kcq_in, wr2_in, wo2_in = ([sem(f"{n}{b}") for b in range(2)] for n in ("wqX_in", "kcq_in", "wr2_in", "wo2_in"))
        p1_done = sem("p1_done"); p2_done = sem("p2_done"); p3_done = sem("p3_done"); p4_done = sem("p4_done")
        qh_ready = sem("qh_ready"); qm_ready = sem("qm_ready"); qb_ready = sem("qb_ready"); qr_ready = sem("qr_ready"); qp_ready = sem("qp_ready")
        qsH_ready = sem("qsH_ready"); rec_ready = sem("rec_ready"); qsL_ready = sem("qsL_ready")
        sX_ps = sem("sX_ps"); sX_out = sem("sX_out"); nm_ready = sem("nm_ready"); exp_done = sem("exp_done")
        t_done = sem("t_done"); pH_ready = sem("pH_ready"); pL_ready = sem("pL_ready"); v_done = sem("v_done")
        cT_ready = sem("cT_ready"); w3_ps = sem("w3_ps"); w3_ready = sem("w3_ready"); oX_ps = sem("oX_ps"); oX_added = sem("oX_added")
        csum_done = sem("csum_done")
        win_in = sem("win_in"); wout_in = sem("wout_in"); ssm_in = sem("ssm_in")
        wrow_in = sem("wrow_in"); wmax_ready = sem("wmax_ready"); wscale_ready = sem("wscale_ready"); winv_ready = sem("winv_ready")
        wdiv_ready = sem("wdiv_ready"); wrnd_ready = sem("wrnd_ready"); wint_ready = sem("wint_ready"); wint_stored = sem("wint_stored")
        wblk_in = sem("wblk_in"); wqT_ps = sem("wqT_ps"); wqT_ready = sem("wqT_ready")
        swb_in = sem("swb_in")
        ssm_consts = sem("ssm_consts"); xp_ready = sem("xp_ready"); zs_ready = sem("zs_ready"); identb_ready = sem("identb_ready")


        
        ua_ready = sem("ua_ready"); d_ps = sem("d_ps"); decay_ready = sem("decay_ready"); mh_ready = sem("mh_ready"); y_ps = sem("y_ps")
        skip_ready = sem("skip_ready"); yrs_ready = sem("yrs_ready")


        gs_ready = sem("gs_ready"); us_ready = sem("us_ready"); hF_ready = sem("hF_ready")
        hr_ready = sem("hr_ready")
        x_done = sem("x_done"); stored = sem("stored")
        dve_step = sem("dve_step"); pool_step = sem("pool_step")

        ssm_pe = Marks(sem("ssm_pe"), dt=1, xbc=CT // 2, z=NT, xsT=NT, g=1)
        ssm_act = Marks(sem("ssm_act"), dte=2, tap=CT, silu=CT, xs=NT)
        ssm_dve = Marks(sem("ssm_dve"), dta=1, a=1, cv=CT, xdt=NT)
        late_pe = Marks(sem("late_pe"), yT=2, yo=1, xqT=1, guF=4 * NT, hqT=3, oF=1)
        late_act = Marks(sem("late_act"), ss=1, yT=IT, xq=1, xqT=1, sgF=4 * NT, hq=NT, hqT=3)
        late_dve = Marks(sem("late_dve"), y=1, ms=1, xr=NT)

        def wait(eng, s, value):
            if not (isinstance(value, int) and value <= 0):
                eng.wait_ge(s, value)

        def pairs(eng, step, first=1):
            for i in range(first):
                for b in range(2):
                    step(2 * i + b, i, b)
            with eng.Fori(first, PAIRS // 2 - 1) as i:
                for b in range(2):
                    step(i * 2 + b, i, b)
            for b in range(2):
                step(PAIRS - 2 + b, PAIRS // 2 - 1, b)

        block = ctx.enter_context(nc.Block())

        def ctx_chunk(sp, c):
            rows = slice(c * CC * P, (c + 1) * CC * P)
            sp.dma_start(craw[:, c % 2], a["ctx"][rows].rearrange("(t p) d -> p t d", p=P)).then_inc(ctx_in[c % 2], 16)
            sp.dma_start(ccos[:, c % 2], a["cosK"][rows].rearrange("(t p) d -> p t d", p=P)).then_inc(ctx_in[c % 2], 16)
            sp.dma_start(csin[:, c % 2], a["sinK"][rows].rearrange("(t p) d -> p t d", p=P)).then_inc(ctx_in[c % 2], 16)

        @block.sync
        def _(sp):
            sp.dma_start(x[:], a["x"].rearrange("o (t p) d -> p (o t) d", p=P)).then_inc(x_in, 16)
            sp.dma_start(ctxT[:], a["ctxT"]).then_inc(ctxT_in, 16)
            sp.dma_start(wkvA[:], a["wkvA"]).then_inc(wkvA_in, 16)
            sp.dma_start(wqA[:], a["wqA"].rearrange("(k p) n -> p k n", p=P)).then_inc(wqA_in, 16)
            for c in range(2):
                ctx_chunk(sp, c)
            sp.dma_start(woA[:], a["woA"].rearrange("(k p) n -> p k n", p=P)).then_inc(woA_in, 16)
            sp.dma_start(wqkvB[:], a["wqkvB"].rearrange("(k p) n -> p k n", p=P)).then_inc(wqkvB_in, 16)
            sp.dma_start(bqkv[:], a["bqkv"].partition_broadcast(P)).then_inc(smallB_in, 16)
            sp.dma_start(boB[:], a["bo"].partition_broadcast(P)).then_inc(smallB_in, 16)
            sp.dma_start(nw[:, 0:NH, :], a["qn"].unsqueeze(0).broadcast_to([NH, HD]).partition_broadcast(P)).then_inc(smallB_in, 16)
            sp.dma_start(nw[:, NH:, :], a["kn"].unsqueeze(0).broadcast_to([KVH, HD]).partition_broadcast(P)).then_inc(smallB_in, 16)
            sp.dma_start(scB[:], a["scale"].partition_broadcast(P)).then_inc(smallB_in, 16)
            sp.dma_start(cosB[:], a["cosB"].rearrange("(t p) i -> p t i", p=P)).then_inc(smallB_in, 16)
            sp.dma_start(sinB[:], a["sinB"].rearrange("(t p) i -> p t i", p=P)).then_inc(smallB_in, 16)
            sp.dma_start(woB[:], a["woB"].rearrange("(k p) n -> p k n", p=P)).then_inc(woB_in, 16)
            for c in range(2, L // P // CC):
                sp.wait_ge(ctx_used, c - 1)
                ctx_chunk(sp, c)
            sp.wait_ge(ctx_used, L // P // CC)
            sp.wait_ge(x_done, 2)
            sp.dma_start(wr[:], a["wr"].rearrange("(k p) n -> p k n", p=P)).then_inc(wr_in, 16)

            def expert_weights(n, i, b):
                wait(sp, d_ready, n - 1)
                wait(sp, wL_ready, 2 * n - 2)
                sp.dma_start(rawG[:, b], a["wg"][n]).then_inc(raw_in[b], 16)
                sp.dma_start(rawU[:, b], a["wu"][n]).then_inc(raw_in[b], 16)
                sp.dma_start(rawD[:, b], a["wd"][n]).then_inc(raw_in[b], 16)

            def token_weights(n, i, b):
                wait(sp, hw_ready, n - 1)
                for m in range(2):
                    sp.dma_start(wb[:, b, m], w_rows[2 * n + m].partition_broadcast(P)).then_inc(wb_in[b], 16)
                    sp.dma_start(wb[64 * m:64 * m + 64, b, 2], w_rows[2 * n + m].partition_broadcast(64)).then_inc(wb_in[b], 16)

            for b in range(2):
                expert_weights(b, 0, b)
            sp.wait_ge(wT_ready, 1)
            sp.dma_start(w_rows[:], wT[:]).then_inc(w_stored, 16)
            sp.wait_ge(w_stored, 16)
            for b in range(2):
                token_weights(b, 0, b)
            with sp.Fori(1, PAIRS // 2) as i:
                for b in range(2):
                    expert_weights(i * 2 + b, i, b)
                    token_weights(i * 2 + b, i, b)
            sp.wait_ge(x_done, 3)

            def load_wq(n, i, b):
                sp.dma_start(wqX[:, b], a["wqX"][n].rearrange("p (k n) -> p k n", k=KT)).then_inc(wqX_in[b], 16)

            def load_kcq(n, i, b):
                sp.dma_start(kcq[:, b], a["kcq"][n]).then_inc(kcq_in[b], 16)

            def load_rank(n, i, b):
                sp.dma_start(wqr[:, b], a["wqr"][n].rearrange("p (k n) -> p k n", k=4)).then_inc(wr2_in[b], 16)
                sp.dma_start(wkr[:, b], a["wkr"][n]).then_inc(wr2_in[b], 16)

            for b in range(2):
                load_wq(b, 0, b)
                load_kcq(b, 0, b)
                if b == 0:
                    sp.dma_start(cosQ[:], a["cosQ"]).then_inc(qtab_in, 16)
                    sp.dma_start(sinQ[:], a["sinQ"]).then_inc(qtab_in, 16)
            load_rank(0, 0, 0)

            def head_loads(n, i, b):
                if not (isinstance(n, int) and n + 2 >= XH):
                    sp.wait_ge(p1_done, n + 1)
                    load_wq(n + 2, i + 1, b)
                if not (isinstance(n, int) and (n + 1 >= XH or n == 0)):
                    sp.wait_ge(p2_done, n)
                    load_kcq(n + 1, i + b, 1 - b)
                if not (isinstance(n, int) and n < 2):
                    sp.wait_ge(p4_done, n - 2)
                    load_rank(n - 1, i + b - 1, 1 - b)

            pairs(sp, head_loads, 2)
            sp.wait_ge(p4_done, XH - 2)
            load_rank(XH - 1, XH // 2 - 1, 1)

            def load_out(n, b):
                sp.dma_start(kcv[:, b], a["kcv"][n]).then_inc(wo2_in[b], 16)
                sp.dma_start(woX[:, b], a["woX"][n]).then_inc(wo2_in[b], 16)

            sp.wait_ge(qp_ready, XH)
            def load_rows(n):
                sp.dma_start(wrow1[:], a["w1"].rearrange("(n p j) d -> n p j d", n=XH, j=2)[n]).then_inc(wrow_in, 16)
                for t in range(DT):
                    sp.dma_start(wrow2[t * (RB2 // DT):(t + 1) * (RB2 // DT)], a["w2"].rearrange("(n r t) d -> n t r d", n=XH, t=DT)[n][t]).then_inc(wrow_in, 16)

            def rows1(n, k):
                return blocks[:, k * GT:(k + 1) * GT].rearrange("(n r) t d -> n r (t d)", n=XH)[n]

            def rows2(n, t):
                return blocks[:, KT * GT:].rearrange("(n r) (m t) d -> n t r m d", n=XH, t=DT)[n][t]

            scales1 = s_rows[0:2 * FF].rearrange("(n p j) -> n p j", n=XH, j=2)
            scales2 = s_rows[2 * FF:].rearrange("(n p j) -> n p j", n=XH, j=1)

            def store_rows(n):
                for k in range(KT):
                    sp.dma_start(rows1(n, k), wint1[:, :, k * P:(k + 1) * P]).then_inc(wint_stored, 16)
                for t in range(DT):
                    sp.dma_start(rows2(n, t), wint2[t * (RB2 // DT):(t + 1) * (RB2 // DT)].rearrange("p (m d) -> p m d", d=P)).then_inc(wint_stored, 16)
                sp.dma_start(scales1[n], wscale[:, 0:2]).then_inc(wint_stored, 16)
                sp.dma_start(scales2[n], wscale[0:RB2, 2:3]).then_inc(wint_stored, 16)

            for b in range(2):
                load_out(b, b)
            load_rows(0)
            sp.wait_ge(kvL_ready, 1)
            sp.dma_start(win[:], a["win"].rearrange("(k p) n -> p k n", p=P)).then_inc(win_in, 16)

            def out_loads(n, i, b):
                last = isinstance(n, int) and n + 1 >= XH
                if not (isinstance(n, int) and n + 2 >= XH):
                    sp.wait_ge(w3_ps, n + 1)
                    load_out(n + 2, b)
                sp.wait_ge(wint_ready, n + 1)
                if not last:
                    load_rows(n + 1)
                store_rows(n)

            pairs(sp, out_loads)
            sp.wait_ge(x_done, 4)
            sp.dma_start(cw[:], a["cw"]).then_inc(ssm_in, 16)
            sp.dma_start(cb[:], a["cb"]).then_inc(ssm_in, 16)
            sp.dma_start(dtb[:], a["dtb"].partition_broadcast(P)).then_inc(ssm_in, 16)
            sp.dma_start(alog[:], a["alog"].partition_broadcast(P)).then_inc(ssm_in, 16)
            sp.dma_start(dskip[:], a["dskip"].partition_broadcast(P)).then_inc(ssm_in, 16)
            sp.dma_start(ns[:], a["ns"]).then_inc(ssm_in, 16)
            sp.dma_start(wout[:], a["wout"].rearrange("(k p) n -> p k n", p=P)).then_inc(wout_in, 16)
            sp.wait_ge(wint_stored, STORES * XH)
            sp.wait_ge(ssm_pe.sem, ssm_pe.at("z", NT))
            for part in range(4):
                e = slice(part * BLOCKS // 4, (part + 1) * BLOCKS // 4)
                sp.dma_start(wblk[:, e], blocks[:, e]).then_inc(wblk_in, 16)
            sp.wait_ge(x_done, 5)
            sp.dma_start(swb[:], s_rows[:].partition_broadcast(P)).then_inc(swb_in, 16)
            sp.wait_ge(x_done, 6)
            sp.dma_start(out.rearrange("o (t p) d -> p (o t) d", p=P), x[:]).then_inc(stored, 16)
            sp.wait_ge(stored, 16)

        @block.gpsimd
        def _(pool):
            step = Chain(pool, pool_step)
            pool.memset(mhalf[:], -0.5).then_inc(consts_ready, 1)
            step(pool.memset(ident[:], 0.0))
            pool.affine_select(out=ident[:], in_=ident[:], compare_op=ALU.not_equal, fill=1.0, base=0,
                               pattern=[[-1, P]], channel_multiplier=1).then_inc(consts_ready, 1)
            pool.wait_ge(consts_ready, 2)

            def rstd(k):
                pool.wait_ge(ln_var, k + 1)
                pool.tensor_tensor(ln_rs[:], ln_ve[:], mhalf[:], ALU.pow).then_inc(ln_rstd, 1)

            rstd(0)
            step(pool.memset(maskA[:], 0.0))
            step(pool.affine_select(out=maskA[:], in_=maskA[:], compare_op=ALU.is_ge, fill=NEG, base=0,
                                    pattern=[[P, NT], [-1, T]], channel_multiplier=1))
            pool.affine_select(out=maskB[:], in_=maskA[:], compare_op=ALU.is_ge, fill=NEG, base=WINDOW,
                               pattern=[[-P, NT], [1, T]], channel_multiplier=-1).then_inc(consts_ready, 1)
            for c in range(L // P // CC):
                b = c % 2
                pool.wait_ge(ctx_in[b], 48 * (c // 2 + 1))
                dst = kvr[:, c * CC:(c + 1) * CC, :]
                def pair(t):
                    return t.rearrange("p t (i two) -> p t i two", two=2)
                def tab(t, lo, hi):
                    return t[:, :, lo:hi].unsqueeze(3).broadcast_to([P, CC, hi - lo, 2])
                pool.tensor_tensor(pair(crot[:, :, 0:64]), pair(craw[:, b, :, 64:128]), tab(csin[:, b], 0, 32), ALU.mult).then_inc(pool_step, 1)
                pool.tensor_tensor(pair(crot[:, :, 64:128]), pair(craw[:, b, :, 0:64]), tab(csin[:, b], 32, 64), ALU.mult).then_inc(pool_step, 1)
                step.n += 2
                step(pool.tensor_tensor(pair(dst), pair(craw[:, b]), tab(ccos[:, b], 0, 64), ALU.mult))
                ins = pool.tensor_tensor(dst, dst, crot[:], ALU.add)
                step(ins)
                pool.sem_inc(ctx_used, 1)
                if c == 1:
                    rstd(1)
            rstd(2)

            def split_down(n, i, b):
                pool.wait_ge(dH_ready, n + 1)
                pool.tensor_tensor(dL[:, b].rearrange("p m n -> p (m n)"), rawD[:, b], dH[:, b].rearrange("p m n -> p (m n)").bitcast(F32),
                                   ALU.subtract).then_inc(d_ready, 1)

            def pool_pair(n, i, b):
                if not (isinstance(n, int) and n == PAIRS - 1):
                    split_down(n + 1, i + b, 1 - b)
                pool.wait_ge(hu_ready, n + 1)
                pool.wait_ge(wb_in[b], (i + 1) * 64)
                wait(pool, hL_ready, n)
                pool.tensor_tensor(hw[:], hu[:], wb[:, b], ALU.mult).then_inc(hw_ready, 1)

            split_down(0, 0, 0)
            pairs(pool, pool_pair)
            rstd(3)

            def round_rows(n, i, b):
                pool.wait_ge(winv_ready, n + 1)
                pool.tensor_tensor(wrow1[:], wrow1[:], winv[:, 0:2].unsqueeze(2).broadcast_to([RB1 // 2, 2, D]), ALU.mult).then_inc(wdiv_ready, 1)
                pool.tensor_scalar(wrow2[:], wrow2[:], winv[0:RB2, 2:3], ROUND, ALU.mult, ALU.add)
                pool.wait_ge(wdiv_ready, n + 1)
                pool.tensor_tensor(wrow1[:], wrow1[:], rounding[0:RB1 // 2].unsqueeze(2).broadcast_to([RB1 // 2, 2, D]), ALU.add).then_inc(wrnd_ready, 1)
                pool.wait_ge(wrnd_ready, n + 1)
                wait(pool, wint_stored, n * STORES)
                pool.tensor_tensor(wint1[:], wrow1[:], rounding[0:RB1 // 2].unsqueeze(2).broadcast_to([RB1 // 2, 2, D]), ALU.subtract)
                pool.tensor_tensor(wint2[:], wrow2[:], rounding[0:RB2, 0:1].broadcast_to([RB2, FF]), ALU.subtract).then_inc(wint_ready, 1)

            step(pool.memset(rounding[:], ROUND))
            pairs(pool, round_rows)
            rstd(4)
            step(pool.memset(after[:], 1.0))
            pool.affine_select(out=after[:], in_=after[:], compare_op=ALU.is_gt, fill=0.0, base=0, pattern=[[-1, P]],
                               channel_multiplier=1).then_inc(ssm_consts, 1)
            step(pool.memset(upto[:], 1.0))
            pool.affine_select(out=upto[:], in_=upto[:], compare_op=ALU.is_ge, fill=0.0, base=0, pattern=[[1, T]],
                               channel_multiplier=-1).then_inc(ssm_consts, 1)
            pool.tensor_copy(identb[:], ident[:]).then_inc(identb_ready, 1)
            step(pool.memset(ones[:], 1.0))
            step(pool.memset(xp[:, :, 0:CONV - 1], 0.0))
            pool.sem_inc(ssm_consts, 1)
            pool.wait_ge(ssm_dve.sem, ssm_dve.at("a", 1))
            pool.wait_ge(ssm_consts, 3)

            avh = av[:].transpose([0, 2, 1])

            def pool_ssm(n, i, b):
                wait(pool, d_ps, n - 1)
                pool.tensor_tensor(ua[:, b, 0:2], after[:].unsqueeze(1).broadcast_to([P, 2, P]),
                                   avh[:, n].unsqueeze(2).broadcast_to([P, NT, P]), ALU.mult)
                pool.tensor_tensor(ua[:, b, 2], ones[:], avh[:, n, 1:2].broadcast_to([P, P]), ALU.mult).then_inc(ua_ready, 1)

            pairs(pool, pool_ssm)
            pool.wait_ge(ssm_act.sem, ssm_act.at("xs", NT))
            for t in range(NT):
                pool.tensor_tensor(y[:, t].rearrange("p (h c) -> p h c", c=HP), xs[:, t].rearrange("p (h c) -> p h c", c=HP),
                                   dskip[:].unsqueeze(2).broadcast_to([P, SH, HP]), ALU.mult).then_inc(skip_ready, 1)
            pool.wait_ge(late_dve.sem, late_dve.at("ms", 1))
            pool.tensor_tensor(yrs[:], ss[:], mhalf[:], ALU.pow).then_inc(yrs_ready, 1)
            rstd(5)
            for n in range(4 * NT):
                pool.wait_ge(us_ready, n + 1)
                pool.tensor_tensor(hF[:, n // 4, (n % 4) * FC:(n % 4 + 1) * FC].rearrange("p (r t) -> p t r", t=GT),
                                   sgF[:, n % 2].rearrange("p (t r) -> p t r", t=GT), us[:, n % 2].rearrange("p (t r) -> p t r", t=GT),
                                   ALU.mult).then_inc(hF_ready, 1)

        @block.scalar
        def _(act):
            act.wait_ge(kvA_ps, 1)
            act.activation(kTA[:], PS[:, 0:2, :].rearrange("p b (h t) -> p (b h) t", t=T), ACT.Copy).then_inc(kvA_ready, 1)
            act.activation(vA[:], PS[:, 2:4, :], ACT.Copy).then_inc(kvA_ready, 1)
            for k in range(2):
                act.wait_ge(xnT_ps, k + 1)
                act.activation(xnT[:], PS[:, 0:2, :].rearrange("p b (h t) -> p (b h) t", t=T), ACT.Copy).then_inc(xnT_ready, 1)
                if k == 0:
                    act.wait_ge(q_ps, 1)
                    act.activation(qTA[:], PS[:, 4:6, :].rearrange("p b (h t) -> p (b h) t", t=T), ACT.Copy).then_inc(q_ready, 1)
                else:
                    act.wait_ge(msq, 1)
                    act.activation(ms[:], ms[:], ACT.Sqrt).then_inc(rms_ready, 1)
                    act.wait_ge(qkT_ps, 1)
                    act.activation(qkT[:, 0:4, :], PS[:, 4:6, :].rearrange("p b (h t) -> p (b h) t", t=T), ACT.Copy).then_inc(qkT_ready, 1)
                    act.activation(qkT[:, 4, :], PS[:, 6, 0:T], ACT.Copy).then_inc(qkT_ready, 1)

                def exps(t):
                    act.wait_ge(max_ready, 4 * k + t + 1)
                    for j in range(4):
                        for q in range(NT):
                            ins = act.activation(pr[:, t % 2, j, q * T:(q + 1) * T], sm[:, t % 2, j, q * T:(q + 1) * T], ACT.Exp,
                                                 bias=nmx[:, t % 2, 2 * j + q:2 * j + q + 1], accum_out=sums[:, q, 4 * t + j:4 * t + j + 1])
                    ins.then_inc(p_ready, 1)

                exps(0)
                for t in range(4):
                    if t < 3:
                        exps(t + 1)
                    for j in (1, 3):
                        act.wait_ge(pT_ps, 16 * k + 4 * t + j + 1)
                        act.activation(PT[:, j], PS[:, 5, 0:3 * P].rearrange("p (b t) -> p b t", t=P), ACT.Copy).then_inc(pT_odd, 1)
                act.wait_ge(oT_ps, k + 1)
                act.activation(oT[:], PS[:, 0:2, :].rearrange("p b (h t) -> p (b h) t", t=T), ACT.Copy).then_inc(oT_ready, 1)

            act.wait_ge(xnT_ps, 3)
            src = PS[:, 0:2, :].rearrange("p b (h t) -> p (b h) t", t=T)
            act.activation(xnT[:], src, ACT.Copy).then_inc(xnT_ready, 1)
            act.wait_ge(xnT_ready, 3)
            act.activation(xH[:], xnT[:], ACT.Copy).then_inc(xH_ready, 1)

            def split_gate_up(n, i, b):
                act.wait_ge(raw_in[b], (i + 1) * 48)
                wait(act, gu_done, n - 1)
                act.activation(gH[:, b].rearrange("p k m n -> p (k m n)"), rawG[:, b], ACT.Copy).then_inc(wH_ready, 1)
                act.activation(uH[:, b].rearrange("p k m n -> p (k m n)"), rawU[:, b], ACT.Copy).then_inc(wH_ready, 1)
                wait(act, down_done, n - 1)
                act.activation(dH[:, b].rearrange("p m n -> p (m n)"), rawD[:, b], ACT.Copy).then_inc(dH_ready, 1)

            def act_pair(n, i, b):
                if not (isinstance(n, int) and n == PAIRS - 1):
                    split_gate_up(n + 1, i + b, 1 - b)
                act.wait_ge(gu_done, n + 1)
                wait(act, hu_ready, n)
                act.activation(sg[:], PS[:, 3 * b:3 * b + 3, 0:T], ACT.Silu).then_inc(sg_ready, 1)
                act.wait_ge(hw_ready, n + 1)
                wait(act, down_done, n - 1)
                act.activation(hH[:, b], hw[:], ACT.Copy).then_inc(hH_ready, 1)

            split_gate_up(0, 0, 0)
            act.wait_ge(lmax_ready, 1)
            for t in range(NT):
                ins = act.activation(ex[:, t], PS[:, 6, t * NE:(t + 1) * NE], ACT.Exp, bias=lmx[:, t:t + 1])
            ins.then_inc(ex_ready, 1)
            act.wait_ge(wT_ps, 1)
            act.activation(wT[:], PS[0:NE, 7, 0:T], ACT.Copy).then_inc(wT_ready, 1)
            pairs(act, act_pair)

            act.wait_ge(x_done, 3)
            act.activation(kvH[:], kvr[:], ACT.Copy).then_inc(kvH_ready, 1)
            for c in range(NCH):
                act.wait_ge(kvT_ps, c + 1)
                act.activation(kvTH[:, c * CH:(c + 1) * CH], PS[:, c % 4, :], ACT.Copy).then_inc(kvTH_ready, 1)
            act.wait_ge(xnT_ps, 4)
            act.activation(xnT[:], PS[:, 4:6, :].rearrange("p b (h t) -> p (b h) t", t=T), ACT.Copy).then_inc(xnT_ready, 1)

            def act_head(n, i, b):
                if not (isinstance(n, int) and n + 1 >= XH):
                    act.wait_ge(p1_done, n + 2)
                    wait(act, p2_done, n)
                    act.activation(qh[:, 1 - b], PS[:, 1 - b, 0:T], ACT.Copy).then_inc(qh_ready, 1)
                if not (isinstance(n, int) and n < 2):
                    low_rank(n - 2)

            def low_rank(n):
                act.wait_ge(p3_done, n + 1)
                wait(act, p4_done, n)
                act.activation(qr[:], PS[0:XR, 6, 0:T], ACT.Copy).then_inc(qr_ready, 1)
                act.wait_ge(p4_done, n + 1)
                act.activation(qp[:, n], PS[:, 7, 0:T], ACT.Copy).then_inc(qp_ready, 1)

            act.wait_ge(p1_done, 1)
            act.activation(qh[:, 0], PS[:, 0, 0:T], ACT.Copy).then_inc(qh_ready, 1)
            pairs(act, act_head, 2)
            low_rank(XH - 2)
            low_rank(XH - 1)

            def stage_query(n, b):
                act.activation(qsH[:, b], qp[:, n], ACT.Copy).then_inc(qsH_ready, 1)

            def exps_of(n, b, c):
                for q in range(NT):
                    at = sp_[:, q, c * CH:(c + 1) * CH]
                    ins = act.activation(at, at, ACT.Exp, bias=nmX[:, b, q:q + 1], accum_out=csum[:, b, q, c:c + 1])
                ins.then_inc(exp_done, 1)

            def context_out(n, b):
                act.wait_ge(v_done, n * NCH + NCH)
                act.activation(cT[:, b], PS[:, 6, 0:T], ACT.Copy).then_inc(cT_ready, 1)

            def act_scores(n, i, b):
                act.wait_ge(nm_ready, n + 1)
                wait(act, csum_done, n - 1)
                exps_of(n, b, 0)
                for c in range(NCH):
                    if c + 1 < NCH:
                        exps_of(n, b, c + 1)
                    act.wait_ge(t_done, n * NCH + (c + 1))
                    wait(act, v_done, n * NCH + (c - 1))
                    act.activation(pH[:, c % 2], PS[:, 2 + 2 * (c % 2):4 + 2 * (c % 2), :].rearrange("p k (h t) -> p (k h) t", t=T),
                                   ACT.Copy).then_inc(pH_ready, 1)
                    if c == 0 and not (isinstance(n, int) and n == 0):
                        context_out(n - 1, 1 - b)
                    if c == 4:
                        act.wait_ge(w3_ps, n + 1)
                        act.activation(w3[:, b], PS[:, 7, :], ACT.Copy).then_inc(w3_ready, 1)
                    if c == 5 and not (isinstance(n, int) and n + 2 >= XH):
                        stage_query(n + 2, b)

            act.wait_ge(qp_ready, XH)
            for b in range(2):
                stage_query(b, b)
            pairs(act, act_scores)
            context_out(XH - 1, 1)

            act.wait_ge(xnT_ps, 5)
            act.activation(xnT[:], PS[:, 4:6, :].rearrange("p b (h t) -> p (b h) t", t=T), ACT.Copy).then_inc(xnT_ready, 1)
            act.wait_ge(ssm_consts, 3)
            act.wait_ge(ssm_in, 96)
            act.wait_ge(ssm_dve.sem, ssm_dve.at("dta", 1))
            act.activation(dte[:], dta[:], ACT.Exp, scale=-1.0).then_inc(ssm_act.sem, 1)
            act.activation(alog[:], alog[:], ACT.Exp).then_inc(ssm_act.sem, 1)
            for m in range(CT // 2):
                act.wait_ge(ssm_pe.sem, ssm_pe.at("xbc", m + 1))
                act.activation(xp[:, 2 * m:2 * m + 2, CONV - 1:], PS[:, m, :].rearrange("p (c t) -> p c t", t=T), ACT.Copy).then_inc(xp_ready, 1)
                act.wait_ge(xp_ready, m + 1)
                for c in (2 * m, 2 * m + 1):
                    act.activation(cv[:, c], xp[:, c, 0:T], ACT.Identity, bias=cb[:, c:c + 1], scale=cw[:, c, 0:1]).then_inc(ssm_act.sem, 1)
            for m in range(CT):
                act.wait_ge(ssm_dve.sem, ssm_dve.at("cv", m + 1))
                act.activation(act_[:, m], cv[:, m], ACT.Silu).then_inc(ssm_act.sem, 1)
                if m in (3, 5):
                    t = (m - 3) // 2
                    act.wait_ge(ssm_pe.sem, ssm_pe.at("z", t + 1))
                    act.activation(zs[:, t], (PS[:, 6:8, :] if t == 0 else PS[:, 0:2, :]).rearrange("p b n -> p (b n)"), ACT.Silu).then_inc(zs_ready, 1)
            for t in range(NT):
                act.wait_ge(ssm_pe.sem, ssm_pe.at("xsT", t + 1))
                act.activation(xs[:, t], PS[:, 2 + 2 * t:4 + 2 * t, :].rearrange("p b n -> p (b n)"), ACT.Copy).then_inc(ssm_act.sem, 1)

            def act_ssm(n, i, b):
                act.wait_ge(d_ps, n + 1)
                wait(act, mh_ready, n - 1)
                act.activation(decay[:, b], PS[:, 6 + b, 0:3 * P], ACT.Exp).then_inc(decay_ready, 1)

            pairs(act, act_ssm)
            act.wait_ge(late_dve.sem, late_dve.at("y", 1))
            for t in range(NT):
                ins = act.activation(xdt[:, t], y[:, t], ACT.Square, accum_out=ss[:, t:t + 1])
            ins.then_inc(late_act.sem, 1)
            for m in range(IT):
                act.wait_ge(late_pe.sem, late_pe.at("yT", m // 4 + 1))
                act.activation(yT[:, m], PS[:, 4 + m // 2, (m % 2) * T:(m % 2 + 1) * T], ACT.Copy, scale=ns[:, m:m + 1]).then_inc(late_act.sem, 1)

            act.wait_ge(late_dve.sem, late_dve.at("xr", NT))
            act.activation(xq[:], xr[:], ACT.Copy, bias=-ROUND).then_inc(late_act.sem, 1)
            act.wait_ge(late_pe.sem, late_pe.at("xqT", 1))
            act.activation(xqT[:], PSb[:, 0, :].rearrange("p (k t) -> p k t", t=T), ACT.Copy).then_inc(late_act.sem, 1)
            for n in range(4 * NT):
                act.wait_ge(gs_ready, n + 1)
                if n >= 2:
                    act.wait_ge(hF_ready, n - 1)
                act.activation(sgF[:, n % 2], gs[:, n % 2], ACT.Silu, scale=sx[:, n // 4:n // 4 + 1]).then_inc(late_act.sem, 1)
            for t in range(NT):
                act.wait_ge(hr_ready, t + 1)
                act.activation(hq[:, t], hr[:, t], ACT.Copy, bias=-ROUND).then_inc(late_act.sem, 1)
            for g in range(3):
                k = 4 if g < 2 else 3
                act.wait_ge(late_pe.sem, late_pe.at("hqT", g + 1))
                act.activation(hqT[:, 4 * g:4 * g + k], PSb[:, 4 + g, 0:k * T].rearrange("p (k t) -> p k t", t=T), ACT.Copy).then_inc(late_act.sem, 1)

        @block.vector
        def _(dve):
            step = Chain(dve, dve_step)

            def layer_norm(k):
                for t in range(NT):
                    step(dve.bn_stats(ln_st[:, t, :], x[:, t, :]))
                    step(dve.bn_aggr(ln_mv[:, t, :], ln_st[:, t, :]))
                step(dve.tensor_scalar(ln_ve[:], ln_mv[:, :, 1], LN_EPS, None, ALU.add))
                dve.sem_inc(ln_var, 1)
                dve.wait_ge(ln_rstd, k + 1)
                for t in range(NT):
                    dve.tensor_scalar(xn[:, t, :], x[:, t, :], ln_mv[:, t, 0:1], ln_rs[:, t:t + 1],
                                      ALU.subtract, ALU.mult).then_inc(xn_ready, 1)

            def attention(k, scale, mask, head_major):
                def masked(t):
                    dve.wait_ge(s_ps, 4 * k + t + 1)
                    step(dve.scalar_tensor_tensor(sm[:, t % 2], PS[:, 0:4, :], scale,
                                                  mask[:].rearrange("p q t -> p (q t)").unsqueeze(1).broadcast_to([P, 4, 512]),
                                                  ALU.mult, ALU.add))
                    dve.sem_inc(s_masked, 1)
                    step(dve.tensor_reduce(mx[:], sm[:, t % 2].rearrange("p j (q t) -> p (j q) t", q=NT), AX.X, ALU.max))
                    step(dve.tensor_scalar(nmx[:, t % 2], mx[:], -1.0, None, ALU.mult))
                    dve.sem_inc(max_ready, 1)

                masked(0)
                for t in range(4):
                    if t < 3:
                        masked(t + 1)
                    for j in (0, 2):
                        dve.wait_ge(pT_ps, 16 * k + 4 * t + j + 1)
                        dve.tensor_copy(PT[:, j], PS[:, 4, 0:3 * P].rearrange("p (b t) -> p b t", t=P)).then_inc(pT_even, 1)
                dve.wait_ge(o_ps, k + 1)
                step(dve.reciprocal(rec[:], sums[:]))
                for q in range(NT):
                    r = rec[:, q, :].rearrange("p (t j) -> p t j", t=4)
                    if not head_major:
                        r = r.transpose([0, 2, 1])
                    dve.tensor_tensor(on[:, q, :].rearrange("p (g h d) -> p g h d", g=4, d=HD),
                                      PS[:, 6 + q, :].rearrange("p (g h d) -> p g h d", g=4, d=HD),
                                      r.unsqueeze(3).broadcast_to([P, 4, 4, HD]), ALU.mult).then_inc(on_ready, 1)
                dve.wait_ge(proj_ps, k + 1)
                for q in range(NT):
                    step(dve.tensor_tensor(x[:, q, :], x[:, q, :], PS[:, 2 + q, :], ALU.add))
                dve.sem_inc(x_done, 1)

            dve.wait_ge(x_in, 16)
            layer_norm(0)
            dve.wait_ge(consts_ready, 3)
            attention(0, HD ** -0.5, maskA, True)

            layer_norm(1)
            dve.wait_ge(smallB_in, 112)
            for q in range(NT):
                step(dve.tensor_tensor(x[:, q, :], x[:, q, :], boB[:], ALU.add))
            dve.wait_ge(qkv_ps, 1)
            NQK = NH + KVH
            for q in range(NT):
                step(dve.tensor_tensor(qkv[:, q, :], PS[:, 2 * q:2 * q + 2, :].rearrange("p b n -> p (b n)")[:, 0:QKV], bqkv[:], ALU.add))
            for q in range(NT):
                src = qkv[:, q, 0:NQK * HD]
                tmp = qk[:, q].rearrange("p h d -> p (h d)")
                step(dve.tensor_tensor(tmp, src, src, ALU.mult))
                step(dve.tensor_reduce(ms[:, q, :], qk[:, q], AX.X, ALU.add))
            step(dve.tensor_scalar(ms[:], ms[:], 1.0 / HD, RMS_EPS, ALU.mult, ALU.add))
            dve.sem_inc(msq, 1)
            dve.wait_ge(rms_ready, 1)
            step(dve.reciprocal(ms[:], ms[:]))
            for q in range(NT):
                src = qkv[:, q, 0:NQK * HD].rearrange("p (h d) -> p h d", d=HD)
                step(dve.tensor_tensor(src, src, ms[:, q, :].unsqueeze(2).broadcast_to([P, NQK, HD]), ALU.mult))
                step(dve.tensor_tensor(src, src, nw[:], ALU.mult))
                even, odd = (src.rearrange("p h (i two) -> p h i two", two=2)[:, :, :, e] for e in range(2))
                deven, dodd = (qk[:, q].rearrange("p h (i two) -> p h i two", two=2)[:, :, :, e] for e in range(2))
                c, s = (t[:, q, :].unsqueeze(1).broadcast_to([P, NQK, HALF]) for t in (cosB, sinB))
                r = [rt[:, i, :].rearrange("p (h i) -> p h i", i=HALF) for i in range(4)]
                dve.tensor_tensor(r[0], even, c, ALU.mult).then_inc(dve_step, 1)
                dve.tensor_tensor(r[1], odd, s, ALU.mult).then_inc(dve_step, 1)
                dve.tensor_tensor(r[2], even, s, ALU.mult).then_inc(dve_step, 1)
                step.n += 3
                step(dve.tensor_tensor(r[3], odd, c, ALU.mult))
                dve.tensor_tensor(deven, r[0], r[1], ALU.subtract).then_inc(dve_step, 1)
                step.n += 1
                step(dve.tensor_tensor(dodd, r[2], r[3], ALU.add))
                dve.sem_inc(qk_ready, 1)
            attention(1, scB[:, 0:1], maskB, False)

            layer_norm(2)
            dve.wait_ge(xH_ready, 1)
            step(dve.tensor_tensor(xL[:], xnT[:], xH[:].bitcast(F32), ALU.subtract))
            dve.sem_inc(xL_ready, 1)

            def split_gate_up(n, i, b):
                for j, (raw, hi, lo) in enumerate(((rawG, gH, gL), (rawU, uH, uL))):
                    dve.wait_ge(wH_ready, n * 2 + (j + 1))
                    dve.tensor_tensor(lo[:, b].rearrange("p k m n -> p (k m n)"), raw[:, b],
                                      hi[:, b].rearrange("p k m n -> p (k m n)").bitcast(F32), ALU.subtract).then_inc(wL_ready, 1)

            def dve_pair(n, i, b):
                if not (isinstance(n, int) and n == PAIRS - 1):
                    split_gate_up(n + 1, i + b, 1 - b)
                dve.wait_ge(sg_ready, n + 1)
                wait(dve, hw_ready, n)
                dve.tensor_tensor(hu[:], sg[:], PS[:, 3 * b:3 * b + 3, T:2 * T], ALU.mult).then_inc(hu_ready, 1)
                dve.wait_ge(hH_ready, n + 1)
                dve.tensor_tensor(hL[:, b], hw[:], hH[:, b].bitcast(F32), ALU.subtract).then_inc(hL_ready, 1)

            split_gate_up(0, 0, 0)
            dve.wait_ge(logit_ps, 1)
            logits = PS[:, 6, 0:NT * NE].rearrange("p (t e) -> p t e", e=NE)
            step(dve.tensor_reduce(lmx[:], logits, AX.X, ALU.max))
            step(dve.tensor_scalar(lmx[:], lmx[:], -1.0, None, ALU.mult))
            dve.sem_inc(lmax_ready, 1)
            dve.wait_ge(ex_ready, 1)
            for t in range(NT):
                step(dve.max(top[:, t], ex[:, t]))
                step(dve.match_replace(rest[:, t], top[:, t], ex[:, t], 0.0))
            step(dve.tensor_tensor(rest[:], ex[:], rest[:], ALU.subtract))
            step(dve.tensor_reduce(wsum[:], rest[:], AX.X, ALU.add))
            step(dve.reciprocal(wsum[:], wsum[:]))
            step(dve.tensor_tensor(wt[:], rest[:], wsum[:].unsqueeze(2).broadcast_to([P, NT, NE]), ALU.mult))
            dve.sem_inc(wt_ready, 1)
            pairs(dve, dve_pair)
            dve.wait_ge(down_done, PAIRS)
            for t in range(NT):
                step(dve.tensor_tensor(x[:, t, :], x[:, t, :], PS[:, 6 + t, :], ALU.add))
            dve.sem_inc(x_done, 1)

            layer_norm(3)
            for c in range(NCH):
                dve.wait_ge(kvTH_ready, c + 1)
                dve.tensor_tensor(kvTL[:, c * CH:(c + 1) * CH], PS[:, c % 4, :], kvTH[:, c * CH:(c + 1) * CH].bitcast(F32),
                                  ALU.subtract).then_inc(kvTL_ready, 1)
            dve.wait_ge(kvH_ready, 1)
            dve.tensor_tensor(kvL[:], kvr[:], kvH[:].bitcast(F32), ALU.subtract).then_inc(kvL_ready, 1)
            dve.wait_ge(qtab_in, 32)

            def dve_head(n, i, b):
                dve.wait_ge(p2_done, n + 1)
                wait(dve, qb_ready, n)
                big = PS[0:QP, 2 + 2 * b:4 + 2 * b, :].rearrange("p k (h t) -> p (k h) t", t=T)
                dve.tensor_tensor(qm1[:], big, cosQ[:], ALU.mult)
                dve.tensor_tensor(qm2[:, 0:2], big[:, 2:4], sinQ[:, 0:2], ALU.mult)
                dve.tensor_tensor(qm2[:, 2:4], big[:, 0:2], sinQ[:, 2:4], ALU.mult).then_inc(qm_ready, 1)
                dve.wait_ge(qm_ready, n + 1)
                wait(dve, p3_done, n - 1)
                dve.tensor_tensor(qb[:, b], qm1[:], qm2[:], ALU.add).then_inc(qb_ready, 1)

            pairs(dve, dve_head, 2)

            def stage_query(n, b):
                dve.wait_ge(qsH_ready, n + 1)
                dve.tensor_tensor(qsL[:, b], qp[:, n], qsH[:, b].bitcast(F32), ALU.subtract).then_inc(qsL_ready, 1)

            def scores_out(n, c):
                for q in range(NT):
                    dve.wait_ge(sX_ps, n * (NT * NCH) + (NT * c + q + 1))
                    dve.tensor_scalar(sp_[:, q, c * CH:(c + 1) * CH], PS[:, q, :], 1.0, None, ALU.mult, ALU.max,
                                      accum_out=cmax[:, q, c:c + 1]).then_inc(sX_out, 1)

            def negated_max(n, b):
                dve.wait_ge(sX_out, n * (NT * NCH) + NT * NCH)
                dve.tensor_reduce(nmX[:, b], cmax[:], AX.X, ALU.max, negate=True).then_inc(nm_ready, 1)

            def add_out(n, b, q):
                dve.wait_ge(oX_ps, n * NT + (q + 1))
                dve.wait_ge(rec_ready, n + 1)
                wait(dve, oX_added, n * NT + q)
                dve.scalar_tensor_tensor(x[:, q, :], PS[:, 7, :], recX[:, b, q:q + 1], x[:, q, :], ALU.mult, ALU.add).then_inc(oX_added, 1)

            def dve_scores(n, i, b):
                last = isinstance(n, int) and n + 1 >= XH
                for c in range(NCH):
                    if not last:
                        scores_out(n + 1, c)
                    if c == NCH - 1 and not last:
                        negated_max(n + 1, 1 - b)
                    dve.wait_ge(pH_ready, n * NCH + (c + 1))
                    dve.tensor_tensor(pL[:, c % 2], PS[:, 2 + 2 * (c % 2):4 + 2 * (c % 2), :].rearrange("p k (h t) -> p (k h) t", t=T),
                                      pH[:, c % 2].bitcast(F32), ALU.subtract).then_inc(pL_ready, 1)
                    if c == 1 and not (isinstance(n, int) and n < 2):
                        add_out(n - 2, b, 1)
                    if c == 6 and not (isinstance(n, int) and n + 2 >= XH):
                        stage_query(n + 2, b)
                    if c == 2:
                        dve.wait_ge(wrow_in, n * (16 + 16 * DT) + (16 + 16 * DT))
                        dve.tensor_reduce(wmax[:, 0:2], wrow1[:], AX.X, ALU.max, apply_absolute_value=True)
                    if c == 4:
                        dve.tensor_reduce(wmax[0:RB2, 2:3], wrow2[:, 0:FF // 2], AX.X, ALU.max, apply_absolute_value=True)
                    if c == 5:
                        dve.tensor_reduce(wmax[0:RB2, 3:4], wrow2[:, FF // 2:], AX.X, ALU.max, apply_absolute_value=True).then_inc(wmax_ready, 1)
                        dve.wait_ge(wmax_ready, n * 2 + 1)
                        dve.tensor_tensor(wmax[0:RB2, 2:3], wmax[0:RB2, 2:3], wmax[0:RB2, 3:4], ALU.max).then_inc(wmax_ready, 1)
                        dve.wait_ge(wmax_ready, n * 2 + 2)
                        wait(dve, wint_stored, n * STORES)
                        dve.tensor_scalar(wscale[:], wmax[:, 0:3], 1.0 / QMAX, QEPS, ALU.mult, ALU.max).then_inc(wscale_ready, 1)
                        dve.wait_ge(wscale_ready, n + 1)
                        dve.reciprocal(winv[:], wscale[:]).then_inc(winv_ready, 1)
                dve.wait_ge(exp_done, n * NCH + NCH)
                dve.tensor_reduce(recX[:, b], csum[:, b], AX.X, ALU.add).then_inc(csum_done, 1)
                dve.wait_ge(csum_done, n + 1)
                dve.reciprocal(recX[:, b], recX[:, b]).then_inc(rec_ready, 1)
                if not (isinstance(n, int) and n == 0):
                    add_out(n - 1, 1 - b, 0)

            step(dve.memset(wmax[:], 0.0))
            for b in range(2):
                stage_query(b, b)
            for c in range(NCH):
                scores_out(0, c)
            negated_max(0, 0)
            pairs(dve, dve_scores)
            add_out(XH - 2, 0, 1)
            add_out(XH - 1, 1, 0)
            add_out(XH - 1, 1, 1)
            dve.wait_ge(oX_added, NT * XH)
            dve.sem_inc(x_done, 1)

            layer_norm(4)

            def row_scales(scale, inverse, src):
                step(dve.tensor_reduce(scale, src, AX.X, ALU.max, apply_absolute_value=True))
                step(dve.tensor_scalar(scale, scale, 1.0 / QMAX, QEPS, ALU.mult, ALU.max))
                step(dve.reciprocal(inverse, scale))

            def turned_weights(n, b):
                dve.wait_ge(wqT_ps, n + 1)
                dve.tensor_copy(wturned[:, 0:SH * BG * P].rearrange("p (n d) -> p n d", n=SH)[:, n], PSb[:, 4 + b, :]).then_inc(wqT_ready, 1)

            dve.wait_ge(ssm_in, 96)
            dve.wait_ge(ssm_pe.sem, ssm_pe.at("dt", 1))
            step(dve.tensor_tensor(dtv[:], PS[:, 5, 0:NT * SH].rearrange("p (t h) -> p t h", h=SH),
                                   dtb[:].unsqueeze(1).broadcast_to([P, NT, SH]), ALU.add))
            step(dve.scalar_tensor_tensor(dta[:], dtv[:], -1.0, dtv[:], ALU.mult, ALU.max))
            dve.sem_inc(ssm_dve.sem, 1)
            dve.wait_ge(ssm_act.sem, ssm_act.at("dte", 2))
            step(dve.tensor_scalar(dts[:], dte[:], 2.0, None, ALU.add))
            step(dve.reciprocal(dts[:], dts[:]))
            step(dve.tensor_tensor(dts[:], dte[:], dts[:], ALU.mult))
            step(dve.tensor_tensor(dtq[:], dts[:], dts[:], ALU.mult))
            step(dve.tensor_scalar(dtp[:], dtq[:], 1.0 / 15, 1.0 / 13, ALU.mult, ALU.add))
            for k in (11, 9, 7, 5, 3, 1):
                step(dve.tensor_tensor(dtp[:], dtp[:], dtq[:], ALU.mult))
                step(dve.tensor_scalar(dtp[:], dtp[:], 1.0 / k, None, ALU.add))
            step(dve.scalar_tensor_tensor(dtp[:], dts[:], 2.0, dtp[:], ALU.mult, ALU.mult))
            step(dve.scalar_tensor_tensor(dtv[:], dtv[:], 0.0, dtp[:], ALU.max, ALU.add))
            step(dve.scalar_tensor_tensor(av[:], dtv[:], -1.0, alog[:].unsqueeze(1).broadcast_to([P, NT, SH]), ALU.mult, ALU.mult))
            dve.sem_inc(ssm_dve.sem, 1)
            for m in range(0, CT, 2):
                for k in range(1, CONV):
                    for c in (m, m + 1):
                        if k == 1:
                            dve.wait_ge(ssm_act.sem, ssm_act.at("tap", c + 1))
                        ins = dve.scalar_tensor_tensor(cv[:, c], xp[:, c, k:k + T], cw[:, c, k:k + 1], cv[:, c], ALU.mult, ALU.add)
                        if c == m:
                            ins.then_inc(dve_step, 1)
                            step.n += 1
                    step(ins)
                dve.sem_inc(ssm_dve.sem, 2)
            dve.wait_ge(ssm_pe.sem, ssm_pe.at("g", 1))
            dve.wait_ge(ssm_consts, 2)
            step(dve.tensor_tensor(gm[:, 0:T], PS[:, 1, 0:T], upto[:], ALU.mult))
            step(dve.tensor_tensor(gm[:, T:], PS[:, 1, T:T + P], upto[:, 0:P], ALU.mult))
            for t in range(NT):
                dve.wait_ge(ssm_act.sem, ssm_act.at("xs", t + 1))
                dve.tensor_tensor(xdt[:, t].rearrange("p (h c) -> p h c", c=HP), xs[:, t].rearrange("p (h c) -> p h c", c=HP),
                                  dtv[:, t].unsqueeze(2).broadcast_to([P, SH, HP]), ALU.mult).then_inc(ssm_dve.sem, 1)

            def dve_ssm(n, i, b):
                dve.wait_ge(decay_ready, n + 1)
                wait(dve, y_ps, n - 1)
                dve.tensor_tensor(mh[:, b], decay[:, b], gm[:], ALU.mult).then_inc(mh_ready, 1)
                turned_weights(n, b)

            pairs(dve, dve_ssm)
            dve.wait_ge(wqT_ps, SH + 1)
            dve.tensor_copy(wturned[:, SH * BG * P:], PSb[:, 4, 0:(BLOCKS - SH * BG) * P]).then_inc(wqT_ready, 1)
            dve.wait_ge(y_ps, SH)
            dve.wait_ge(skip_ready, NT)
            dve.wait_ge(zs_ready, NT)
            for t in range(NT):
                step(dve.tensor_tensor(y[:, t], y[:, t], PS[:, 2 * t:2 * t + 2, :].rearrange("p b n -> p (b n)"), ALU.add))
                step(dve.tensor_tensor(y[:, t], y[:, t], zs[:, t], ALU.mult))
            dve.sem_inc(late_dve.sem, 1)
            dve.wait_ge(late_act.sem, late_act.at("ss", 1))
            step(dve.tensor_scalar(ss[:], ss[:], 1.0 / DI, LN_EPS, ALU.mult, ALU.add))
            dve.sem_inc(late_dve.sem, 1)
            dve.wait_ge(yrs_ready, 1)
            dve.wait_ge(late_pe.sem, late_pe.at("yo", 1))
            for t in range(NT):
                step(dve.scalar_tensor_tensor(x[:, t, :], PS[:, t, :], yrs[:, t:t + 1], x[:, t, :], ALU.mult, ALU.add))
            dve.sem_inc(x_done, 1)

            layer_norm(5)
            dve.wait_ge(xn_ready, 6 * NT)
            for t in range(NT):
                row_scales(sx[:, t:t + 1], sxi[:, t:t + 1], xn[:, t, :])
                dve.tensor_scalar(xr[:, t, :], xn[:, t, :], sxi[:, t:t + 1], ROUND, ALU.mult, ALU.add).then_inc(late_dve.sem, 1)
            dve.wait_ge(swb_in, 16)

            def scale1(c):
                return swb[:, c * FC:(c + 1) * FC].rearrange("p (r t) -> p t r", t=GT)

            for n in range(4 * NT):
                t, c = n // 4, n % 4
                dve.wait_ge(late_pe.sem, late_pe.at("guF", n + 1))
                if n >= 2:
                    dve.wait_ge(late_act.sem, late_act.at("sgF", n - 1))
                    dve.wait_ge(hF_ready, n - 1)
                dve.tensor_tensor(gs[:, n % 2].rearrange("p (t r) -> p t r", t=GT), PS[:, 2 + 2 * (n % 2), 0:FC].rearrange("p (t r) -> p t r", t=GT), scale1(c), ALU.mult).then_inc(gs_ready, 1)
                dve.wait_ge(late_act.sem, late_act.at("sgF", n + 1))
                dve.scalar_tensor_tensor(us[:, n % 2].rearrange("p (t r) -> p t r", t=GT), PS[:, 3 + 2 * (n % 2), 0:FC].rearrange("p (t r) -> p t r", t=GT), sx[:, t:t + 1], scale1(4 + c),
                                         ALU.mult, ALU.mult).then_inc(us_ready, 1)
            for t in range(NT):
                dve.wait_ge(hF_ready, 4 * (t + 1))
                row_scales(hs[:, t:t + 1], hsi[:, t:t + 1], hF[:, t])
                dve.tensor_scalar(hr[:, t], hF[:, t], hsi[:, t:t + 1], ROUND, ALU.mult, ALU.add).then_inc(hr_ready, 1)
            dve.wait_ge(late_pe.sem, late_pe.at("oF", 1))
            for t in range(NT):
                xt = x[:, t, :].rearrange("p (r t) -> p t r", t=DT)
                step(dve.tensor_tensor(of[:, t].rearrange("p t (n r) -> p t n r", n=XH), PS[:, t, :].rearrange("p (t n r) -> p t n r", t=DT, n=XH),
                                       swb[:, GT * P:].rearrange("p (n t r) -> p t n r", t=DT, n=XH), ALU.mult))
                step(dve.scalar_tensor_tensor(xt, of[:, t], hs[:, t:t + 1], xt, ALU.mult, ALU.add))
            dve.sem_inc(x_done, 1)

        @block.tensor
        def _(pe):
            def transpose_tiles(src, bank, done):
                for kt in range(KT):
                    for t in range(NT):
                        at = (kt % 2) * T + t * P
                        mm = pe.transpose(PS[:, bank + kt // 2, at:at + P], src[:, t, kt * P:(kt + 1) * P], ident[:])
                mm.then_inc(done, 1)

            def attention(k, q, kk, v, col, wo, wo_in):
                def scores(t):
                    if t:
                        pe.wait_ge(s_masked, 4 * k + t)
                    for j in range(4):
                        for i in range(NT):
                            mm = pe.matmul(PS[:, j, i * T:(i + 1) * T], q(t, j)[:, i * P:(i + 1) * P], kk(t, j), start=True, stop=True)
                    mm.then_inc(s_ps, 1)

                def values(t, j):
                    if j % 2 == 0:
                        pe.wait_ge(pT_even, 8 * k + 2 * t + j // 2 + 1)
                    else:
                        pe.wait_ge(pT_odd, 8 * k + 2 * t + j // 2 + 1)
                    c = col(t, j)
                    pe.matmul(PS[:, 6, c:c + HD], PT[:, j, 0], v(t, j, 0), start=True, stop=True)
                    pe.matmul(PS[:, 7, c:c + HD], PT[:, j, 1], v(t, j, 0), start=True, stop=False)
                    mm = pe.matmul(PS[:, 7, c:c + HD], PT[:, j, 2], v(t, j, 1), start=False, stop=True)
                    if t == 3 and j == 3:
                        mm.then_inc(o_ps, 1)

                scores(0)
                for t in range(4):
                    if t < 3:
                        scores(t + 1)
                    pe.wait_ge(p_ready, 4 * k + t + 1)
                    for j in range(4):
                        if j >= 2 or t > 0:
                            prev = 8 * k + 2 * t + j // 2
                            pe.wait_ge(pT_odd if j % 2 else pT_even, prev)
                        for b, (i, kt) in enumerate(((0, 0), (1, 0), (1, 1))):
                            mm = pe.transpose(PS[:, 4 + j % 2, b * P:(b + 1) * P], pr[:, t % 2, j, i * T + kt * P:i * T + (kt + 1) * P], ident[:])
                        mm.then_inc(pT_ps, 1)
                        if j:
                            values(t, j - 1)
                    values(t, 3)
                for q_ in range(NT):
                    pe.wait_ge(on_ready, NT * k + q_ + 1)
                transpose_tiles(on, 0, oT_ps)
                pe.wait_ge(oT_ready, k + 1)
                pe.wait_ge(wo_in, 16)
                for i in range(NT):
                    for kt in range(KT):
                        mm = pe.matmul(PS[:, 2 + i, :], oT[:, kt, i * P:(i + 1) * P], wo[:, kt, :], start=(kt == 0), stop=(kt == KT - 1))
                mm.then_inc(proj_ps, 1)

            pe.wait_ge(ctxT_in, 16)
            pe.wait_ge(wkvA_in, 16)
            for m in range(KT):
                pe.matmul(PS[:, m // 2, (m % 2) * T:(m % 2 + 1) * T], wkvA[:, m * P:(m + 1) * P], ctxT[:], start=True, stop=True)
            for i in range(NT):
                mm = pe.matmul(PS[:, 2 + i, :], ctxT[:, i * P:(i + 1) * P], wkvA[:, D:2 * D], start=True, stop=True)
            mm.then_inc(kvA_ps, 1)
            pe.wait_ge(consts_ready, 2)
            pe.wait_ge(xn_ready, NT)
            pe.wait_ge(kvA_ready, 1)
            transpose_tiles(xn, 0, xnT_ps)
            pe.wait_ge(wqA_in, 16)
            pe.wait_ge(xnT_ready, 1)
            for m in range(KT):
                for kt in range(KT):
                    mm = pe.matmul(PS[:, 4 + m // 2, (m % 2) * T:(m % 2 + 1) * T], wqA[:, kt, m * P:(m + 1) * P], xnT[:, kt, :],
                                   start=(kt == 0), stop=(kt == KT - 1))
            mm.then_inc(q_ps, 1)
            pe.wait_ge(q_ready, 1)
            pe.wait_ge(kvA_ready, 2)
            attention(0, lambda t, j: qTA[32 * j:32 * j + 32, t, :], lambda t, j: kTA[32 * j:32 * j + 32, t, :],
                      lambda t, j, kt: vA[:, kt, (4 * t + j) * HD:(4 * t + j + 1) * HD], lambda t, j: (4 * t + j) * HD, woA, woA_in)

            pe.wait_ge(xn_ready, 2 * NT)
            transpose_tiles(xn, 0, xnT_ps)
            pe.wait_ge(wqkvB_in, 16)
            pe.wait_ge(xnT_ready, 2)
            for i in range(NT):
                for half, n in ((0, 512), (1, QKV - 512)):
                    for kt in range(KT):
                        mm = pe.matmul(PS[:, 2 * i + half, 0:n], xnT[:, kt, i * P:(i + 1) * P], wqkvB[:, kt, half * 512:half * 512 + n],
                                       start=(kt == 0), stop=(kt == KT - 1))
            mm.then_inc(qkv_ps, 1)
            pe.wait_ge(qk_ready, NT)
            for m in range(5):
                for i in range(NT):
                    at = (m % 2) * T + i * P
                    mm = pe.transpose(PS[:, 4 + m // 2, at:at + P], qk[:, i].rearrange("p h d -> p (h d)")[:, m * P:(m + 1) * P], ident[:])
            mm.then_inc(qkT_ps, 1)
            pe.wait_ge(qkT_ready, 2)
            attention(1, lambda t, j: qkT[32 * j:32 * j + 32, t, :], lambda t, j: qkT[32 * j:32 * j + 32, 4, :],
                      lambda t, j, kt: qkv[:, kt, (NH + KVH + j) * HD:(NH + KVH + j + 1) * HD], lambda t, j: (4 * j + t) * HD, woB, woB_in)

            pe.wait_ge(xn_ready, 3 * NT)
            transpose_tiles(xn, 0, xnT_ps)
            pe.wait_ge(xnT_ready, 3)
            pe.wait_ge(wr_in, 16)
            for t in range(NT):
                for kt in range(KT):
                    mm = pe.matmul(PS[:, 6, t * NE:(t + 1) * NE], xnT[:, kt, t * P:(t + 1) * P], wr[:, kt, :], start=(kt == 0), stop=(kt == KT - 1))
            mm.then_inc(logit_ps, 1)
            pe.wait_ge(wt_ready, 1)
            for t in range(NT):
                mm = pe.transpose(PS[0:NE, 7, t * P:(t + 1) * P], wt[:, t], ident[:])
            mm.then_inc(wT_ps, 1)
            pe.wait_ge(xL_ready, 1)

            def gate_up(n, i, b):
                pe.wait_ge(wL_ready, n * 2 + 2)
                wait(pe, hu_ready, n - 1)
                for m in range(3):
                    for j, (hi, lo) in enumerate(((gH, gL), (uH, uL))):
                        for kt in range(KT):
                            for c, (w, v) in enumerate(((hi, xH), (hi, xL), (lo, xH))):
                                mm = pe.matmul(PS[:, 3 * b + m, j * T:(j + 1) * T], w[:, b, kt, m, :], v[:, kt, :],
                                               start=(kt == 0 and c == 0), stop=(kt == KT - 1 and c == 2))
                mm.then_inc(gu_done, 1)

            def down(n, i, b):
                first, last = (isinstance(n, int) and n == e for e in (0, PAIRS - 1))
                pe.wait_ge(hL_ready, n + 1)
                pe.wait_ge(d_ready, n + 1)
                for t in range(NT):
                    for m in range(3):
                        for c, (h, w) in enumerate(((hH, dH), (hH, dL), (hL, dH))):
                            mm = pe.matmul(PS[:, 6 + t, :], h[:, b, m, t * P:(t + 1) * P], w[:, b, m, :],
                                           start=(first and m == 0 and c == 0), stop=(last and m == 2 and c == 2),
                                           skip_group_check=True)
                mm.then_inc(down_done, 1)

            def pe_pair(n, i, b):
                if not (isinstance(n, int) and n == PAIRS - 1):
                    gate_up(n + 1, i + b, 1 - b)
                down(n, i, b)

            gate_up(0, 0, 0)
            pairs(pe, pe_pair)

            pe.wait_ge(x_done, 3)
            for c in range(NCH):
                if c >= 4:
                    pe.wait_ge(kvTL_ready, c - 3)
                for j in range(4):
                    mm = pe.transpose(PS[:, c % 4, j * P:(j + 1) * P], kvr[:, 4 * c + j, :], ident[:])
                mm.then_inc(kvT_ps, 1)
            pe.wait_ge(xn_ready, 4 * NT)
            transpose_tiles(xn, 4, xnT_ps)
            pe.wait_ge(xnT_ready, 4)
            pe.wait_ge(kvTL_ready, NCH)

            def p1(n, i, b):
                pe.wait_ge(wqX_in[b], (i + 1) * 16)
                wait(pe, qh_ready, n - 1)
                for kt in range(KT):
                    mm = pe.matmul(PS[:, b, 0:T], wqX[:, b, kt, :], xnT[:, kt, :], start=(kt == 0), stop=(kt == KT - 1))
                mm.then_inc(p1_done, 1)

            def p2(n, i, b):
                pe.wait_ge(kcq_in[b], (i + 1) * 16)
                pe.wait_ge(qh_ready, n + 1)
                wait(pe, qm_ready, n - 1)
                for m in range(4):
                    mm = pe.matmul(PS[0:QP, 2 + 2 * b + m // 2, (m % 2) * T:(m % 2 + 1) * T], kcq[:, b, m * QP:(m + 1) * QP], qh[:, b, :],
                                   start=True, stop=True)
                mm.then_inc(p2_done, 1)

            def p3(n, i, b):
                pe.wait_ge(wr2_in[b], (i + 1) * 32)
                pe.wait_ge(qb_ready, n + 1)
                wait(pe, qr_ready, n)
                for m in range(4):
                    mm = pe.matmul(PS[0:XR, 6, 0:T], wqr[:, b, m, :], qb[:, b, m, :], start=(m == 0), stop=(m == 3))
                mm.then_inc(p3_done, 1)

            def p4(n, i, b):
                pe.wait_ge(qr_ready, n + 1)
                wait(pe, qp_ready, n)
                pe.matmul(PS[:, 7, 0:T], wkr[:, b, :], qr[:], start=True, stop=True).then_inc(p4_done, 1)

            def pe_head(n, i, b):
                late = not (isinstance(n, int) and n < 2)
                if not (isinstance(n, int) and n + 1 >= XH):
                    p1(n + 1, i + b, 1 - b)
                if late:
                    p3(n - 2, i - 1, b)
                p2(n, i, b)
                if late:
                    p4(n - 2, i - 1, b)

            p1(0, 0, 0)
            pairs(pe, pe_head, 2)
            for b in range(2):
                p3(XH - 2 + b, XH // 2 - 1, b)
                p4(XH - 2 + b, XH // 2 - 1, b)

            def scores(n, b, c):
                if c == 0:
                    pe.wait_ge(qsL_ready, n + 1)
                for q in range(NT):
                    wait(pe, sX_out, n * (NT * NCH) + (NT * c + q - 1))
                    for j, (w, v) in enumerate(((qsH, kvTH), (qsH, kvTL), (qsL, kvTH))):
                        mm = pe.matmul(PS[:, q, :], w[:, b, q * P:(q + 1) * P], v[:, c * CH:(c + 1) * CH], start=(j == 0), stop=(j == 2))
                    mm.then_inc(sX_ps, 1)

            def turn(n, c):
                pe.wait_ge(exp_done, n * NCH + (c + 1))
                wait(pe, pL_ready, n * NCH + (c - 1))
                for j in range(4):
                    for q in range(NT):
                        at = (j % 2) * T + q * P
                        mm = pe.transpose(PS[:, 2 + 2 * (c % 2) + j // 2, at:at + P], sp_[:, q, (4 * c + j) * P:(4 * c + j + 1) * P], ident[:])
                mm.then_inc(t_done, 1)

            def weigh(n, c):
                pe.wait_ge(pL_ready, n * NCH + (c + 1))
                if c == 0:
                    wait(pe, cT_ready, n)
                for j in range(4):
                    for k, (w, v) in enumerate(((kvH, pH), (kvH, pL), (kvL, pH))):
                        mm = pe.matmul(PS[:, 6, 0:T], w[:, 4 * c + j, :], v[:, c % 2, j, :],
                                       start=(c == 0 and j == 0 and k == 0), stop=(c == NCH - 1 and j == 3 and k == 2))
                mm.then_inc(v_done, 1)

            def out_weights(n, i, b):
                pe.wait_ge(wo2_in[b], (i + 1) * 32)
                wait(pe, oX_added, n * NT - 2)
                pe.matmul(PS[:, 7, :], kcv[:, b, :], woX[:, b, :], start=True, stop=True).then_inc(w3_ps, 1)

            def head_out(n, b, q, w3_of):
                pe.wait_ge(cT_ready, n + 1)
                pe.wait_ge(w3_ready, w3_of)
                if q:
                    pe.wait_ge(oX_added, n * NT + 1)
                pe.matmul(PS[:, 7, :], cT[:, b, q * P:(q + 1) * P], w3[:, b, :], start=True, stop=True).then_inc(oX_ps, 1)

            def pe_scores(n, i, b):
                last = isinstance(n, int) and n + 1 >= XH
                for c in range(NCH):
                    if c:
                        turn(n, c)
                    if not last:
                        scores(n + 1, 1 - b, c)
                    if c:
                        weigh(n, c - 1)
                    if c == 1 and not (isinstance(n, int) and n < 2):
                        head_out(n - 2, b, 1, n)
                    if c == 3:
                        out_weights(n, i, b)
                if not (isinstance(n, int) and n == 0):
                    head_out(n - 1, 1 - b, 0, n + 1)
                if not last:
                    turn(n + 1, 0)
                weigh(n, NCH - 1)

            pe.wait_ge(kvL_ready, 1)
            for c in range(NCH):
                scores(0, 0, c)
            turn(0, 0)
            pairs(pe, pe_scores)
            head_out(XH - 2, 0, 1, XH)
            pe.wait_ge(oX_added, (XH - 1) * NT)
            head_out(XH - 1, 1, 0, XH)
            head_out(XH - 1, 1, 1, XH)

            pe.wait_ge(xn_ready, 5 * NT)
            transpose_tiles(xn, 4, xnT_ps)
            pe.wait_ge(xnT_ready, 5)
            pe.wait_ge(win_in, 16)
            for t in range(NT):
                for kt in range(KT):
                    mm = pe.matmul(PS[:, 5, t * SH:(t + 1) * SH], xnT[:, kt, t * P:(t + 1) * P], win[:, kt, DI + XBC:DIN], start=(kt == 0), stop=(kt == KT - 1))
            mm.then_inc(ssm_pe.sem, 1)
            for m in range(CT):
                for kt in range(KT):
                    mm = pe.matmul(PS[:, m // 2, (m % 2) * T:(m % 2 + 1) * T], win[:, kt, DI + m * P:DI + (m + 1) * P], xnT[:, kt, :],
                                   start=(kt == 0), stop=(kt == KT - 1))
                if m % 2:
                    mm.then_inc(ssm_pe.sem, 1)
            for t in range(NT):
                if t:
                    pe.wait_ge(xp_ready, 2)
                for half in range(2):
                    for kt in range(KT):
                        mm = pe.matmul(PS[:, (6 if t == 0 else 0) + half, :], xnT[:, kt, t * P:(t + 1) * P], win[:, kt, half * 512:(half + 1) * 512],
                                       start=(kt == 0), stop=(kt == KT - 1))
                mm.then_inc(ssm_pe.sem, 1)
            pe.wait_ge(xp_ready, CT // 2)
            pe.wait_ge(ssm_act.sem, ssm_act.at("silu", IT))
            pe.wait_ge(ssm_dve.sem, ssm_dve.at("a", 1))
            for t in range(NT):
                for m in range(IT):
                    mm = pe.transpose(PS[:, 2 + 2 * t + m // 4, (m % 4) * P:(m % 4 + 1) * P], act_[:, m, t * P:(t + 1) * P], ident[:])
                mm.then_inc(ssm_pe.sem, 1)
            pe.wait_ge(ssm_act.sem, ssm_act.at("silu", CT))
            pe.wait_ge(zs_ready, NT)
            pe.matmul(PS[:, 1, 0:T], act_[:, IT, 0:P], act_[:, IT + 1, :], start=True, stop=True)
            pe.matmul(PS[:, 1, T:T + P], act_[:, IT, P:T], act_[:, IT + 1, P:T], start=True, stop=True).then_inc(ssm_pe.sem, 1)
            pe.wait_ge(ssm_dve.sem, ssm_dve.at("xdt", NT))
            pe.wait_ge(ssm_consts, 2)
            Y = PS[:, 0:4, :].rearrange("p (l b) (h c) -> p l (b h) c", l=NT, c=HP)
            xdth = xdt[:].rearrange("p t (h c) -> p t h c", c=HP)

            def log_decay(n, i, b):
                pe.wait_ge(ua_ready, n + 1)
                wait(pe, decay_ready, n - 1)
                pe.matmul(PS[:, 6 + b, 0:T], ua[:, b, 0, :], upto[:], start=True, stop=False)
                pe.matmul(PS[:, 6 + b, P:T], ua[:, b, 2, :], upto[:, 0:P], start=False, stop=True)
                pe.matmul(PS[:, 6 + b, T:T + P], ua[:, b, 1, :], upto[:, 0:P], start=True, stop=True).then_inc(d_ps, 1)

            def ssm_out(n, i, b):
                pe.wait_ge(mh_ready, n + 1)
                pe.matmul(Y[:, 0, n, :], mh[:, b, 0:P], xdth[:, 0, n, :], start=True, stop=True)
                pe.matmul(Y[:, 1, n, :], mh[:, b, P:T], xdth[:, 0, n, :], start=True, stop=False)
                pe.matmul(Y[:, 1, n, :], mh[:, b, T:], xdth[:, 1, n, :], start=False, stop=True).then_inc(y_ps, 1)

            def pe_ssm(n, i, b):
                if not (isinstance(n, int) and n == SH - 1):
                    log_decay(n + 1, i + b, 1 - b)
                ssm_out(n, i, b)
                turn_blocks(n, wblk[:, 0:SH * BG].rearrange("p (n e) d -> p n e d", n=SH)[:, n], b, BG)

            def turn_blocks(n, src, b, count):
                wait(pe, wqT_ready, n - 1)
                for m in range(count):
                    mm = pe.transpose(PSb[:, 4 + b, m * P:(m + 1) * P], src[:, m, :], identb[:])
                mm.then_inc(wqT_ps, 1)

            pe.wait_ge(identb_ready, 1)
            log_decay(0, 0, 0)
            pe.wait_ge(wblk_in, 64)
            pairs(pe, pe_ssm)
            turn_blocks(SH, wblk[:, SH * BG:], 0, BLOCKS - SH * BG)
            pe.wait_ge(wqT_ready, SH + 1)
            pe.wait_ge(late_dve.sem, late_dve.at("y", 1))
            for m in range(IT):
                for t in range(NT):
                    mm = pe.transpose(PS[:, 4 + m // 2, (m % 2) * T + t * P:(m % 2) * T + (t + 1) * P], y[:, t, m * P:(m + 1) * P], ident[:])
                if m % 4 == 3:
                    mm.then_inc(late_pe.sem, 1)
            pe.wait_ge(wout_in, 16)
            for m in range(IT):
                pe.wait_ge(late_act.sem, late_act.at("yT", m + 1))
                for t in range(NT):
                    mm = pe.matmul(PS[:, t, :], yT[:, m, t * P:(t + 1) * P], wout[:, m, :], start=(m == 0), stop=(m == IT - 1))
            mm.then_inc(late_pe.sem, 1)

            pe.wait_ge(late_act.sem, late_act.at("xq", 1))
            for m in range(KT):
                for t in range(NT):
                    mm = pe.transpose(PSb[:, 0, m * T + t * P:m * T + (t + 1) * P], xq[:, t, m * P:(m + 1) * P], identb[:])
            mm.then_inc(late_pe.sem, 1)
            pe.wait_ge(late_act.sem, late_act.at("xqT", 1))
            for n in range(4 * NT):
                t, c = n // 4, n % 4
                if n >= 2:
                    pe.wait_ge(us_ready, n - 1)
                for j in range(2):
                    for kt in range(KT):
                        mm = pe.matmul(PS[:, 2 + 2 * (n % 2) + j, 0:FC], xqT[:, kt, t * P:(t + 1) * P], w1T[:, kt, :, (4 * j + c) * FR:(4 * j + c + 1) * FR],
                                       start=(kt == 0), stop=(kt == KT - 1))
                mm.then_inc(late_pe.sem, 1)
            pe.wait_ge(us_ready, 4 * NT)
            pe.wait_ge(late_act.sem, late_act.at("hq", NT))
            for m in range(FT):
                for t in range(NT):
                    mm = pe.transpose(PSb[:, 4 + m // 4, (m % 4) * T + t * P:(m % 4) * T + (t + 1) * P], hq[:, t, m * P:(m + 1) * P], identb[:])
                if m % 4 == 3 or m == FT - 1:
                    mm.then_inc(late_pe.sem, 1)
            for m in range(FT):
                pe.wait_ge(late_act.sem, late_act.at("hqT", m // 4 + 1))
                for t in range(NT):
                    mm = pe.matmul(PS[:, t, :], hqT[:, m, t * P:(t + 1) * P], w2T[:, m, :], start=(m == 0), stop=(m == FT - 1))
            mm.then_inc(late_pe.sem, 1)


def rope_table(length, dim):
    import numpy as np
    e = np.arange(0, dim, 2, dtype=np.float32) / np.float32(dim)
    inv = (np.float32(1) / (10000.0 ** e.astype(np.float64)).astype(np.float32)).astype(np.float32)
    f = (np.arange(length, dtype=np.float32)[:, None] * inv[None, :]).astype(np.float64)
    return np.cos(f).astype(np.float32), np.sin(f).astype(np.float32)


def layouts(i):
    import numpy as np
    c = np.ascontiguousarray
    perm = [4 * g + t for t in range(4) for g in range(4)]
    wq = i["L0_attn_Wq"].reshape(NH, HD, D)[perm].reshape(D, D)
    cosK, sinK = rope_table(L, CD)
    sinK = np.concatenate([-sinK[:, :CD // 4], sinK[:, CD // 4:]], axis=1)
    cosB, sinB = rope_table(T, HD)

    cosQ, sinQ = rope_table(T, XQ)

    def tiles(t, sign=1):
        t = np.repeat(t, 2, axis=1).T.reshape(4, QP, T)
        return c(np.stack([sign * t[0], sign * t[1], t[2], t[3]], axis=1))

    def up(w):
        w = w.reshape(PAIRS, 2, KT, P, FI).transpose(0, 3, 2, 1, 4)
        left = w[..., P:].reshape(PAIRS, P, KT, 1, P)
        return c(np.concatenate([w[..., :P], left], axis=3).reshape(PAIRS, P, KT * 3 * P))

    def down(w):
        w = w.reshape(PAIRS, 2, FI, D)
        left = w[:, :, P:].reshape(PAIRS, 1, P, D)
        return c(np.concatenate([w[:, :, :P], left], axis=1).transpose(0, 2, 1, 3).reshape(PAIRS, P, 3 * D))

    return {
        "x": c(i["x"]), "ctx": c(i["ctx_512"][0]), "ctxT": c(i["ctx_512"][0, :T].T), "cosK": cosK, "sinK": sinK,
        "wqA": c(i["L0_xattn_Wq"].T), "wkvA": c(i["L0_xattn_Wkv_expand"].T), "woA": c(i["L0_xattn_Wout"].T),
        "wqkvB": c(np.concatenate([wq.T, i["L0_attn_Wk"].T, i["L0_attn_Wv"].T], axis=1)),
        "bqkv": c(np.concatenate([i["L0_attn_bq"].reshape(NH, HD)[perm].reshape(D), i["L0_attn_bk"], i["L0_attn_bv"]])),
        "bo": c(i["L0_attn_bo"]), "qn": c(i["L0_attn_qn_w"]), "kn": c(i["L0_attn_kn_w"]), "scale": c(i["L0_attn_scale"].reshape(1)),
        "cosB": cosB, "sinB": sinB, "woB": c(i["L0_attn_Wo"].T),
        "wqX": c(i["L1_xattn_Wq"].reshape(XH, XK, KT, P).transpose(0, 3, 2, 1).reshape(XH, P, KT * XK)), "kcq": c(i["L1_xattn_w_kc_q"]),
        "wqr": c(i["L1_xattn_W_qr"].reshape(XH, 4, QP, XR).transpose(0, 2, 1, 3).reshape(XH, QP, 4 * XR)),
        "wkr": c(i["L1_xattn_W_kr"].transpose(0, 2, 1)), "kcv": c(i["L1_xattn_w_kc_kv"]),
        "woX": c(i["L1_xattn_Wo"].T.reshape(XH, XK, D)), "cosQ": tiles(cosQ), "sinQ": tiles(sinQ, -1),
        "win": c(i["L1_attn_W_in"]), "cw": c(i["L1_attn_conv_w"].T.reshape(CT, P, CONV).transpose(1, 0, 2)),
        "cb": c(i["L1_attn_conv_b"].reshape(CT, P).T), "dtb": c(i["L1_attn_dt_bias"]), "alog": c(i["L1_attn_A_log"]),
        "dskip": c(i["L1_attn_D"]), "ns": c(i["L1_attn_norm_scale"].reshape(IT, P).T), "wout": c(i["L1_attn_W_out"]),
        "w1": c(i["L1_ffn_w_gate_up"]), "w2": c(i["L1_ffn_w_down"]),
        "wr": c(i["L0_ffn_router_w"].T), "wg": up(i["L0_ffn_w_gate"]), "wu": up(i["L0_ffn_w_up"]), "wd": down(i["L0_ffn_w_down"]),
    }


def kernel(**inputs):
    import numpy as np
    import concourse.bacc as bacc
    from concourse import mybir as mb
    from concourse.bass_utils import run_bass_kernel_spmd as run

    nc = bacc.Bacc("TRN2", target_bir_lowering=False, num_devices=1)
    arrays, aps = {}, {}
    for name, v in layouts({k: np.asarray(v) for k, v in inputs.items()}).items():
        arrays[f"in_{name}"] = v
        aps[name] = nc.dram_tensor(f"in_{name}", v.shape, mb.dt.from_np(v.dtype), kind="ExternalInput").ap()
    out = nc.dram_tensor("out_0", (1, T, D), F32, kind="ExternalOutput").ap()
    perceiver(nc, aps, out)
    r = run(nc, [arrays], core_ids=[0])
    return r.results[0]["out_0"]
```

```python
from contextlib import ExitStack

import concourse.bass as bass
from concourse import mybir

P = 128
D = 512
KT = D // P
T = 256
NT = T // P
CD = 128
L = 4096
NH, HD = 16, 32
KVH = 4
HALF = HD // 2
WINDOW = 64
CAUSAL = 3 * P
KEYS = (slice(0, P), slice(P, 3 * P))
QKV = (NH + 2 * KVH) * HD
LN_EPS, RMS_EPS = 1e-5, 1e-8
NEG = -1e30
NE, TOPK, FI = 32, 8, 192
XH, XK, XQ, XR = 16, 128, 384, 64
QT = XQ // P
LEFT = P // 2
CH = 512
NCH = L // CH
DI, DS, SH, HP, CONV = 1024, 128, 16, 64, 4
XBC = DI + 2 * DS
CT = XBC // P
IT = DI // P
DIN = DI + XBC + SH
FF = 1408
GT, DT, FT = 2 * FF // P, D // P, FF // P
FC = FF // 4
FR = FC // (2 * FF // P)
QMAX, QEPS = 127.0, 1e-8
ROUND = 1.5 * 2 ** 23
RB1, RB2 = 2 * FF // XH, D // XH
BLOCKS = KT * GT + FT * DT
BG = 8
STORES = 16 * (KT + DT + 2)
PAIRS = NE // 2

F32 = mybir.dt.float32
F32R = mybir.dt.float32r
BF16 = mybir.dt.bfloat16
ALU = mybir.AluOpType
ACT = mybir.ActivationFunctionType
AX = mybir.AxisListType


class Chain:

    def __init__(self, engine, sem):
        self.engine, self.sem, self.n, self.base = engine, sem, 0, 0

    def __call__(self, instruction):
        instruction.then_inc(self.sem, 1)
        self.n += 1
        self.engine.wait_ge(self.sem, self.base + self.n)


class Marks:

    def __init__(self, sem, **counts):
        self.sem, self.before, n = sem, {}, 0
        for name, count in counts.items():
            self.before[name] = n
            n += count

    def at(self, name, k):
        return self.before[name] + k


def perceiver(nc, a, out):
    ctx = ExitStack()
    with ctx:
        def sb(name, shape, dt=F32, at=ctx):
            return at.enter_context(nc.sbuf_tensor(name, shape, dt))

        def sem(name):
            return ctx.enter_context(nc.semaphore(name))

        PS = ctx.enter_context(nc.psum_tensor("PS", [P, 8, 512], F32))

        PSb = PS[:].rearrange("p b n -> p (b n)").bitcast(BF16).rearrange("p (b n) -> p b n", b=8)

        x = sb("x", [P, NT, D])
        xn = sb("xn", [P, NT, D])
        xnT = sb("xnT", [P, KT, T])
        ident = sb("ident", [P, P])
        ln_st = sb("ln_st", [P, NT, 6])
        ln_mv = sb("ln_mv", [P, NT, 2])
        ln_ve = sb("ln_ve", [P, NT])
        ln_rs = sb("ln_rs", [P, NT])
        mhalf = sb("mhalf", [P, NT])
        early = ExitStack()
        kvr = sb("kvr", [P, L // P, CD], F32, early)
        xH = sb("xH", [P, KT, T], F32R, early)
        xL = sb("xL", [P, KT, T], F32R, early)
        early.close()
        early = ExitStack()
        wblk = sb("wblk", [P, BLOCKS, P], BF16, early)
        early.close()
        win = sb("win", [P, KT, DIN])

        CC = 8
        arena = ExitStack()
        A = lambda n, s, d=F32: sb(n, s, d, arena)
        wqA = A("wqA", [P, KT, D]); wkvA = A("wkvA", [P, 2 * D]); woA = A("woA", [P, KT, D])
        ctxT = A("ctxT", [P, T])
        kTA = A("kTA", [P, KT, T]); vA = A("vA", [P, NT, D]); qTA = A("qTA", [P, KT, T])
        maskA = A("maskA", [P, CAUSAL])
        craw = A("craw", [P, 2, CC, CD]); ccos = A("ccos", [P, 2, CC, CD // 2]); csin = A("csin", [P, 2, CC, CD // 2])
        maskB = A("maskB", [P, CAUSAL])
        sm = A("sm", [P, 2, 4, CAUSAL]); pr = A("pr", [P, 2, 4, CAUSAL])
        nmx = A("nmx", [P, 2, NT, 4]); sums = A("sums", [P, NT, NH]); rec = A("rec", [P, NT, NH])
        PT = A("PT", [P, 4, 3, P])
        on = A("on", [P, NT, D]); oT = A("oT", [P, KT, T])
        wqkvB = A("wqkvB", [P, KT, QKV]); woB = A("woB", [P, KT, D])
        bqkv = A("bqkv", [P, QKV]); boB = A("boB", [P, D]); nw = A("nw", [P, NH + KVH, HD])
        scB = A("scB", [P, 1])
        qkv = A("qkv", [P, NT, QKV]); ms = A("ms", [P, NT, NH + KVH])
        rt = A("rt", [P, 4, (NH + KVH) * HALF]); qk = A("qk", [P, NT, NH + KVH, HD])
        cosB = A("cosB", [P, NT, HALF]); sinB = A("sinB", [P, NT, HALF])
        qkT = A("qkT", [P, 5, T])
        crot = A("crot", [P, CC, CD])
        arena.close()

        arena = ExitStack()
        rawG, rawU, rawD = (A(n, [P, 2, 1536]) for n in ("rawG", "rawU", "rawD"))
        gH, gL, uH, uL = (A(n, [P, 2, KT, 3, P], F32R) for n in ("gH", "gL", "uH", "uL"))
        dH, dL = (A(n, [P, 2, 3, D], F32R) for n in ("dH", "dL"))
        wb = A("wb", [P, 2, 3, T])
        sg, hu, hw = (A(n, [P, 3, T]) for n in ("sg", "hu", "hw"))
        hH, hL = (A(n, [P, 2, 3, T], F32R) for n in ("hH", "hL"))
        wr = A("wr", [P, KT, NE])
        lmx = A("lmx", [P, NT]); ex = A("ex", [P, NT, NE]); top = A("top", [P, NT, TOPK]); rest = A("rest", [P, NT, NE])
        wsum = A("wsum", [P, NT]); wt = A("wt", [P, NT, NE]); wT = A("wT", [NE, T])
        w_rows = nc.dram_tensor("w_rows", [NE, T], F32)
        arena.close()

        arena = ExitStack()
        kvH, kvL = (A(n, [P, L // P, CD], F32R) for n in ("kvH", "kvL"))
        kvTH, kvTL = (A(n, [P, L], F32R) for n in ("kvTH", "kvTL"))
        qp = A("qp", [P, XH, T])
        both = arena
        arena = ExitStack()
        wqX = A("wqX", [P, 2, KT, XK]); kcq = A("kcq", [P, 2, XQ]); wqr = A("wqr", [P, 2, QT, XR]); wkr = A("wkr", [XR, 2, CD])
        cosQ = A("cosQ", [P, QT, T]); sinQ = A("sinQ", [P, QT, T])
        qh = A("qh", [P, 2, T]); qm1 = A("qm1", [P, QT, T]); qm2 = A("qm2", [P, QT, T]); qb = A("qb", [P, 2, QT, T]); qr = A("qr", [XR, T])
        arena.close()
        arena = ExitStack()
        sp_ = A("scores", [P, NT, L])
        pH, pL = (A(n, [P, 2, 4, T], F32R) for n in ("pH", "pL"))
        qsH, qsL = (A(n, [P, 2, T], F32R) for n in ("qsH", "qsL"))
        kcv = A("kcv", [P, 2, CD]); woX = A("woX", [P, 2, D]); vT = A("vT", [XK, 2, T]); cT = A("cT", [P, 2, T])
        cmax = A("cmax", [P, NT, NCH]); nmX = A("nmX", [P, 2, NT]); csum = A("csum", [P, 2, NT, NCH]); recX = A("recX", [P, 2, NT])
        wrow1 = A("wrow1", [RB1 // 2, 2, D])
        wrow2 = A("wrow2", [RB2, FF])
        wint1 = A("wint1", [RB1 // 2, 2, D], BF16); wint2 = A("wint2", [RB2, FF], BF16)
        rounding = A("rounding", [P, 2]); wmax = A("wmax", [RB1 // 2, 4]); wscale, winv = (A(n, [RB1 // 2, 3]) for n in ("wscale", "winv"))
        blocks = nc.dram_tensor("blocks", [P, BLOCKS, P], BF16)
        s_rows = nc.dram_tensor("s_rows", [2 * FF + D], F32)
        arena.close()
        both.close()

        arena = ExitStack()
        wturned = A("wturned", [P, BLOCKS * P], BF16)
        w1T = wturned[:, 0:KT * GT * P].rearrange("p (k t r) -> p k t r", k=KT, r=P); w2T = wturned[:, KT * GT * P:].rearrange("p (k n) -> p k n", k=FT)
        identb = A("identb", [P, P], BF16)
        quant = arena
        arena = ExitStack()
        wout = A("wout", [P, IT, D])
        cw = A("cw", [P, CT, CONV]); cb = A("cb", [P, CT]); dtb = A("dtb", [P, SH]); alog = A("alog", [P, SH]); dskip = A("dskip", [P, SH])
        ns = A("ns", [P, IT])
        xp = A("xp", [P, CT, CONV - 1 + T]); cv = A("cv", [P, CT, T]); act_ = A("act_", [P, CT, T])
        zs = A("zs", [P, NT, DI]); xs = A("xs", [P, NT, DI]); xdt = A("xdt", [P, NT, DI]); y = A("y", [P, NT, DI])
        dtv = A("dtv", [P, NT, SH]); dta = A("dta", [P, NT, SH]); dte = A("dte", [P, NT, SH]); dts = A("dts", [P, NT, SH])
        dtq = A("dtq", [P, NT, SH]); dtp = A("dtp", [P, NT, SH]); av = A("av", [P, NT, SH])
        after = A("after", [P, P]); upto = A("upto", [P, T]); gm = A("gm", [P, 3 * P])
        ua = A("ua", [P, 2, 3, P]); ones = A("ones", [P, P]); decay = A("decay", [P, 2, 3 * P]); mh = A("mh", [P, 2, 3 * P])
        ss = A("ss", [P, NT]); yrs = A("yrs", [P, NT])
        yT = cv
        arena.close()
        arena = ExitStack()
        swb = A("swb", [P, (GT + DT) * P])
        sx = A("sx", [P, NT]); sxi = A("sxi", [P, NT]); xr = A("xr", [P, NT, D]); xq = A("xq", [P, NT, D], BF16); xqT = A("xqT", [P, KT, T], BF16)
        gs = A("gs", [P, 2, FC]); sgF = A("sgF", [P, 2, FC]); us = A("us", [P, 2, FC]); hF = A("hF", [P, NT, FF])
        hr = A("hr", [P, NT, FF]); hq = A("hq", [P, NT, FF], BF16); hqT = A("hqT", [P, FT, T], BF16)
        hs = A("hs", [P, NT]); hsi = A("hsi", [P, NT]); of = A("of", [P, NT, DT, P])
        arena.close()
        quant.close()

        x_in = sem("x_in"); ctxT_in = sem("ctxT_in"); wkvA_in = sem("wkvA_in"); wqA_in = sem("wqA_in")
        woA_in = sem("woA_in"); wqkvB_in = sem("wqkvB_in"); woB_in = sem("woB_in"); smallB_in = sem("smallB_in")
        ctx_in = [sem("ctx_in0"), sem("ctx_in1")]; ctx_used = sem("ctx_used")
        consts_ready = sem("consts_ready")
        ln_var = sem("ln_var"); ln_rstd = sem("ln_rstd"); xn_ready = sem("xn_ready")
        xnT_ps = sem("xnT_ps"); xnT_ready = sem("xnT_ready")
        kvA_ps = sem("kvA_ps"); kvA_ready = sem("kvA_ready")
        q_ps = sem("q_ps"); q_ready = sem("q_ready")
        s_ps = sem("s_ps"); s_masked = sem("s_masked"); max_ready = sem("max_ready"); p_ready = sem("p_ready")
        pT_ps = sem("pT_ps"); pT_even = sem("pT_even"); pT_odd = sem("pT_odd"); o_ps = sem("o_ps")
        on_ready = sem("on_ready"); oT_ps = sem("oT_ps"); oT_ready = sem("oT_ready"); proj_ps = sem("proj_ps")
        qkv_ps = sem("qkv_ps"); qk_ready = sem("qk_ready"); qkT_ps = sem("qkT_ps"); qkT_ready = sem("qkT_ready")
        msq = sem("msq"); rms_ready = sem("rms_ready")
        wr_in = sem("wr_in"); raw_in = [sem("raw_in0"), sem("raw_in1")]; wb_in = [sem("wb_in0"), sem("wb_in1")]
        wH_ready = sem("wH_ready"); wL_ready = sem("wL_ready"); d_ready = sem("d_ready"); dH_ready = sem("dH_ready")
        gu_done = sem("gu_done"); sg_ready = sem("sg_ready"); hu_ready = sem("hu_ready"); hw_ready = sem("hw_ready")
        hH_ready = sem("hH_ready"); hL_ready = sem("hL_ready"); down_done = sem("down_done")
        xH_ready = sem("xH_ready"); xL_ready = sem("xL_ready")
        logit_ps = sem("logit_ps"); lmax_ready = sem("lmax_ready"); ex_ready = sem("ex_ready"); wt_ready = sem("wt_ready")
        wT_ps = sem("wT_ps"); wT_ready = sem("wT_ready"); w_stored = sem("w_stored")
        kvT_ps = sem("kvT_ps"); kvTH_ready = sem("kvTH_ready"); kvTL_ready = sem("kvTL_ready"); kvH_ready = sem("kvH_ready"); kvL_ready = sem("kvL_ready")
        qtab_in = sem("qtab_in")
        wqX_in, kcq_in, wr2_in, wo2_in = ([sem(f"{n}{b}") for b in range(2)] for n in ("wqX_in", "kcq_in", "wr2_in", "wo2_in"))
        p1_done = sem("p1_done"); p2_done = sem("p2_done"); p3_done = sem("p3_done"); p4_done = sem("p4_done")
        qh_ready = sem("qh_ready"); qm_ready = sem("qm_ready"); qb_ready = sem("qb_ready"); qr_ready = sem("qr_ready"); qp_ready = sem("qp_ready")
        qsH_ready = sem("qsH_ready"); rec_ready = sem("rec_ready"); qsL_ready = sem("qsL_ready")
        sX_ps = sem("sX_ps"); sX_out = sem("sX_out"); nm_ready = sem("nm_ready"); exp_done = sem("exp_done")
        t_done = sem("t_done"); pH_ready = sem("pH_ready"); pL_ready = sem("pL_ready"); v_done = sem("v_done")
        cT_ready = sem("cT_ready"); vX_ps = sem("vX_ps"); vX_ready = sem("vX_ready"); oX_ps = sem("oX_ps"); oX_added = sem("oX_added")
        csum_done = sem("csum_done")
        win_in = sem("win_in"); wout_in = sem("wout_in"); ssm_in = sem("ssm_in")
        wrow_in = sem("wrow_in"); wmax_ready = sem("wmax_ready"); wscale_ready = sem("wscale_ready"); winv_ready = sem("winv_ready")
        wdiv_ready = sem("wdiv_ready"); wrnd_ready = sem("wrnd_ready"); wint_ready = sem("wint_ready"); wint_stored = sem("wint_stored")
        wblk_in = sem("wblk_in"); wqT_ps = sem("wqT_ps"); wqT_ready = sem("wqT_ready"); wqT_late = sem("wqT_late")
        swb_in = sem("swb_in")
        ssm_consts = sem("ssm_consts"); xp_ready = sem("xp_ready"); zs_ready = sem("zs_ready"); identb_ready = sem("identb_ready")
        ua_ready = sem("ua_ready"); d_ps = sem("d_ps"); decay_ready = sem("decay_ready"); mh_ready = sem("mh_ready"); y_ps = sem("y_ps")
        skip_ready = sem("skip_ready"); yrs_ready = sem("yrs_ready")
        gs_ready = sem("gs_ready"); us_ready = sem("us_ready"); hF_ready = sem("hF_ready")
        hr_ready = sem("hr_ready"); hq_ready = sem("hq_ready"); inner_done = sem("inner_done"); hqT_ready = sem("hqT_ready")
        x_done = sem("x_done"); stored = sem("stored")
        dve_step = sem("dve_step"); pool_step = sem("pool_step")

        ssm_pe = Marks(sem("ssm_pe"), dt=1, xbc=CT // 2, z=NT, xsT=NT, g=1)
        ssm_act = Marks(sem("ssm_act"), dte=2, tap=CT, silu=CT, xs=NT)
        ssm_dve = Marks(sem("ssm_dve"), dta=1, a=1, cv=CT, xdt=NT)
        late_pe = Marks(sem("late_pe"), yT=2, yo=1, xqT=1, guF=4 * NT, hqT=NT)
        late_act = Marks(sem("late_act"), ss=1, yT=IT, xq=NT, xqT=1, sgF=4 * NT)
        late_dve = Marks(sem("late_dve"), y=NT, ms=1, xr=NT)

        def wait(eng, s, value):
            if not (isinstance(value, int) and value <= 0):
                eng.wait_ge(s, value)

        def pairs(eng, step, first=1):
            for i in range(first):
                for b in range(2):
                    step(2 * i + b, i, b)
            with eng.Fori(first, PAIRS // 2 - 1) as i:
                for b in range(2):
                    step(i * 2 + b, i, b)
            for b in range(2):
                step(PAIRS - 2 + b, PAIRS // 2 - 1, b)

        block = ctx.enter_context(nc.Block())

        def ctx_chunk(sp, c):
            rows = slice(c * CC * P, (c + 1) * CC * P)
            sp.dma_start(craw[:, c % 2], a["ctx"][rows].rearrange("(t p) d -> p t d", p=P)).then_inc(ctx_in[c % 2], 16)
            sp.dma_start(ccos[:, c % 2], a["cosK"][rows].rearrange("(t p) d -> p t d", p=P)).then_inc(ctx_in[c % 2], 16)
            sp.dma_start(csin[:, c % 2], a["sinK"][rows].rearrange("(t p) d -> p t d", p=P)).then_inc(ctx_in[c % 2], 16)

        @block.sync
        def _(sp):
            sp.dma_start(x[:], a["x"].rearrange("o (t p) d -> p (o t) d", p=P)).then_inc(x_in, 16)
            sp.dma_start(ctxT[:], a["ctxT"]).then_inc(ctxT_in, 16)
            sp.dma_start(wkvA[:], a["wkvA"]).then_inc(wkvA_in, 16)
            sp.dma_start(wqA[:], a["wqA"].rearrange("(k p) n -> p k n", p=P)).then_inc(wqA_in, 16)
            for c in range(2):
                ctx_chunk(sp, c)
            sp.dma_start(woA[:], a["woA"].rearrange("(k p) n -> p k n", p=P)).then_inc(woA_in, 16)
            sp.dma_start(wqkvB[:], a["wqkvB"].rearrange("(k p) n -> p k n", p=P)).then_inc(wqkvB_in, 16)
            sp.dma_start(bqkv[:], a["bqkv"].partition_broadcast(P)).then_inc(smallB_in, 16)
            sp.dma_start(boB[:], a["bo"].partition_broadcast(P)).then_inc(smallB_in, 16)
            sp.dma_start(nw[:, 0:NH, :], a["qn"].unsqueeze(0).broadcast_to([NH, HD]).partition_broadcast(P)).then_inc(smallB_in, 16)
            sp.dma_start(nw[:, NH:, :], a["kn"].unsqueeze(0).broadcast_to([KVH, HD]).partition_broadcast(P)).then_inc(smallB_in, 16)
            sp.dma_start(scB[:], a["scale"].partition_broadcast(P)).then_inc(smallB_in, 16)
            sp.dma_start(cosB[:], a["cosB"].rearrange("(t p) i -> p t i", p=P)).then_inc(smallB_in, 16)
            sp.dma_start(sinB[:], a["sinB"].rearrange("(t p) i -> p t i", p=P)).then_inc(smallB_in, 16)
            sp.dma_start(woB[:], a["woB"].rearrange("(k p) n -> p k n", p=P)).then_inc(woB_in, 16)
            for c in range(2, L // P // CC):
                sp.wait_ge(ctx_used, c - 1)
                ctx_chunk(sp, c)
            def expert_weights(n, i, b):
                wait(sp, d_ready, n - 1)
                wait(sp, wL_ready, 2 * n - 2)
                sp.dma_start(rawG[:, b], a["wg"][n]).then_inc(raw_in[b], 16)
                sp.dma_start(rawU[:, b], a["wu"][n]).then_inc(raw_in[b], 16)
                sp.dma_start(rawD[:, b], a["wd"][n]).then_inc(raw_in[b], 16)

            sp.wait_ge(ctx_used, L // P // CC)
            sp.wait_ge(x_done, 1)
            for b in range(2):
                expert_weights(b, 0, b)
            sp.wait_ge(x_done, 2)
            sp.dma_start(wr[:], a["wr"].rearrange("(k p) n -> p k n", p=P)).then_inc(wr_in, 16)

            def token_weights(n, i, b):
                wait(sp, hw_ready, n - 1)
                for m in range(2):
                    sp.dma_start(wb[:, b, m], w_rows[2 * n + m].partition_broadcast(P)).then_inc(wb_in[b], 16)
                    sp.dma_start(wb[64 * m:64 * m + 64, b, 2], w_rows[2 * n + m].partition_broadcast(64)).then_inc(wb_in[b], 16)

            expert_weights(2, 1, 0)
            sp.wait_ge(wT_ready, 1)
            sp.dma_start(w_rows[:], wT[:]).then_inc(w_stored, 16)
            sp.wait_ge(w_stored, 16)
            for b in range(2):
                token_weights(b, 0, b)
            token_weights(2, 1, 0)
            expert_weights(3, 1, 1)
            token_weights(3, 1, 1)
            with sp.Fori(2, PAIRS // 2) as i:
                for b in range(2):
                    expert_weights(i * 2 + b, i, b)
                    token_weights(i * 2 + b, i, b)
            sp.wait_ge(x_done, 3)

            def load_wq(n, i, b):
                sp.dma_start(wqX[:, b], a["wqX"][n].rearrange("p (k n) -> p k n", k=KT)).then_inc(wqX_in[b], 16)

            def load_kcq(n, i, b):
                sp.dma_start(kcq[:, b], a["kcq"][n]).then_inc(kcq_in[b], 16)

            def load_rank(n, i, b):
                sp.dma_start(wqr[:, b], a["wqr"][n].rearrange("p (k n) -> p k n", k=QT)).then_inc(wr2_in[b], 16)
                sp.dma_start(wkr[:, b], a["wkr"][n]).then_inc(wr2_in[b], 16)

            for b in range(2):
                load_wq(b, 0, b)
                load_kcq(b, 0, b)
                if b == 0:
                    sp.dma_start(cosQ[:], a["cosQ"]).then_inc(qtab_in, 16)
                    sp.dma_start(sinQ[:], a["sinQ"]).then_inc(qtab_in, 16)
            load_rank(0, 0, 0)

            def head_loads(n, i, b):
                if not (isinstance(n, int) and n + 2 >= XH):
                    sp.wait_ge(p1_done, n + 1)
                    load_wq(n + 2, i + 1, b)
                if not (isinstance(n, int) and (n + 1 >= XH or n == 0)):
                    sp.wait_ge(p2_done, n)
                    load_kcq(n + 1, i + b, 1 - b)
                if not (isinstance(n, int) and n < 2):
                    sp.wait_ge(p4_done, n - 2)
                    load_rank(n - 1, i + b - 1, 1 - b)

            pairs(sp, head_loads, 2)
            sp.wait_ge(p4_done, XH - 2)
            load_rank(XH - 1, XH // 2 - 1, 1)

            def load_out(n, b):
                sp.dma_start(kcv[:, b], a["kcv"][n]).then_inc(wo2_in[b], 16)
                sp.dma_start(woX[:, b], a["woX"][n]).then_inc(wo2_in[b], 16)

            sp.wait_ge(qp_ready, XH)
            def load_rows(n):
                sp.dma_start(wrow1[:], a["w1"].rearrange("(n p j) d -> n p j d", n=XH, j=2)[n]).then_inc(wrow_in, 16)
                for t in range(DT):
                    sp.dma_start(wrow2[t * (RB2 // DT):(t + 1) * (RB2 // DT)], a["w2"].rearrange("(n r t) d -> n t r d", n=XH, t=DT)[n][t]).then_inc(wrow_in, 16)

            def rows1(n, k):
                return blocks[:, k * GT:(k + 1) * GT].rearrange("(n r) t d -> n r (t d)", n=XH)[n]

            def rows2(n, t):
                return blocks[:, KT * GT:].rearrange("(n r) (m t) d -> n t r m d", n=XH, t=DT)[n][t]

            scales1 = s_rows[0:2 * FF].rearrange("(n p j) -> n p j", n=XH, j=2)
            scales2 = s_rows[2 * FF:].rearrange("(n p j) -> n p j", n=XH, j=1)

            def store_rows(n):
                for k in range(KT):
                    sp.dma_start(rows1(n, k), wint1[:, :, k * P:(k + 1) * P]).then_inc(wint_stored, 16)
                for t in range(DT):
                    sp.dma_start(rows2(n, t), wint2[t * (RB2 // DT):(t + 1) * (RB2 // DT)].rearrange("p (m d) -> p m d", d=P)).then_inc(wint_stored, 16)
                sp.dma_start(scales1[n], wscale[:, 0:2]).then_inc(wint_stored, 16)
                sp.dma_start(scales2[n], wscale[0:RB2, 2:3]).then_inc(wint_stored, 16)

            for b in range(2):
                load_out(b, b)
            load_rows(0)
            sp.wait_ge(kvL_ready, 1)
            sp.dma_start(win[:], a["win"].rearrange("(k p) n -> p k n", p=P)).then_inc(win_in, 16)

            def out_loads(n, i, b):
                last = isinstance(n, int) and n + 1 >= XH
                sp.wait_ge(wint_ready, n + 1)
                if not last:
                    load_rows(n + 1)
                store_rows(n)
                if not (isinstance(n, int) and (n == 0 or last)):
                    sp.wait_ge(oX_ps, n * NT)
                    load_out(n + 1, 1 - b)

            pairs(sp, out_loads)
            sp.wait_ge(x_done, 4)
            sp.dma_start(cw[:], a["cw"]).then_inc(ssm_in, 16)
            sp.dma_start(cb[:], a["cb"]).then_inc(ssm_in, 16)
            sp.dma_start(dtb[:], a["dtb"].partition_broadcast(P)).then_inc(ssm_in, 16)
            sp.dma_start(alog[:], a["alog"].partition_broadcast(P)).then_inc(ssm_in, 16)
            sp.dma_start(dskip[:], a["dskip"].partition_broadcast(P)).then_inc(ssm_in, 16)
            sp.dma_start(ns[:], a["ns"]).then_inc(ssm_in, 16)
            sp.dma_start(wout[:], a["wout"].rearrange("(k p) n -> p k n", p=P)).then_inc(wout_in, 16)
            sp.wait_ge(wint_stored, STORES * XH)
            sp.wait_ge(ssm_pe.sem, ssm_pe.at("z", NT))
            for part in range(4):
                e = slice(part * BLOCKS // 4, (part + 1) * BLOCKS // 4)
                sp.dma_start(wblk[:, e], blocks[:, e]).then_inc(wblk_in, 16)
            sp.wait_ge(x_done, 5)
            sp.dma_start(swb[:], s_rows[:].partition_broadcast(P)).then_inc(swb_in, 16)
            sp.wait_ge(x_done, 6)
            sp.dma_start(out.rearrange("o (t p) d -> p (o t) d", p=P), x[:]).then_inc(stored, 16)
            sp.wait_ge(stored, 16)

        @block.gpsimd
        def _(pool):
            step = Chain(pool, pool_step)
            pool.memset(mhalf[:], -0.5).then_inc(consts_ready, 1)
            step(pool.memset(ident[:], 0.0))
            pool.affine_select(out=ident[:], in_=ident[:], compare_op=ALU.not_equal, fill=1.0, base=0,
                               pattern=[[-1, P]], channel_multiplier=1).then_inc(consts_ready, 1)
            pool.wait_ge(consts_ready, 2)

            def rstd(k):
                pool.wait_ge(ln_var, k + 1)
                pool.tensor_tensor(ln_rs[:], ln_ve[:], mhalf[:], ALU.pow).then_inc(ln_rstd, 1)

            rstd(0)
            step(pool.memset(maskA[:], 0.0))
            for q in range(NT):
                step(pool.affine_select(out=maskA[:, KEYS[q]], in_=maskA[:, KEYS[q]], compare_op=ALU.is_ge, fill=NEG, base=q * P,
                                        pattern=[[-1, (q + 1) * P]], channel_multiplier=1))
            for q in range(NT):
                ins = pool.affine_select(out=maskB[:, KEYS[q]], in_=maskA[:, KEYS[q]], compare_op=ALU.is_ge, fill=NEG, base=WINDOW - q * P,
                                         pattern=[[1, (q + 1) * P]], channel_multiplier=-1)
            ins.then_inc(consts_ready, 1)
            for c in range(L // P // CC):
                b = c % 2
                pool.wait_ge(ctx_in[b], 48 * (c // 2 + 1))
                dst = kvr[:, c * CC:(c + 1) * CC, :]
                def pair(t):
                    return t.rearrange("p t (i two) -> p t i two", two=2)
                def tab(t, lo, hi):
                    return t[:, :, lo:hi].unsqueeze(3).broadcast_to([P, CC, hi - lo, 2])
                pool.tensor_tensor(pair(crot[:, :, 0:64]), pair(craw[:, b, :, 64:128]), tab(csin[:, b], 0, 32), ALU.mult).then_inc(pool_step, 1)
                pool.tensor_tensor(pair(crot[:, :, 64:128]), pair(craw[:, b, :, 0:64]), tab(csin[:, b], 32, 64), ALU.mult).then_inc(pool_step, 1)
                step.n += 2
                step(pool.tensor_tensor(pair(dst), pair(craw[:, b]), tab(ccos[:, b], 0, 64), ALU.mult))
                ins = pool.tensor_tensor(dst, dst, crot[:], ALU.add)
                step(ins)
                pool.sem_inc(ctx_used, 1)
                if c == 1:
                    rstd(1)
            rstd(2)

            def split_down(n, i, b):
                pool.wait_ge(dH_ready, n + 1)
                pool.tensor_tensor(dL[:, b].rearrange("p m n -> p (m n)"), rawD[:, b], dH[:, b].rearrange("p m n -> p (m n)").bitcast(F32),
                                   ALU.subtract).then_inc(d_ready, 1)

            def pool_pair(n, i, b):
                pool.wait_ge(hu_ready, n + 1)
                pool.wait_ge(wb_in[b], (i + 1) * 64)
                wait(pool, hL_ready, n)
                pool.tensor_tensor(hw[:], hu[:], wb[:, b], ALU.mult).then_inc(hw_ready, 1)
                if not (isinstance(n, int) and n == PAIRS - 1):
                    split_down(n + 1, i + b, 1 - b)

            split_down(0, 0, 0)
            pairs(pool, pool_pair)
            rstd(3)
            pool.wait_ge(kvH_ready, 1)
            pool.tensor_tensor(kvL[:], kvr[:], kvH[:].bitcast(F32), ALU.subtract).then_inc(kvL_ready, 1)

            def round_rows(n, i, b):
                pool.wait_ge(winv_ready, n + 1)
                pool.tensor_tensor(wrow1[:], wrow1[:], winv[:, 0:2].unsqueeze(2).broadcast_to([RB1 // 2, 2, D]), ALU.mult).then_inc(wdiv_ready, 1)
                pool.tensor_scalar(wrow2[:], wrow2[:], winv[0:RB2, 2:3], ROUND, ALU.mult, ALU.add)
                pool.wait_ge(wdiv_ready, n + 1)
                pool.tensor_tensor(wrow1[:], wrow1[:], rounding[0:RB1 // 2].unsqueeze(2).broadcast_to([RB1 // 2, 2, D]), ALU.add).then_inc(wrnd_ready, 1)
                pool.wait_ge(wrnd_ready, n + 1)
                wait(pool, wint_stored, n * STORES)
                pool.tensor_tensor(wint1[:], wrow1[:], rounding[0:RB1 // 2].unsqueeze(2).broadcast_to([RB1 // 2, 2, D]), ALU.subtract)
                pool.tensor_tensor(wint2[:], wrow2[:], rounding[0:RB2, 0:1].broadcast_to([RB2, FF]), ALU.subtract).then_inc(wint_ready, 1)

            step(pool.memset(rounding[:], ROUND))
            pairs(pool, round_rows)
            rstd(4)
            step(pool.memset(after[:], 1.0))
            pool.affine_select(out=after[:], in_=after[:], compare_op=ALU.is_gt, fill=0.0, base=0, pattern=[[-1, P]],
                               channel_multiplier=1).then_inc(ssm_consts, 1)
            step(pool.memset(upto[:], 1.0))
            pool.affine_select(out=upto[:], in_=upto[:], compare_op=ALU.is_ge, fill=0.0, base=0, pattern=[[1, T]],
                               channel_multiplier=-1).then_inc(ssm_consts, 1)
            pool.tensor_copy(identb[:], ident[:]).then_inc(identb_ready, 1)
            step(pool.memset(ones[:], 1.0))
            step(pool.memset(xp[:, :, 0:CONV - 1], 0.0))
            pool.sem_inc(ssm_consts, 1)
            pool.wait_ge(ssm_dve.sem, ssm_dve.at("a", 1))
            pool.wait_ge(ssm_consts, 3)

            avh = av[:].transpose([0, 2, 1])

            def pool_ssm(n, i, b):
                wait(pool, d_ps, n - 1)
                pool.tensor_tensor(ua[:, b, 0:2], after[:].unsqueeze(1).broadcast_to([P, 2, P]),
                                   avh[:, n].unsqueeze(2).broadcast_to([P, NT, P]), ALU.mult)
                pool.tensor_tensor(ua[:, b, 2], ones[:], avh[:, n, 1:2].broadcast_to([P, P]), ALU.mult).then_inc(ua_ready, 1)

            pairs(pool, pool_ssm)
            pool.wait_ge(ssm_act.sem, ssm_act.at("xs", NT))
            for t in range(NT):
                pool.tensor_tensor(y[:, t].rearrange("p (h c) -> p h c", c=HP), xs[:, t].rearrange("p (h c) -> p h c", c=HP),
                                   dskip[:].unsqueeze(2).broadcast_to([P, SH, HP]), ALU.mult).then_inc(skip_ready, 1)
            pool.wait_ge(late_dve.sem, late_dve.at("ms", 1))
            pool.tensor_tensor(yrs[:], ss[:], mhalf[:], ALU.pow).then_inc(yrs_ready, 1)
            rstd(5)
            for n in range(4 * NT):
                pool.wait_ge(us_ready, n + 1)
                pool.wait_ge(late_act.sem, late_act.at("sgF", n + 1))
                pool.tensor_tensor(hF[:, n // 4, (n % 4) * FC:(n % 4 + 1) * FC].rearrange("p (r t) -> p t r", t=GT),
                                   sgF[:, n % 2].rearrange("p (t r) -> p t r", t=GT), us[:, n % 2].rearrange("p (t r) -> p t r", t=GT),
                                   ALU.mult).then_inc(hF_ready, 1)

        @block.scalar
        def _(act):
            act.wait_ge(kvA_ps, 1)
            act.activation(kTA[:], PS[:, 0:2, :].rearrange("p b (h t) -> p (b h) t", t=T), ACT.Copy).then_inc(kvA_ready, 1)
            act.activation(vA[:], PS[:, 2:4, :], ACT.Copy).then_inc(kvA_ready, 1)
            for k in range(2):
                act.wait_ge(xnT_ps, k + 1)
                act.activation(xnT[:], PS[:, 0:2, :].rearrange("p b (h t) -> p (b h) t", t=T), ACT.Copy).then_inc(xnT_ready, 1)
                if k == 0:
                    act.wait_ge(q_ps, 1)
                    act.activation(qTA[:], PS[:, 4:6, :].rearrange("p b (h t) -> p (b h) t", t=T), ACT.Copy).then_inc(q_ready, 1)
                else:
                    for q in range(NT):
                        act.wait_ge(msq, q + 1)
                        act.activation(ms[:, q], ms[:, q], ACT.Sqrt).then_inc(rms_ready, 1)
                    act.wait_ge(qkT_ps, 1)
                    act.activation(qkT[:, 0:4, :], PS[:, 4:6, :].rearrange("p b (h t) -> p (b h) t", t=T), ACT.Copy).then_inc(qkT_ready, 1)
                    act.activation(qkT[:, 4, :], PS[:, 6, 0:T], ACT.Copy).then_inc(qkT_ready, 1)

                def exps(t):
                    act.wait_ge(max_ready, 4 * k + t + 1)
                    for j in range(4):
                        for q in range(NT):
                            ins = act.activation(pr[:, t % 2, j, KEYS[q]], sm[:, t % 2, j, KEYS[q]], ACT.Exp,
                                                 bias=nmx[:, t % 2, q, j:j + 1], accum_out=sums[:, q, 4 * t + j:4 * t + j + 1])
                        ins.then_inc(p_ready, 1)

                exps(0)
                for t in range(4):
                    for j in (1, 3):
                        act.wait_ge(pT_ps, 16 * k + 4 * t + j + 1)
                        act.activation(PT[:, j], PS[:, 5, 0:3 * P].rearrange("p (b t) -> p b t", t=P), ACT.Copy).then_inc(pT_odd, 1)
                    if t < 3:
                        exps(t + 1)
                act.wait_ge(oT_ps, k + 1)
                act.activation(oT[:], PS[:, 0:2, :].rearrange("p b (h t) -> p (b h) t", t=T), ACT.Copy).then_inc(oT_ready, 1)

            act.wait_ge(xnT_ps, 3)
            src = PS[:, 0:2, :].rearrange("p b (h t) -> p (b h) t", t=T)
            act.activation(xnT[:], src, ACT.Copy).then_inc(xnT_ready, 1)
            act.wait_ge(xnT_ready, 3)
            act.activation(xH[:], xnT[:], ACT.Copy).then_inc(xH_ready, 1)

            def split_gate_up(n, i, b):
                act.wait_ge(raw_in[b], (i + 1) * 48)
                wait(act, gu_done, n - 1)
                act.activation(gH[:, b].rearrange("p k m n -> p (k m n)"), rawG[:, b], ACT.Copy).then_inc(wH_ready, 1)
                act.activation(uH[:, b].rearrange("p k m n -> p (k m n)"), rawU[:, b], ACT.Copy).then_inc(wH_ready, 1)
                wait(act, down_done, n - 1)
                act.activation(dH[:, b].rearrange("p m n -> p (m n)"), rawD[:, b], ACT.Copy).then_inc(dH_ready, 1)

            def act_pair(n, i, b):
                if not (isinstance(n, int) and n == PAIRS - 1):
                    split_gate_up(n + 1, i + b, 1 - b)
                if isinstance(n, int) and n == 0:
                    act.wait_ge(wT_ps, 1)
                    act.activation(wT[:], PS[0:NE, 7, 0:T], ACT.Copy).then_inc(wT_ready, 1)
                act.wait_ge(gu_done, n + 1)
                wait(act, hu_ready, n)
                act.activation(sg[:], PS[:, 3 * b:3 * b + 3, 0:T], ACT.Silu).then_inc(sg_ready, 1)
                act.wait_ge(hw_ready, n + 1)
                wait(act, down_done, n - 1)
                act.activation(hH[:, b], hw[:], ACT.Copy).then_inc(hH_ready, 1)

            split_gate_up(0, 0, 0)
            act.wait_ge(lmax_ready, 1)
            for t in range(NT):
                ins = act.activation(ex[:, t], PS[:, 6, t * NE:(t + 1) * NE], ACT.Exp, bias=lmx[:, t:t + 1])
            ins.then_inc(ex_ready, 1)
            pairs(act, act_pair)

            act.wait_ge(x_done, 3)
            for c in range(NCH):
                if c == 4:
                    act.wait_ge(xnT_ps, 4)
                    act.activation(xnT[:], PS[:, 4:6, :].rearrange("p b (h t) -> p (b h) t", t=T), ACT.Copy).then_inc(xnT_ready, 1)
                act.wait_ge(kvT_ps, c + 1)
                act.activation(kvTH[:, c * CH:(c + 1) * CH], PS[:, c % 4, :], ACT.Copy).then_inc(kvTH_ready, 1)
            act.activation(kvH[:], kvr[:], ACT.Copy).then_inc(kvH_ready, 1)

            def act_head(n, i, b):
                if not (isinstance(n, int) and n + 1 >= XH):
                    act.wait_ge(p1_done, n + 2)
                    wait(act, p2_done, n)
                    act.activation(qh[:, 1 - b], PS[:, 1 - b, 0:T], ACT.Copy).then_inc(qh_ready, 1)
                if not (isinstance(n, int) and n < 2):
                    low_rank(n - 2)

            def low_rank(n):
                act.wait_ge(p3_done, n + 1)
                wait(act, p4_done, n)
                act.activation(qr[:], PS[0:XR, 6, 0:T], ACT.Copy).then_inc(qr_ready, 1)
                act.wait_ge(p4_done, n + 1)
                act.activation(qp[:, n], PS[:, 7, 0:T], ACT.Copy).then_inc(qp_ready, 1)

            act.wait_ge(p1_done, 1)
            act.activation(qh[:, 0], PS[:, 0, 0:T], ACT.Copy).then_inc(qh_ready, 1)
            pairs(act, act_head, 2)
            low_rank(XH - 2)
            low_rank(XH - 1)

            def stage_query(n, b):
                act.activation(qsH[:, b], qp[:, n], ACT.Copy).then_inc(qsH_ready, 1)

            def exps_of(n, b, c):
                for q in range(NT):
                    if c == 0:
                        act.wait_ge(nm_ready, n * NT + (q + 1))
                    at = sp_[:, q, c * CH:(c + 1) * CH]
                    act.activation(at, at, ACT.Exp, bias=nmX[:, b, q:q + 1], accum_out=csum[:, b, q, c:c + 1]).then_inc(exp_done, 1)

            def context_out(n, b):
                act.wait_ge(v_done, n * NCH + NCH)
                act.activation(cT[:, b], PS[:, 6, 0:T], ACT.Copy).then_inc(cT_ready, 1)

            def values_out(n, b):
                act.wait_ge(vX_ps, n + 1)
                act.activation(vT[:, b], PS[:, 7, 0:T], ACT.Copy).then_inc(vX_ready, 1)

            def act_scores(n, i, b):
                wait(act, csum_done, n - 1)
                exps_of(n, b, 0)
                for c in range(NCH):
                    if c + 1 < NCH:
                        exps_of(n, b, c + 1)
                    act.wait_ge(t_done, n * NCH + (c + 1))
                    wait(act, v_done, n * NCH + (c - 1))
                    act.activation(pH[:, c % 2], PS[:, 2 + 2 * (c % 2):4 + 2 * (c % 2), :].rearrange("p k (h t) -> p (k h) t", t=T),
                                   ACT.Copy).then_inc(pH_ready, 1)
                    if c == 0 and not (isinstance(n, int) and n == 0):
                        context_out(n - 1, 1 - b)
                    if c == 2 and not (isinstance(n, int) and n == 0):
                        values_out(n - 1, 1 - b)
                    if c == 5 and not (isinstance(n, int) and n + 2 >= XH):
                        stage_query(n + 2, b)

            act.wait_ge(qp_ready, XH)
            for b in range(2):
                stage_query(b, b)
            pairs(act, act_scores)
            context_out(XH - 1, 1)
            values_out(XH - 1, 1)

            act.wait_ge(xnT_ps, 5)
            act.activation(xnT[:], PS[:, 4:6, :].rearrange("p b (h t) -> p (b h) t", t=T), ACT.Copy).then_inc(xnT_ready, 1)
            act.wait_ge(ssm_consts, 3)
            act.wait_ge(ssm_in, 96)
            act.wait_ge(ssm_dve.sem, ssm_dve.at("dta", 1))
            act.activation(dte[:], dta[:], ACT.Exp, scale=-1.0).then_inc(ssm_act.sem, 1)
            act.activation(alog[:], alog[:], ACT.Exp).then_inc(ssm_act.sem, 1)
            for m in range(CT // 2):
                act.wait_ge(ssm_pe.sem, ssm_pe.at("xbc", m + 1))
                act.activation(xp[:, 2 * m:2 * m + 2, CONV - 1:], PS[:, m, :].rearrange("p (c t) -> p c t", t=T), ACT.Copy).then_inc(xp_ready, 1)
                act.wait_ge(xp_ready, m + 1)
                for c in (2 * m, 2 * m + 1):
                    act.activation(cv[:, c], xp[:, c, 0:T], ACT.Identity, bias=cb[:, c:c + 1], scale=cw[:, c, 0:1]).then_inc(ssm_act.sem, 1)
            for m in range(CT):
                act.wait_ge(ssm_dve.sem, ssm_dve.at("cv", m + 1))
                act.activation(act_[:, m], cv[:, m], ACT.Silu).then_inc(ssm_act.sem, 1)
                if m in (3, 5):
                    t = (m - 3) // 2
                    act.wait_ge(ssm_pe.sem, ssm_pe.at("z", t + 1))
                    act.activation(zs[:, t], (PS[:, 6:8, :] if t == 0 else PS[:, 0:2, :]).rearrange("p b n -> p (b n)"), ACT.Silu).then_inc(zs_ready, 1)
            for t in range(NT):
                act.wait_ge(ssm_pe.sem, ssm_pe.at("xsT", t + 1))
                act.activation(xs[:, t], PS[:, 2 + 2 * t:4 + 2 * t, :].rearrange("p b n -> p (b n)"), ACT.Copy).then_inc(ssm_act.sem, 1)

            def act_ssm(n, i, b):
                act.wait_ge(d_ps, n + 1)
                wait(act, mh_ready, n - 1)
                act.activation(decay[:, b], PS[:, 6 + b, 0:3 * P], ACT.Exp).then_inc(decay_ready, 1)

            pairs(act, act_ssm)
            for n in range(SH - 3, SH + 1):
                blocks_of = slice(n * BG * P, min((n + 1) * BG, BLOCKS) * P)
                act.wait_ge(wqT_ps, n + 1)
                act.activation(wturned[:, blocks_of], PSb[:, 4 + n % 2, 0:blocks_of.stop - blocks_of.start], ACT.Copy).then_inc(wqT_late, 1)
            for t in range(NT):
                act.wait_ge(late_dve.sem, late_dve.at("y", t + 1))
                ins = act.activation(xdt[:, t], y[:, t], ACT.Square, accum_out=ss[:, t:t + 1])
            ins.then_inc(late_act.sem, 1)
            for m in range(IT):
                act.wait_ge(late_pe.sem, late_pe.at("yT", m // 4 + 1))
                act.activation(yT[:, m], PS[:, 4 + m // 2, (m % 2) * T:(m % 2 + 1) * T], ACT.Copy, scale=ns[:, m:m + 1]).then_inc(late_act.sem, 1)

            for t in range(NT):
                act.wait_ge(late_dve.sem, late_dve.at("xr", t + 1))
                act.activation(xq[:, t], xr[:, t], ACT.Copy, bias=-ROUND).then_inc(late_act.sem, 1)
            act.wait_ge(late_pe.sem, late_pe.at("xqT", 1))
            act.activation(xqT[:], PSb[:, 0, :].rearrange("p (k t) -> p k t", t=T), ACT.Copy).then_inc(late_act.sem, 1)

            def integers(t):
                act.wait_ge(hr_ready, t + 1)
                act.activation(hq[:, t], hr[:, t], ACT.Copy, bias=-ROUND).then_inc(hq_ready, 1)

            for n in range(4 * NT):
                act.wait_ge(gs_ready, n + 1)
                if n >= 2:
                    act.wait_ge(hF_ready, n - 1)
                act.activation(sgF[:, n % 2], gs[:, n % 2], ACT.Silu, scale=sx[:, n // 4:n // 4 + 1]).then_inc(late_act.sem, 1)
                if n == 6:
                    integers(0)
            for t in range(NT):
                if t:
                    integers(t)
                act.wait_ge(late_pe.sem, late_pe.at("hqT", t + 1))
                act.activation(hqT[:, :, t * P:(t + 1) * P], PSb[:, 6 - 2 * t:8 - 2 * t, :].rearrange("p b n -> p (b n)")[:, 0:FF].rearrange("p (k t) -> p k t", t=P),
                               ACT.Copy).then_inc(hqT_ready, 1)

        @block.vector
        def _(dve):
            step = Chain(dve, dve_step)

            def layer_norm(k, stats=True):
                if stats:
                    for t in range(NT):
                        ins = dve.bn_stats(ln_st[:, t, :], x[:, t, :])
                    step(ins)
                for t in range(NT):
                    ins = dve.bn_aggr(ln_mv[:, t, :], ln_st[:, t, :])
                step(ins)
                step(dve.tensor_scalar(ln_ve[:], ln_mv[:, :, 1], LN_EPS, None, ALU.add))
                dve.sem_inc(ln_var, 1)
                dve.wait_ge(ln_rstd, k + 1)
                for t in range(NT):
                    dve.tensor_scalar(xn[:, t, :], x[:, t, :], ln_mv[:, t, 0:1], ln_rs[:, t:t + 1],
                                      ALU.subtract, ALU.mult).then_inc(xn_ready, 1)

            def attention(k, scale, mask, head_major):
                def masked(t):
                    if t >= 2:
                        dve.wait_ge(p_ready, 16 * k + 4 * (t - 1))
                    for h in range(2):
                        two = slice(2 * h, 2 * h + 2)
                        dve.wait_ge(s_ps, 8 * k + 2 * t + h + 1)
                        ins = dve.scalar_tensor_tensor(sm[:, t % 2, two], PS[:, two, 0:CAUSAL], scale,
                                                       mask[:].unsqueeze(1).broadcast_to([P, 2, CAUSAL]), ALU.mult, ALU.add)
                        ins.then_inc(s_masked, 1)
                    dve.wait_ge(s_masked, 8 * k + 2 * t + 2)
                    for q in range(NT):
                        ins = dve.tensor_reduce(nmx[:, t % 2, q], sm[:, t % 2, :, KEYS[q]], AX.X, ALU.max, negate=True)
                    ins.then_inc(max_ready, 1)

                masked(0)
                masked(1)
                for t in range(4):
                    for j in (0, 2):
                        dve.wait_ge(pT_ps, 16 * k + 4 * t + j + 1)
                        dve.tensor_copy(PT[:, j], PS[:, 4, 0:3 * P].rearrange("p (b t) -> p b t", t=P)).then_inc(pT_even, 1)
                    if t + 2 < 4:
                        masked(t + 2)
                dve.wait_ge(o_ps, k + 1)
                step(dve.reciprocal(rec[:], sums[:]))
                for q in range(NT):
                    r = rec[:, q, :].rearrange("p (t j) -> p t j", t=4)
                    if not head_major:
                        r = r.transpose([0, 2, 1])
                    dve.tensor_tensor(on[:, q, :].rearrange("p (g h d) -> p g h d", g=4, d=HD),
                                      PS[:, 6 + q, :].rearrange("p (g h d) -> p g h d", g=4, d=HD),
                                      r.unsqueeze(3).broadcast_to([P, 4, 4, HD]), ALU.mult).then_inc(on_ready, 1)
                for q in range(NT):
                    dve.wait_ge(proj_ps, NT * k + q + 1)
                    step(dve.tensor_tensor(x[:, q, :], x[:, q, :], PS[:, 2 + q, :], ALU.add))
                    if q == NT - 1:
                        dve.sem_inc(x_done, 1)
                    ins = dve.bn_stats(ln_st[:, q, :], x[:, q, :])
                    ins.then_inc(dve_step, 1)
                    step.n += 1
                dve.wait_ge(dve_step, step.n)

            dve.wait_ge(x_in, 16)
            layer_norm(0)
            dve.wait_ge(consts_ready, 3)
            attention(0, HD ** -0.5, maskA, True)

            layer_norm(1, stats=False)
            dve.wait_ge(smallB_in, 112)
            for q in range(NT):
                step(dve.tensor_tensor(x[:, q, :], x[:, q, :], boB[:], ALU.add))
            NQK = NH + KVH
            for q in range(NT):
                dve.wait_ge(qkv_ps, q + 1)
                step(dve.tensor_tensor(qkv[:, q, :], PS[:, 2 * q:2 * q + 2, :].rearrange("p b n -> p (b n)")[:, 0:QKV], bqkv[:], ALU.add))
                src = qkv[:, q, 0:NQK * HD]
                step(dve.tensor_tensor(qk[:, q].rearrange("p h d -> p (h d)"), src, src, ALU.mult))
                step(dve.tensor_reduce(ms[:, q, :], qk[:, q], AX.X, ALU.add))
                step(dve.tensor_scalar(ms[:, q], ms[:, q], 1.0 / HD, RMS_EPS, ALU.mult, ALU.add))
                dve.sem_inc(msq, 1)
                src = src.rearrange("p (h d) -> p h d", d=HD)
                dve.wait_ge(rms_ready, q + 1)
                step(dve.reciprocal(ms[:, q], ms[:, q]))
                step(dve.tensor_tensor(src, src, ms[:, q, :].unsqueeze(2).broadcast_to([P, NQK, HD]), ALU.mult))
                step(dve.tensor_tensor(src, src, nw[:], ALU.mult))
                even, odd = (src.rearrange("p h (i two) -> p h i two", two=2)[:, :, :, e] for e in range(2))
                deven, dodd = (qk[:, q].rearrange("p h (i two) -> p h i two", two=2)[:, :, :, e] for e in range(2))
                c, s = (t[:, q, :].unsqueeze(1).broadcast_to([P, NQK, HALF]) for t in (cosB, sinB))
                r = [rt[:, i, :].rearrange("p (h i) -> p h i", i=HALF) for i in range(4)]
                dve.tensor_tensor(r[0], even, c, ALU.mult).then_inc(dve_step, 1)
                dve.tensor_tensor(r[1], odd, s, ALU.mult).then_inc(dve_step, 1)
                dve.tensor_tensor(r[2], even, s, ALU.mult).then_inc(dve_step, 1)
                step.n += 3
                step(dve.tensor_tensor(r[3], odd, c, ALU.mult))
                dve.tensor_tensor(deven, r[0], r[1], ALU.subtract).then_inc(dve_step, 1)
                step.n += 1
                step(dve.tensor_tensor(dodd, r[2], r[3], ALU.add))
                dve.sem_inc(qk_ready, 1)
            attention(1, scB[:, 0:1], maskB, False)

            layer_norm(2, stats=False)
            dve.wait_ge(xH_ready, 1)
            step(dve.tensor_tensor(xL[:], xnT[:], xH[:].bitcast(F32), ALU.subtract))
            dve.sem_inc(xL_ready, 1)

            def split_gate_up(n, i, b):
                for j, (raw, hi, lo) in enumerate(((rawG, gH, gL), (rawU, uH, uL))):
                    dve.wait_ge(wH_ready, n * 2 + (j + 1))
                    dve.tensor_tensor(lo[:, b].rearrange("p k m n -> p (k m n)"), raw[:, b],
                                      hi[:, b].rearrange("p k m n -> p (k m n)").bitcast(F32), ALU.subtract).then_inc(wL_ready, 1)

            def dve_pair(n, i, b):
                if not (isinstance(n, int) and n == PAIRS - 1):
                    split_gate_up(n + 1, i + b, 1 - b)
                dve.wait_ge(sg_ready, n + 1)
                wait(dve, hw_ready, n)
                dve.tensor_tensor(hu[:], sg[:], PS[:, 3 * b:3 * b + 3, T:2 * T], ALU.mult).then_inc(hu_ready, 1)
                dve.wait_ge(hH_ready, n + 1)
                dve.tensor_tensor(hL[:, b], hw[:], hH[:, b].bitcast(F32), ALU.subtract).then_inc(hL_ready, 1)

            split_gate_up(0, 0, 0)
            dve.wait_ge(logit_ps, 1)
            logits = PS[:, 6, 0:NT * NE].rearrange("p (t e) -> p t e", e=NE)
            step(dve.tensor_reduce(lmx[:], logits, AX.X, ALU.max))
            step(dve.tensor_scalar(lmx[:], lmx[:], -1.0, None, ALU.mult))
            dve.sem_inc(lmax_ready, 1)
            dve.wait_ge(ex_ready, 1)
            for t in range(NT):
                step(dve.max(top[:, t], ex[:, t]))
                step(dve.match_replace(rest[:, t], top[:, t], ex[:, t], 0.0))
            step(dve.tensor_tensor(rest[:], ex[:], rest[:], ALU.subtract))
            step(dve.tensor_reduce(wsum[:], rest[:], AX.X, ALU.add))
            step(dve.reciprocal(wsum[:], wsum[:]))
            step(dve.tensor_tensor(wt[:], rest[:], wsum[:].unsqueeze(2).broadcast_to([P, NT, NE]), ALU.mult))
            dve.sem_inc(wt_ready, 1)
            pairs(dve, dve_pair)
            dve.wait_ge(down_done, PAIRS)
            for t in range(NT):
                step(dve.tensor_tensor(x[:, t, :], x[:, t, :], PS[:, 6 + t, :], ALU.add))
            dve.sem_inc(x_done, 1)

            layer_norm(3)
            for c in range(NCH):
                dve.wait_ge(kvTH_ready, c + 1)
                dve.tensor_tensor(kvTL[:, c * CH:(c + 1) * CH], PS[:, c % 4, :], kvTH[:, c * CH:(c + 1) * CH].bitcast(F32),
                                  ALU.subtract).then_inc(kvTL_ready, 1)
            dve.wait_ge(qtab_in, 32)

            def dve_head(n, i, b):
                dve.wait_ge(p2_done, n + 1)
                wait(dve, qb_ready, n)
                big = PS[:, 2 + 2 * b:4 + 2 * b, :].rearrange("p k (h t) -> p (k h) t", t=T)
                dve.tensor_tensor(qm1[:], big[:, 0:QT], cosQ[:], ALU.mult)
                dve.tensor_tensor(qm2[:, 0], big[:, 1], sinQ[:, 0], ALU.mult)
                dve.tensor_tensor(qm2[:, 1], big[:, 0], sinQ[:, 1], ALU.mult)
                dve.tensor_tensor(qm2[0:LEFT, 2], big[LEFT:P, 2], sinQ[LEFT:P, 2], ALU.mult)
                dve.tensor_tensor(qm2[LEFT:P, 2], big[0:LEFT, 2], sinQ[0:LEFT, 2], ALU.mult).then_inc(qm_ready, 1)
                dve.wait_ge(qm_ready, n + 1)
                wait(dve, p3_done, n - 1)
                dve.tensor_tensor(qb[:, b], qm1[:], qm2[:], ALU.add).then_inc(qb_ready, 1)

            pairs(dve, dve_head, 2)

            def stage_query(n, b):
                dve.wait_ge(qsH_ready, n + 1)
                dve.tensor_tensor(qsL[:, b], qp[:, n], qsH[:, b].bitcast(F32), ALU.subtract).then_inc(qsL_ready, 1)

            def scores_out(n, c, b):
                for q in range(NT):
                    dve.wait_ge(sX_ps, n * (NT * NCH) + (NT * c + q + 1))
                    dve.tensor_scalar(sp_[:, q, c * CH:(c + 1) * CH], PS[:, q, :], 1.0, None, ALU.mult, ALU.max,
                                      accum_out=cmax[:, q, c:c + 1]).then_inc(sX_out, 1)
                    if c == NCH - 1:
                        dve.wait_ge(sX_out, n * (NT * NCH) + (NT * c + q + 1))
                        dve.tensor_reduce(nmX[:, b, q:q + 1], cmax[:, q], AX.X, ALU.max, negate=True).then_inc(nm_ready, 1)

            def add_out(n, b, q):
                dve.wait_ge(oX_ps, n * NT + (q + 1))
                dve.wait_ge(rec_ready, n + 1)
                wait(dve, oX_added, n * NT + q)
                dve.scalar_tensor_tensor(x[:, q, :], PS[:, 7, :], recX[:, b, q:q + 1], x[:, q, :], ALU.mult, ALU.add).then_inc(oX_added, 1)

            def dve_scores(n, i, b):
                last = isinstance(n, int) and n + 1 >= XH
                for c in range(NCH):
                    if not last:
                        scores_out(n + 1, c, 1 - b)
                    dve.wait_ge(pH_ready, n * NCH + (c + 1))
                    dve.tensor_tensor(pL[:, c % 2], PS[:, 2 + 2 * (c % 2):4 + 2 * (c % 2), :].rearrange("p k (h t) -> p (k h) t", t=T),
                                      pH[:, c % 2].bitcast(F32), ALU.subtract).then_inc(pL_ready, 1)
                    if c == 6 and not (isinstance(n, int) and n == 0):
                        add_out(n - 1, 1 - b, 0)
                    if c == 6 and not (isinstance(n, int) and n + 2 >= XH):
                        stage_query(n + 2, b)
                    if c == 2:
                        dve.wait_ge(wrow_in, n * (16 + 16 * DT) + (16 + 16 * DT))
                        dve.tensor_reduce(wmax[:, 0:2], wrow1[:], AX.X, ALU.max, apply_absolute_value=True)
                    if c == 4:
                        dve.tensor_reduce(wmax[0:RB2, 2:3], wrow2[:, 0:FF // 2], AX.X, ALU.max, apply_absolute_value=True)
                    if c == 5:
                        dve.tensor_reduce(wmax[0:RB2, 3:4], wrow2[:, FF // 2:], AX.X, ALU.max, apply_absolute_value=True).then_inc(wmax_ready, 1)
                        dve.wait_ge(wmax_ready, n * 2 + 1)
                        dve.tensor_tensor(wmax[0:RB2, 2:3], wmax[0:RB2, 2:3], wmax[0:RB2, 3:4], ALU.max).then_inc(wmax_ready, 1)
                        dve.wait_ge(wmax_ready, n * 2 + 2)
                        wait(dve, wint_stored, n * STORES)
                        dve.tensor_scalar(wscale[:], wmax[:, 0:3], 1.0 / QMAX, QEPS, ALU.mult, ALU.max).then_inc(wscale_ready, 1)
                        dve.wait_ge(wscale_ready, n + 1)
                        dve.reciprocal(winv[:], wscale[:]).then_inc(winv_ready, 1)
                dve.wait_ge(exp_done, n * (NT * NCH) + NT * NCH)
                dve.tensor_reduce(recX[:, b], csum[:, b], AX.X, ALU.add).then_inc(csum_done, 1)
                dve.wait_ge(csum_done, n + 1)
                dve.reciprocal(recX[:, b], recX[:, b]).then_inc(rec_ready, 1)
                if not (isinstance(n, int) and n == 0):
                    add_out(n - 1, 1 - b, 1)

            step(dve.memset(wmax[:], 0.0))
            for b in range(2):
                stage_query(b, b)
            for c in range(NCH):
                scores_out(0, c, 0)
            pairs(dve, dve_scores)
            add_out(XH - 1, 1, 0)
            add_out(XH - 1, 1, 1)
            dve.wait_ge(oX_added, NT * XH)
            dve.sem_inc(x_done, 1)

            layer_norm(4)

            def row_scales(scale, inverse, src):
                step(dve.tensor_reduce(scale, src, AX.X, ALU.max, apply_absolute_value=True))
                step(dve.tensor_scalar(scale, scale, 1.0 / QMAX, QEPS, ALU.mult, ALU.max))
                step(dve.reciprocal(inverse, scale))

            def turned_weights(n, b):
                dve.wait_ge(wqT_ps, n + 1)
                dve.tensor_copy(wturned[:, 0:SH * BG * P].rearrange("p (n d) -> p n d", n=SH)[:, n], PSb[:, 4 + b, :]).then_inc(wqT_ready, 1)

            dve.wait_ge(ssm_in, 96)
            dve.wait_ge(ssm_pe.sem, ssm_pe.at("dt", 1))
            step(dve.tensor_tensor(dtv[:], PS[:, 5, 0:NT * SH].rearrange("p (t h) -> p t h", h=SH),
                                   dtb[:].unsqueeze(1).broadcast_to([P, NT, SH]), ALU.add))
            step(dve.scalar_tensor_tensor(dta[:], dtv[:], -1.0, dtv[:], ALU.mult, ALU.max))
            dve.sem_inc(ssm_dve.sem, 1)
            dve.wait_ge(ssm_act.sem, ssm_act.at("dte", 2))
            step(dve.tensor_scalar(dts[:], dte[:], 2.0, None, ALU.add))
            step(dve.reciprocal(dts[:], dts[:]))
            step(dve.tensor_tensor(dts[:], dte[:], dts[:], ALU.mult))
            step(dve.tensor_tensor(dtq[:], dts[:], dts[:], ALU.mult))
            step(dve.tensor_scalar(dtp[:], dtq[:], 1.0 / 15, 1.0 / 13, ALU.mult, ALU.add))
            for k in (11, 9, 7, 5, 3, 1):
                step(dve.tensor_tensor(dtp[:], dtp[:], dtq[:], ALU.mult))
                step(dve.tensor_scalar(dtp[:], dtp[:], 1.0 / k, None, ALU.add))
            step(dve.scalar_tensor_tensor(dtp[:], dts[:], 2.0, dtp[:], ALU.mult, ALU.mult))
            step(dve.scalar_tensor_tensor(dtv[:], dtv[:], 0.0, dtp[:], ALU.max, ALU.add))
            step(dve.scalar_tensor_tensor(av[:], dtv[:], -1.0, alog[:].unsqueeze(1).broadcast_to([P, NT, SH]), ALU.mult, ALU.mult))
            dve.sem_inc(ssm_dve.sem, 1)
            for m in range(0, CT, 2):
                for k in range(1, CONV):
                    for c in (m, m + 1):
                        if k == 1:
                            dve.wait_ge(ssm_act.sem, ssm_act.at("tap", c + 1))
                        ins = dve.scalar_tensor_tensor(cv[:, c], xp[:, c, k:k + T], cw[:, c, k:k + 1], cv[:, c], ALU.mult, ALU.add)
                        if c == m:
                            ins.then_inc(dve_step, 1)
                            step.n += 1
                    step(ins)
                dve.sem_inc(ssm_dve.sem, 2)
            dve.wait_ge(ssm_pe.sem, ssm_pe.at("g", 1))
            dve.wait_ge(ssm_consts, 2)
            step(dve.tensor_tensor(gm[:, 0:T], PS[:, 1, 0:T], upto[:], ALU.mult))
            step(dve.tensor_tensor(gm[:, T:], PS[:, 1, T:T + P], upto[:, 0:P], ALU.mult))
            for t in range(NT):
                dve.wait_ge(ssm_act.sem, ssm_act.at("xs", t + 1))
                dve.tensor_tensor(xdt[:, t].rearrange("p (h c) -> p h c", c=HP), xs[:, t].rearrange("p (h c) -> p h c", c=HP),
                                  dtv[:, t].unsqueeze(2).broadcast_to([P, SH, HP]), ALU.mult).then_inc(ssm_dve.sem, 1)

            def dve_ssm(n, i, b):
                dve.wait_ge(decay_ready, n + 1)
                wait(dve, y_ps, n - 1)
                dve.tensor_tensor(mh[:, b], decay[:, b], gm[:], ALU.mult).then_inc(mh_ready, 1)
                if not (isinstance(n, int) and n < 3):
                    turned_weights(n - 3, 1 - b)

            pairs(dve, dve_ssm, 2)
            dve.wait_ge(skip_ready, NT)
            dve.wait_ge(zs_ready, NT)
            dve.wait_ge(y_ps, SH)
            for t in range(NT):
                step(dve.tensor_tensor(y[:, t], y[:, t], PS[:, 2 * t:2 * t + 2, :].rearrange("p b n -> p (b n)"), ALU.add))
                dve.tensor_tensor(y[:, t], y[:, t], zs[:, t], ALU.mult).then_inc(late_dve.sem, 1)
            dve.wait_ge(late_act.sem, late_act.at("ss", 1))
            step(dve.tensor_scalar(ss[:], ss[:], 1.0 / DI, LN_EPS, ALU.mult, ALU.add))
            dve.sem_inc(late_dve.sem, 1)
            dve.wait_ge(yrs_ready, 1)
            dve.wait_ge(late_pe.sem, late_pe.at("yo", 1))
            for t in range(NT):
                step(dve.scalar_tensor_tensor(x[:, t, :], PS[:, t, :], yrs[:, t:t + 1], x[:, t, :], ALU.mult, ALU.add))
            dve.sem_inc(x_done, 1)

            layer_norm(5)
            dve.wait_ge(xn_ready, 6 * NT)
            row_scales(sx[:], sxi[:], xn[:])
            for t in range(NT):
                dve.tensor_scalar(xr[:, t, :], xn[:, t, :], sxi[:, t:t + 1], ROUND, ALU.mult, ALU.add).then_inc(late_dve.sem, 1)
            dve.wait_ge(swb_in, 16)

            def rounded(t):
                dve.wait_ge(hF_ready, 4 * (t + 1))
                row_scales(hs[:, t:t + 1], hsi[:, t:t + 1], hF[:, t])
                dve.tensor_scalar(hr[:, t], hF[:, t], hsi[:, t:t + 1], ROUND, ALU.mult, ALU.add).then_inc(hr_ready, 1)

            def scale1(c):
                return swb[:, c * FC:(c + 1) * FC].rearrange("p (r t) -> p t r", t=GT)

            for n in range(4 * NT):
                t, c = n // 4, n % 4
                dve.wait_ge(late_pe.sem, late_pe.at("guF", n + 1))
                if n >= 2:
                    dve.wait_ge(late_act.sem, late_act.at("sgF", n - 1))
                    dve.wait_ge(hF_ready, n - 1)
                dve.tensor_tensor(gs[:, n % 2].rearrange("p (t r) -> p t r", t=GT), PS[:, 2 + 2 * (n % 2), 0:FC].rearrange("p (t r) -> p t r", t=GT), scale1(c), ALU.mult).then_inc(gs_ready, 1)
                dve.scalar_tensor_tensor(us[:, n % 2].rearrange("p (t r) -> p t r", t=GT), PS[:, 3 + 2 * (n % 2), 0:FC].rearrange("p (t r) -> p t r", t=GT), sx[:, t:t + 1], scale1(4 + c),
                                         ALU.mult, ALU.mult).then_inc(us_ready, 1)
                if n == 5:
                    rounded(0)
            rounded(1)
            for t in range(NT):
                dve.wait_ge(inner_done, t + 1)
                xt = x[:, t, :].rearrange("p (r t) -> p t r", t=DT)
                step(dve.tensor_tensor(of[:, t].rearrange("p t (n r) -> p t n r", n=XH), PS[:, t, :].rearrange("p (t n r) -> p t n r", t=DT, n=XH),
                                       swb[:, GT * P:].rearrange("p (n t r) -> p t n r", t=DT, n=XH), ALU.mult))
                step(dve.scalar_tensor_tensor(xt, of[:, t], hs[:, t:t + 1], xt, ALU.mult, ALU.add))
            dve.sem_inc(x_done, 1)

        @block.tensor
        def _(pe):
            def transpose_tiles(src, bank, done):
                for kt in range(KT):
                    for t in range(NT):
                        at = (kt % 2) * T + t * P
                        mm = pe.transpose(PS[:, bank + kt // 2, at:at + P], src[:, t, kt * P:(kt + 1) * P], ident[:])
                mm.then_inc(done, 1)

            def attention(k, q, kk, v, col, wo, wo_in):
                def scores(t):
                    for j in range(4):
                        if t and j % 2 == 0:
                            pe.wait_ge(s_masked, 8 * k + 2 * t + j // 2 - 1)
                        for i in range(NT):
                            mm = pe.matmul(PS[:, j, KEYS[i]], q(t, j)[:, i * P:(i + 1) * P], kk(t, j)[:, 0:(i + 1) * P], start=True, stop=True)
                        if j % 2:
                            mm.then_inc(s_ps, 1)

                def values(t, j):
                    if j % 2 == 0:
                        pe.wait_ge(pT_even, 8 * k + 2 * t + j // 2 + 1)
                    else:
                        pe.wait_ge(pT_odd, 8 * k + 2 * t + j // 2 + 1)
                    c = col(t, j)
                    pe.matmul(PS[:, 6, c:c + HD], PT[:, j, 0], v(t, j, 0), start=True, stop=True)
                    pe.matmul(PS[:, 7, c:c + HD], PT[:, j, 1], v(t, j, 0), start=True, stop=False)
                    mm = pe.matmul(PS[:, 7, c:c + HD], PT[:, j, 2], v(t, j, 1), start=False, stop=True)
                    if t == 3 and j == 3:
                        mm.then_inc(o_ps, 1)

                scores(0)
                scores(1)
                for t in range(4):
                    if t + 2 < 4:
                        scores(t + 2)
                    for j in range(4):
                        pe.wait_ge(p_ready, 16 * k + 4 * t + j + 1)
                        if j >= 2 or t > 0:
                            prev = 8 * k + 2 * t + j // 2
                            pe.wait_ge(pT_odd if j % 2 else pT_even, prev)
                        for b in range(3):
                            mm = pe.transpose(PS[:, 4 + j % 2, b * P:(b + 1) * P], pr[:, t % 2, j, b * P:(b + 1) * P], ident[:])
                        mm.then_inc(pT_ps, 1)
                        if j:
                            values(t, j - 1)
                    values(t, 3)
                for q_ in range(NT):
                    pe.wait_ge(on_ready, NT * k + q_ + 1)
                transpose_tiles(on, 0, oT_ps)
                pe.wait_ge(oT_ready, k + 1)
                pe.wait_ge(wo_in, 16)
                for i in range(NT):
                    for kt in range(KT):
                        mm = pe.matmul(PS[:, 2 + i, :], oT[:, kt, i * P:(i + 1) * P], wo[:, kt, :], start=(kt == 0), stop=(kt == KT - 1))
                    mm.then_inc(proj_ps, 1)

            pe.wait_ge(ctxT_in, 16)
            pe.wait_ge(wkvA_in, 16)
            for m in range(KT):
                pe.matmul(PS[:, m // 2, (m % 2) * T:(m % 2 + 1) * T], wkvA[:, m * P:(m + 1) * P], ctxT[:], start=True, stop=True)
            for i in range(NT):
                mm = pe.matmul(PS[:, 2 + i, :], ctxT[:, i * P:(i + 1) * P], wkvA[:, D:2 * D], start=True, stop=True)
            mm.then_inc(kvA_ps, 1)
            pe.wait_ge(consts_ready, 2)
            pe.wait_ge(xn_ready, NT)
            pe.wait_ge(kvA_ready, 1)
            transpose_tiles(xn, 0, xnT_ps)
            pe.wait_ge(wqA_in, 16)
            pe.wait_ge(xnT_ready, 1)
            for m in range(KT):
                for kt in range(KT):
                    mm = pe.matmul(PS[:, 4 + m // 2, (m % 2) * T:(m % 2 + 1) * T], wqA[:, kt, m * P:(m + 1) * P], xnT[:, kt, :],
                                   start=(kt == 0), stop=(kt == KT - 1))
            mm.then_inc(q_ps, 1)
            pe.wait_ge(q_ready, 1)
            pe.wait_ge(kvA_ready, 2)
            attention(0, lambda t, j: qTA[32 * j:32 * j + 32, t, :], lambda t, j: kTA[32 * j:32 * j + 32, t, :],
                      lambda t, j, kt: vA[:, kt, (4 * t + j) * HD:(4 * t + j + 1) * HD], lambda t, j: (4 * t + j) * HD, woA, woA_in)

            pe.wait_ge(xn_ready, 2 * NT)
            transpose_tiles(xn, 0, xnT_ps)
            pe.wait_ge(wqkvB_in, 16)
            pe.wait_ge(xnT_ready, 2)
            for i in range(NT):
                for half, n in ((0, 512), (1, QKV - 512)):
                    for kt in range(KT):
                        mm = pe.matmul(PS[:, 2 * i + half, 0:n], xnT[:, kt, i * P:(i + 1) * P], wqkvB[:, kt, half * 512:half * 512 + n],
                                       start=(kt == 0), stop=(kt == KT - 1))
                mm.then_inc(qkv_ps, 1)
            for i in range(NT):
                pe.wait_ge(qk_ready, i + 1)
                for m in range(5):
                    at = (m % 2) * T + i * P
                    mm = pe.transpose(PS[:, 4 + m // 2, at:at + P], qk[:, i].rearrange("p h d -> p (h d)")[:, m * P:(m + 1) * P], ident[:])
            mm.then_inc(qkT_ps, 1)
            pe.wait_ge(qkT_ready, 2)
            attention(1, lambda t, j: qkT[32 * j:32 * j + 32, t, :], lambda t, j: qkT[32 * j:32 * j + 32, 4, :],
                      lambda t, j, kt: qkv[:, kt, (NH + KVH + j) * HD:(NH + KVH + j + 1) * HD], lambda t, j: (4 * j + t) * HD, woB, woB_in)

            pe.wait_ge(xn_ready, 3 * NT)
            transpose_tiles(xn, 0, xnT_ps)
            pe.wait_ge(xnT_ready, 3)
            pe.wait_ge(wr_in, 16)
            for t in range(NT):
                for kt in range(KT):
                    mm = pe.matmul(PS[:, 6, t * NE:(t + 1) * NE], xnT[:, kt, t * P:(t + 1) * P], wr[:, kt, :], start=(kt == 0), stop=(kt == KT - 1))
            mm.then_inc(logit_ps, 1)
            pe.wait_ge(xL_ready, 1)

            def gate_up(n, i, b):
                pe.wait_ge(wL_ready, n * 2 + 2)
                wait(pe, hu_ready, n - 1)
                for m in range(3):
                    for j, (hi, lo) in enumerate(((gH, gL), (uH, uL))):
                        for kt in range(KT):
                            for c, (w, v) in enumerate(((hi, xH), (hi, xL), (lo, xH))):
                                mm = pe.matmul(PS[:, 3 * b + m, j * T:(j + 1) * T], w[:, b, kt, m, :], v[:, kt, :],
                                               start=(kt == 0 and c == 0), stop=(kt == KT - 1 and c == 2))
                mm.then_inc(gu_done, 1)

            def down(n, i, b):
                first, last = (isinstance(n, int) and n == e for e in (0, PAIRS - 1))
                pe.wait_ge(hL_ready, n + 1)
                pe.wait_ge(d_ready, n + 1)
                for t in range(NT):
                    for m in range(3):
                        for c, (h, w) in enumerate(((hH, dH), (hH, dL), (hL, dH))):
                            mm = pe.matmul(PS[:, 6 + t, :], h[:, b, m, t * P:(t + 1) * P], w[:, b, m, :],
                                           start=(first and m == 0 and c == 0), stop=(last and m == 2 and c == 2),
                                           skip_group_check=True)
                mm.then_inc(down_done, 1)

            def pe_pair(n, i, b):
                if not (isinstance(n, int) and n == PAIRS - 1):
                    gate_up(n + 1, i + b, 1 - b)
                else:
                    pe.wait_ge(hu_ready, n)
                    for c in range(3):
                        turn_context(c)
                down(n, i, b)

            def turn_context(c):
                for j in range(4):
                    mm = pe.transpose(PS[:, c % 4, j * P:(j + 1) * P], kvr[:, 4 * c + j, :], ident[:])
                mm.then_inc(kvT_ps, 1)

            gate_up(0, 0, 0)
            pe.wait_ge(wt_ready, 1)
            for t in range(NT):
                mm = pe.transpose(PS[0:NE, 7, t * P:(t + 1) * P], wt[:, t], ident[:])
            mm.then_inc(wT_ps, 1)
            pairs(pe, pe_pair)

            turn_context(3)
            pe.wait_ge(xn_ready, 4 * NT)
            transpose_tiles(xn, 4, xnT_ps)
            for c in range(4, NCH):
                pe.wait_ge(kvTL_ready, c - 3)
                turn_context(c)
            pe.wait_ge(xnT_ready, 4)

            def p1(n, i, b):
                pe.wait_ge(wqX_in[b], (i + 1) * 16)
                wait(pe, qh_ready, n - 1)
                for kt in range(KT):
                    mm = pe.matmul(PS[:, b, 0:T], wqX[:, b, kt, :], xnT[:, kt, :], start=(kt == 0), stop=(kt == KT - 1))
                mm.then_inc(p1_done, 1)

            def p2(n, i, b):
                pe.wait_ge(kcq_in[b], (i + 1) * 16)
                pe.wait_ge(qh_ready, n + 1)
                wait(pe, qm_ready, n - 1)
                for m in range(QT):
                    mm = pe.matmul(PS[:, 2 + 2 * b + m // 2, (m % 2) * T:(m % 2 + 1) * T], kcq[:, b, m * P:(m + 1) * P], qh[:, b, :],
                                   start=True, stop=True)
                mm.then_inc(p2_done, 1)

            def p3(n, i, b):
                pe.wait_ge(wr2_in[b], (i + 1) * 32)
                pe.wait_ge(qb_ready, n + 1)
                wait(pe, qr_ready, n)
                for m in range(QT):
                    mm = pe.matmul(PS[0:XR, 6, 0:T], wqr[:, b, m, :], qb[:, b, m, :], start=(m == 0), stop=(m == QT - 1))
                mm.then_inc(p3_done, 1)

            def p4(n, i, b):
                pe.wait_ge(qr_ready, n + 1)
                wait(pe, qp_ready, n)
                pe.matmul(PS[:, 7, 0:T], wkr[:, b, :], qr[:], start=True, stop=True).then_inc(p4_done, 1)

            def pe_head(n, i, b):
                late = not (isinstance(n, int) and n < 2)
                if not (isinstance(n, int) and n + 1 >= XH):
                    p1(n + 1, i + b, 1 - b)
                if late:
                    p3(n - 2, i - 1, b)
                p2(n, i, b)
                if late:
                    p4(n - 2, i - 1, b)

            pe.wait_ge(kvTL_ready, NCH)
            p1(0, 0, 0)
            pairs(pe, pe_head, 2)
            for b in range(2):
                p3(XH - 2 + b, XH // 2 - 1, b)
                p4(XH - 2 + b, XH // 2 - 1, b)

            def scores(n, b, c):
                if c == 0:
                    pe.wait_ge(qsL_ready, n + 1)
                for q in range(NT):
                    wait(pe, sX_out, n * (NT * NCH) + (NT * c + q - 1))
                    for j, (w, v) in enumerate(((qsH, kvTH), (qsH, kvTL), (qsL, kvTH))):
                        mm = pe.matmul(PS[:, q, :], w[:, b, q * P:(q + 1) * P], v[:, c * CH:(c + 1) * CH], start=(j == 0), stop=(j == 2))
                    mm.then_inc(sX_ps, 1)

            def turn(n, c):
                wait(pe, pL_ready, n * NCH + (c - 1))
                for q in range(NT):
                    pe.wait_ge(exp_done, n * (NT * NCH) + (NT * c + q + 1))
                    for j in range(4):
                        at = (j % 2) * T + q * P
                        mm = pe.transpose(PS[:, 2 + 2 * (c % 2) + j // 2, at:at + P], sp_[:, q, (4 * c + j) * P:(4 * c + j + 1) * P], ident[:])
                mm.then_inc(t_done, 1)

            def weigh(n, c):
                pe.wait_ge(pL_ready, n * NCH + (c + 1))
                if c == 0:
                    wait(pe, cT_ready, n)
                for j in range(4):
                    for k, (w, v) in enumerate(((kvH, pH), (kvH, pL), (kvL, pH))):
                        mm = pe.matmul(PS[:, 6, 0:T], w[:, 4 * c + j, :], v[:, c % 2, j, :],
                                       start=(c == 0 and j == 0 and k == 0), stop=(c == NCH - 1 and j == 3 and k == 2))
                mm.then_inc(v_done, 1)

            def values(n, b, loads):
                pe.wait_ge(wo2_in[b], loads * 32)
                pe.wait_ge(cT_ready, n + 1)
                wait(pe, oX_added, n * NT)
                pe.matmul(PS[:, 7, 0:T], kcv[:, b, :], cT[:, b, :], start=True, stop=True).then_inc(vX_ps, 1)

            def head_out(n, b, q):
                if q:
                    pe.wait_ge(oX_added, n * NT + 1)
                else:
                    pe.wait_ge(vX_ready, n + 1)
                pe.matmul(PS[:, 7, :], vT[:, b, q * P:(q + 1) * P], woX[:, b, :], start=True, stop=True).then_inc(oX_ps, 1)

            def pe_scores(n, i, b):
                last = isinstance(n, int) and n + 1 >= XH
                for c in range(NCH):
                    if c:
                        turn(n, c)
                    if not last:
                        scores(n + 1, 1 - b, c)
                    if c:
                        weigh(n, c - 1)
                    if not (isinstance(n, int) and n == 0):
                        if c == 1:
                            values(n - 1, 1 - b, i + b)
                        if c in (4, 7):
                            head_out(n - 1, 1 - b, c // 7)
                if not last:
                    turn(n + 1, 0)
                weigh(n, NCH - 1)

            pe.wait_ge(kvL_ready, 1)
            for c in range(NCH):
                scores(0, 0, c)
            turn(0, 0)
            pairs(pe, pe_scores)
            values(XH - 1, 1, XH // 2)
            for q in range(NT):
                head_out(XH - 1, 1, q)

            pe.wait_ge(xn_ready, 5 * NT)
            transpose_tiles(xn, 4, xnT_ps)
            pe.wait_ge(xnT_ready, 5)
            pe.wait_ge(win_in, 16)
            for t in range(NT):
                for kt in range(KT):
                    mm = pe.matmul(PS[:, 5, t * SH:(t + 1) * SH], xnT[:, kt, t * P:(t + 1) * P], win[:, kt, DI + XBC:DIN], start=(kt == 0), stop=(kt == KT - 1))
            mm.then_inc(ssm_pe.sem, 1)
            for m in range(CT):
                for kt in range(KT):
                    mm = pe.matmul(PS[:, m // 2, (m % 2) * T:(m % 2 + 1) * T], win[:, kt, DI + m * P:DI + (m + 1) * P], xnT[:, kt, :],
                                   start=(kt == 0), stop=(kt == KT - 1))
                if m % 2:
                    mm.then_inc(ssm_pe.sem, 1)
            for t in range(NT):
                if t:
                    pe.wait_ge(xp_ready, 2)
                for half in range(2):
                    for kt in range(KT):
                        mm = pe.matmul(PS[:, (6 if t == 0 else 0) + half, :], xnT[:, kt, t * P:(t + 1) * P], win[:, kt, half * 512:(half + 1) * 512],
                                       start=(kt == 0), stop=(kt == KT - 1))
                mm.then_inc(ssm_pe.sem, 1)
            pe.wait_ge(xp_ready, CT // 2)
            pe.wait_ge(ssm_act.sem, ssm_act.at("silu", IT))
            pe.wait_ge(ssm_dve.sem, ssm_dve.at("a", 1))
            for t in range(NT):
                for m in range(IT):
                    mm = pe.transpose(PS[:, 2 + 2 * t + m // 4, (m % 4) * P:(m % 4 + 1) * P], act_[:, m, t * P:(t + 1) * P], ident[:])
                mm.then_inc(ssm_pe.sem, 1)
            pe.wait_ge(ssm_act.sem, ssm_act.at("silu", CT))
            pe.wait_ge(zs_ready, NT)
            pe.matmul(PS[:, 1, 0:T], act_[:, IT, 0:P], act_[:, IT + 1, :], start=True, stop=True)
            pe.matmul(PS[:, 1, T:T + P], act_[:, IT, P:T], act_[:, IT + 1, P:T], start=True, stop=True).then_inc(ssm_pe.sem, 1)
            pe.wait_ge(ssm_consts, 2)
            Y = PS[:, 0:4, :].rearrange("p (l b) (h c) -> p l (b h) c", l=NT, c=HP)
            xdth = xdt[:].rearrange("p t (h c) -> p t h c", c=HP)

            def log_decay(n, i, b):
                pe.wait_ge(ua_ready, n + 1)
                wait(pe, decay_ready, n - 1)
                pe.matmul(PS[:, 6 + b, 0:T], ua[:, b, 0, :], upto[:], start=True, stop=False)
                pe.matmul(PS[:, 6 + b, P:T], ua[:, b, 2, :], upto[:, 0:P], start=False, stop=True)
                pe.matmul(PS[:, 6 + b, T:T + P], ua[:, b, 1, :], upto[:, 0:P], start=True, stop=True).then_inc(d_ps, 1)

            def ssm_out(n, i, b):
                pe.wait_ge(mh_ready, n + 1)
                pe.matmul(Y[:, 0, n, :], mh[:, b, 0:P], xdth[:, 0, n, :], start=True, stop=True)
                pe.matmul(Y[:, 1, n, :], mh[:, b, P:T], xdth[:, 0, n, :], start=True, stop=False)
                pe.matmul(Y[:, 1, n, :], mh[:, b, T:], xdth[:, 1, n, :], start=False, stop=True).then_inc(y_ps, 1)

            def pe_ssm(n, i, b):
                if not (isinstance(n, int) and n == SH - 1):
                    log_decay(n + 1, i + b, 1 - b)
                ssm_out(n, i, b)
                if isinstance(n, int) and n == 2:
                    pe.wait_ge(wblk_in, 64)
                if not (isinstance(n, int) and n < 2):
                    turn_blocks(n - 2, groups[:, n - 2], b, BG)

            groups = wblk[:, 0:SH * BG].rearrange("p (n e) d -> p n e d", n=SH)

            def turn_blocks(n, src, b, count, ready=None):
                wait(pe, wqT_ready, n - 1 if ready is None else ready)
                for m in range(count):
                    mm = pe.transpose(PSb[:, 4 + b, m * P:(m + 1) * P], src[:, m, :], identb[:])
                mm.then_inc(wqT_ps, 1)

            pe.wait_ge(identb_ready, 1)
            log_decay(0, 0, 0)
            pe.wait_ge(ssm_dve.sem, ssm_dve.at("xdt", NT))
            pairs(pe, pe_ssm, 2)
            turn_blocks(SH - 2, groups[:, SH - 2], 0, BG)
            pe.wait_ge(wqT_late, 1)
            turn_blocks(SH - 1, groups[:, SH - 1], 1, BG, ready=SH - 3)
            pe.wait_ge(wqT_late, 2)
            turn_blocks(SH, wblk[:, SH * BG:], 0, BLOCKS - SH * BG, ready=SH - 3)
            pe.wait_ge(wqT_late, 4)
            for t in range(NT):
                pe.wait_ge(late_dve.sem, late_dve.at("y", t + 1))
                for m in range(IT):
                    mm = pe.transpose(PS[:, 4 + m // 2, (m % 2) * T + t * P:(m % 2) * T + (t + 1) * P], y[:, t, m * P:(m + 1) * P], ident[:])
                    if t == NT - 1 and m % 4 == 3:
                        mm.then_inc(late_pe.sem, 1)
            pe.wait_ge(wout_in, 16)
            for m in range(IT):
                pe.wait_ge(late_act.sem, late_act.at("yT", m + 1))
                for t in range(NT):
                    mm = pe.matmul(PS[:, t, :], yT[:, m, t * P:(t + 1) * P], wout[:, m, :], start=(m == 0), stop=(m == IT - 1))
            mm.then_inc(late_pe.sem, 1)

            for t in range(NT):
                pe.wait_ge(late_act.sem, late_act.at("xq", t + 1))
                for m in range(KT):
                    mm = pe.transpose(PSb[:, 0, m * T + t * P:m * T + (t + 1) * P], xq[:, t, m * P:(m + 1) * P], identb[:])
            mm.then_inc(late_pe.sem, 1)
            pe.wait_ge(late_act.sem, late_act.at("xqT", 1))
            for n in range(4 * NT):
                t, c = n // 4, n % 4
                if n >= 2:
                    pe.wait_ge(us_ready, n - 1)
                for j in range(2):
                    for kt in range(KT):
                        mm = pe.matmul(PS[:, 2 + 2 * (n % 2) + j, 0:FC], xqT[:, kt, t * P:(t + 1) * P], w1T[:, kt, :, (4 * j + c) * FR:(4 * j + c + 1) * FR],
                                       start=(kt == 0), stop=(kt == KT - 1))
                mm.then_inc(late_pe.sem, 1)

            def turn_inner(t):
                pe.wait_ge(hq_ready, t + 1)
                for m in range(FT):
                    mm = pe.transpose(PSb[:, 6 - 2 * t + m // 8, (m % 8) * P:(m % 8 + 1) * P], hq[:, t, m * P:(m + 1) * P], identb[:])
                mm.then_inc(late_pe.sem, 1)

            def down_inner(t):
                pe.wait_ge(hqT_ready, t + 1)
                for m in range(FT):
                    mm = pe.matmul(PS[:, t, :], hqT[:, m, t * P:(t + 1) * P], w2T[:, m, :], start=(m == 0), stop=(m == FT - 1))
                mm.then_inc(inner_done, 1)

            turn_inner(0)
            down_inner(0)
            pe.wait_ge(us_ready, 4 * NT)
            turn_inner(1)
            down_inner(1)


def rope_table(length, dim):
    import numpy as np
    e = np.arange(0, dim, 2, dtype=np.float32) / np.float32(dim)
    inv = (np.float32(1) / (10000.0 ** e.astype(np.float64)).astype(np.float32)).astype(np.float32)
    f = (np.arange(length, dtype=np.float32)[:, None] * inv[None, :]).astype(np.float64)
    return np.cos(f).astype(np.float32), np.sin(f).astype(np.float32)


def layouts(i):
    import numpy as np
    c = np.ascontiguousarray
    perm = [4 * g + t for t in range(4) for g in range(4)]
    wq = i["L0_attn_Wq"].reshape(NH, HD, D)[perm].reshape(D, D)
    cosK, sinK = rope_table(L, CD)
    sinK = np.concatenate([-sinK[:, :CD // 4], sinK[:, CD // 4:]], axis=1)
    cosB, sinB = rope_table(T, HD)

    cosQ, sinQ = rope_table(T, XQ)

    half = XQ // 2
    rows = np.concatenate([np.arange(P), half + np.arange(P), P + np.arange(LEFT), half + P + np.arange(LEFT)])
    cosQ, sinQ = (np.repeat(t, 2, axis=1).T for t in (cosQ, sinQ))
    sinQ = np.concatenate([-sinQ[:half], sinQ[half:]])
    sines = np.concatenate([rows[:2 * P], rows[2 * P + LEFT:], rows[2 * P:2 * P + LEFT]])

    def up(w):
        w = w.reshape(PAIRS, 2, KT, P, FI).transpose(0, 3, 2, 1, 4)
        left = w[..., P:].reshape(PAIRS, P, KT, 1, P)
        return c(np.concatenate([w[..., :P], left], axis=3).reshape(PAIRS, P, KT * 3 * P))

    def down(w):
        w = w.reshape(PAIRS, 2, FI, D)
        left = w[:, :, P:].reshape(PAIRS, 1, P, D)
        return c(np.concatenate([w[:, :, :P], left], axis=1).transpose(0, 2, 1, 3).reshape(PAIRS, P, 3 * D))

    return {
        "x": c(i["x"]), "ctx": c(i["ctx_512"][0]), "ctxT": c(i["ctx_512"][0, :T].T), "cosK": cosK, "sinK": sinK,
        "wqA": c(i["L0_xattn_Wq"].T), "wkvA": c(i["L0_xattn_Wkv_expand"].T), "woA": c(i["L0_xattn_Wout"].T),
        "wqkvB": c(np.concatenate([wq.T, i["L0_attn_Wk"].T, i["L0_attn_Wv"].T], axis=1)),
        "bqkv": c(np.concatenate([i["L0_attn_bq"].reshape(NH, HD)[perm].reshape(D), i["L0_attn_bk"], i["L0_attn_bv"]])),
        "bo": c(i["L0_attn_bo"]), "qn": c(i["L0_attn_qn_w"]), "kn": c(i["L0_attn_kn_w"]), "scale": c(i["L0_attn_scale"].reshape(1)),
        "cosB": cosB, "sinB": sinB, "woB": c(i["L0_attn_Wo"].T),
        "wqX": c(i["L1_xattn_Wq"].reshape(XH, XK, KT, P).transpose(0, 3, 2, 1).reshape(XH, P, KT * XK)), "kcq": c(i["L1_xattn_w_kc_q"][:, :, rows]),
        "wqr": c(i["L1_xattn_W_qr"][:, rows].reshape(XH, QT, P, XR).transpose(0, 2, 1, 3).reshape(XH, P, QT * XR)),
        "wkr": c(i["L1_xattn_W_kr"].transpose(0, 2, 1)), "kcv": c(i["L1_xattn_w_kc_kv"].transpose(0, 2, 1)),
        "woX": c(i["L1_xattn_Wo"].T.reshape(XH, XK, D)), 
        "cosQ": c(cosQ[rows].reshape(QT, P, T).transpose(1, 0, 2)), "sinQ": c(sinQ[sines].reshape(QT, P, T).transpose(1, 0, 2)),
        "win": c(i["L1_attn_W_in"]), "cw": c(i["L1_attn_conv_w"].T.reshape(CT, P, CONV).transpose(1, 0, 2)),
        "cb": c(i["L1_attn_conv_b"].reshape(CT, P).T), "dtb": c(i["L1_attn_dt_bias"]), "alog": c(i["L1_attn_A_log"]),
        "dskip": c(i["L1_attn_D"]), "ns": c(i["L1_attn_norm_scale"].reshape(IT, P).T), "wout": c(i["L1_attn_W_out"]),
        "w1": c(i["L1_ffn_w_gate_up"]), "w2": c(i["L1_ffn_w_down"]),
        "wr": c(i["L0_ffn_router_w"].T), "wg": up(i["L0_ffn_w_gate"]), "wu": up(i["L0_ffn_w_up"]), "wd": down(i["L0_ffn_w_down"]),
    }


def kernel(**inputs):
    import numpy as np
    import concourse.bacc as bacc
    from concourse import mybir as mb
    from concourse.bass_utils import run_bass_kernel_spmd as run

    nc = bacc.Bacc("TRN2", target_bir_lowering=False, num_devices=1)
    arrays, aps = {}, {}
    for name, v in layouts({k: np.asarray(v) for k, v in inputs.items()}).items():
        arrays[f"in_{name}"] = v
        aps[name] = nc.dram_tensor(f"in_{name}", v.shape, mb.dt.from_np(v.dtype), kind="ExternalInput").ap()
    out = nc.dram_tensor("out_0", (1, T, D), F32, kind="ExternalOutput").ap()
    perceiver(nc, aps, out)
    r = run(nc, [arrays], core_ids=[0])
    return r.results[0]["out_0"]
```
